# Optimizing a Trainium2 kernel written in Bass

```python
import numpy as np
import jax
import jax.numpy as jnp

def _softmax(x, axis=-1):
    return jax.nn.softmax(x, axis=axis)

def _gelu(x):
    return jax.nn.gelu(x, approximate=True)

def _silu(x):
    return jax.nn.silu(x)

def _sigmoid(x):
    return jax.nn.sigmoid(x)

def _layernorm(x, axis=-1, eps=1e-05):
    m = jnp.mean(x, axis=axis, keepdims=True)
    v = jnp.var(x, axis=axis, keepdims=True)
    return (x - m) / jnp.sqrt(v + eps)

def _scatter_add(tgt, idx, src, axis=0):
    return tgt.at[idx].add(src)

def _segment_sum(src, seg, n):
    return jax.ops.segment_sum(src, seg, n)
kernel_name = 'mk_xattn_ffn_d1_seqx_r8_88a702'

def setup_inputs(seed: int=0):
    np.random.seed(seed)
    _w = jnp.asarray

    def _rec_inputs():
        import jax
        import jax.numpy as jnp
        _rk = jax.random.key(seed)
        x = 7.22e-05 + 1 * jax.random.normal(jax.random.fold_in(_rk, 1), (1, 1024, 128), jnp.float32)
        _lenS = 1024 - jax.random.randint(jax.random.fold_in(_rk, 7), (1,), 0, max(1, 1024 // 4) + 1, jnp.int32)
        _lenS2 = 6404 - jax.random.randint(jax.random.fold_in(_rk, 8), (1,), 0, max(1, 6404 // 4) + 1, jnp.int32)
        _ctx_1024P = jax.random.normal(jax.random.fold_in(_rk, 11), (1, 16, 128), jnp.float32)
        _ctx_1024c = jax.random.dirichlet(jax.random.fold_in(_rk, 511), 0.3 * jnp.ones((16,), jnp.float32), (1, 6404))
        _ctx_1024t = jnp.einsum('bsk,bkd->bsd', _ctx_1024c, _ctx_1024P)
        _ctx_1024t = _ctx_1024t * jax.lax.rsqrt(jnp.mean(jnp.square(_ctx_1024t)) + 1e-12) * 0.953939
        ctx_1024 = 4.13588e-05 + 0.999923 * (_ctx_1024t + 0.3 * jax.random.normal(jax.random.fold_in(_rk, 611), (1, 6404, 128), jnp.float32))
        return (x, ctx_1024)
    x, ctx_1024 = _rec_inputs()

    def _L0_xattn_setup():
        import jax, jax.numpy as jnp
        import numpy as np
        B, N, E = (4, 256, 128)
        H = 16
        D = E
        HD = D // H
        key = jax.random.key(seed)
        ks = jax.random.split(key, 11)
        s = 0.02
        return {'q': jax.random.normal(ks[0], (B, N, E), jnp.float32), 'k': jax.random.normal(ks[1], (B, N, E), jnp.float32), 'v': jax.random.normal(ks[2], (B, N, E), jnp.float32), 'Wq': jax.random.normal(ks[3], (E, D), jnp.float32) * s, 'bq': jnp.zeros((D,), jnp.float32), 'Wk': jax.random.normal(ks[4], (E, D), jnp.float32) * s, 'bk': jnp.zeros((D,), jnp.float32), 'Wv': jax.random.normal(ks[5], (E, D), jnp.float32) * s, 'bv': jnp.zeros((D,), jnp.float32), 'Wo': jax.random.normal(ks[6], (D, E), jnp.float32) * s, 'bo': jnp.zeros((E,), jnp.float32)}
    _L0_xattn_all = _L0_xattn_setup()
    _L0_xattn_in = {k: v for k, v in _L0_xattn_all.items() if k in ('Wq', 'bq', 'Wk', 'bk', 'Wv', 'bv', 'Wo', 'bo')}
    del _L0_xattn_all

    def _L0_ffn_setup():
        import jax, jax.numpy as jnp
        import numpy as np
        D_MODEL = 128
        N_HEADS = 16
        HEAD_DIM = D_MODEL // N_HEADS
        FFN_DIM = 512
        N_EXPERTS = 8
        TOP_K = 2
        BATCH = 4
        SEQ = 128

        def _layernorm(x, w, b, eps=1e-05):
            mu = jnp.mean(x, axis=-1, keepdims=True)
            var = jnp.mean(jnp.square(x - mu), axis=-1, keepdims=True)
            return (x - mu) * jax.lax.rsqrt(var + eps) * w + b

        def _causal_attention(nx, Wqkv, bqkv, Wo, bo):
            B, S, D = nx.shape
            qkv = nx @ Wqkv + bqkv
            q, k, v = jnp.split(qkv, 3, axis=-1)
            q = q.reshape(B, S, N_HEADS, HEAD_DIM)
            k = k.reshape(B, S, N_HEADS, HEAD_DIM)
            v = v.reshape(B, S, N_HEADS, HEAD_DIM)
            scores = jnp.einsum('bqhd,bkhd->bhqk', q, k) / jnp.sqrt(jnp.float32(HEAD_DIM))
            causal = jnp.tril(jnp.ones((S, S), bool))
            scores = jnp.where(causal, scores, jnp.finfo(scores.dtype).min)
            attn = jax.nn.softmax(scores, axis=-1)
            out = jnp.einsum('bhqk,bkhd->bqhd', attn, v).reshape(B, S, D)
            return out @ Wo + bo

        def _moe_ffn(nx, gate_W, fc1_w, fc1_b, fc2_w, fc2_b):
            gate_logits = nx @ gate_W
            topk_vals, topk_idx = jax.lax.top_k(gate_logits, TOP_K)
            gate_w = jax.nn.softmax(topk_vals, axis=-1)
            dense_gates = jnp.sum(jax.nn.one_hot(topk_idx, N_EXPERTS, dtype=nx.dtype) * gate_w[..., None], axis=-2)
            moe_out = jnp.zeros_like(nx)
            for e in range(N_EXPERTS):
                h = jax.nn.gelu(jnp.einsum('bsd,fd->bsf', nx, fc1_w[e]) + fc1_b[e], approximate=False)
                y = jnp.einsum('bsf,df->bsd', h, fc2_w[e]) + fc2_b[e]
                moe_out = moe_out + y * dense_gates[..., e:e + 1]
            return moe_out
        key = jax.random.key(seed)
        ks = jax.random.split(key, 12)
        s = lambda k, shape, scale: jax.random.normal(k, shape, dtype=jnp.float32) * scale
        inp = {'x': s(ks[0], (BATCH, SEQ, D_MODEL), 1.0), 'ln1_w': jnp.ones((D_MODEL,), jnp.float32), 'ln1_b': jnp.zeros((D_MODEL,), jnp.float32), 'ln2_w': jnp.ones((D_MODEL,), jnp.float32), 'ln2_b': jnp.zeros((D_MODEL,), jnp.float32), 'Wqkv': s(ks[1], (D_MODEL, 3 * D_MODEL), 0.02), 'bqkv': jnp.zeros((3 * D_MODEL,), jnp.float32), 'Wo': s(ks[2], (D_MODEL, D_MODEL), 0.02), 'bo': jnp.zeros((D_MODEL,), jnp.float32), 'gate_W': s(ks[3], (D_MODEL, N_EXPERTS), 0.02), 'fc1_w': s(ks[4], (N_EXPERTS, FFN_DIM, D_MODEL), (2.0 / D_MODEL) ** 0.5), 'fc1_b': jnp.zeros((N_EXPERTS, FFN_DIM), jnp.float32), 'fc2_w': s(ks[5], (N_EXPERTS, D_MODEL, FFN_DIM), (1.0 / FFN_DIM) ** 0.5), 'fc2_b': jnp.zeros((N_EXPERTS, D_MODEL), jnp.float32)}
        return inp
    _L0_ffn_all = _L0_ffn_setup()
    _L0_ffn_in = {k: v for k, v in _L0_ffn_all.items() if k in ('ln1_w', 'ln1_b', 'ln2_w', 'ln2_b', 'Wqkv', 'bqkv', 'Wo', 'bo', 'gate_W', 'fc1_w', 'fc1_b', 'fc2_w', 'fc2_b')}
    del _L0_ffn_all
    return {'x': x, 'ctx_1024': ctx_1024, 'L0_xattn_Wq': _L0_xattn_in['Wq'], 'L0_xattn_bq': _L0_xattn_in['bq'], 'L0_xattn_Wk': _L0_xattn_in['Wk'], 'L0_xattn_bk': _L0_xattn_in['bk'], 'L0_xattn_Wv': _L0_xattn_in['Wv'], 'L0_xattn_bv': _L0_xattn_in['bv'], 'L0_xattn_Wo': _L0_xattn_in['Wo'], 'L0_xattn_bo': _L0_xattn_in['bo'], 'L0_ffn_ln1_w': _L0_ffn_in['ln1_w'], 'L0_ffn_ln1_b': _L0_ffn_in['ln1_b'], 'L0_ffn_ln2_w': _L0_ffn_in['ln2_w'], 'L0_ffn_ln2_b': _L0_ffn_in['ln2_b'], 'L0_ffn_Wqkv': _L0_ffn_in['Wqkv'], 'L0_ffn_bqkv': _L0_ffn_in['bqkv'], 'L0_ffn_Wo': _L0_ffn_in['Wo'], 'L0_ffn_bo': _L0_ffn_in['bo'], 'L0_ffn_gate_W': _L0_ffn_in['gate_W'], 'L0_ffn_fc1_w': _L0_ffn_in['fc1_w'], 'L0_ffn_fc1_b': _L0_ffn_in['fc1_b'], 'L0_ffn_fc2_w': _L0_ffn_in['fc2_w'], 'L0_ffn_fc2_b': _L0_ffn_in['fc2_b']}

def reference(x, ctx_1024, L0_xattn_Wq, L0_xattn_bq, L0_xattn_Wk, L0_xattn_bk, L0_xattn_Wv, L0_xattn_bv, L0_xattn_Wo, L0_xattn_bo, L0_ffn_ln1_w, L0_ffn_ln1_b, L0_ffn_ln2_w, L0_ffn_ln2_b, L0_ffn_Wqkv, L0_ffn_bqkv, L0_ffn_Wo, L0_ffn_bo, L0_ffn_gate_W, L0_ffn_fc1_w, L0_ffn_fc1_b, L0_ffn_fc2_w, L0_ffn_fc2_b):
    import jax
    import jax.numpy as jnp

    def _L0_xattn_ref(q, k, v, Wq, bq, Wk, bk, Wv, bv, Wo, bo):
        import jax, jax.numpy as jnp
        import numpy as np
        B, N, E = (4, 256, 128)
        H = 16
        D = E
        HD = D // H
        qp = q @ Wq + bq
        kp = k @ Wk + bk
        vp = v @ Wv + bv

        def split(x):
            b, n, _ = x.shape
            return x.reshape(b, n, H, HD).transpose(0, 2, 1, 3)
        qh, kh, vh = (split(qp), split(kp), split(vp))
        scale = 1.0 / jnp.sqrt(jnp.asarray(HD, qh.dtype))
        attn = jnp.einsum('bhqd,bhkd->bhqk', qh, kh) * scale
        attn = jax.nn.softmax(attn, axis=-1)
        out = jnp.einsum('bhqk,bhkd->bhqd', attn, vh)
        b, h, n, hd = out.shape
        out = out.transpose(0, 2, 1, 3).reshape(b, n, h * hd)
        return out @ Wo + bo

    def _L0_ffn_ref(x, ln1_w, ln1_b, ln2_w, ln2_b, Wqkv, bqkv, Wo, bo, gate_W, fc1_w, fc1_b, fc2_w, fc2_b):
        import jax, jax.numpy as jnp
        import numpy as np
        D_MODEL = 128
        N_HEADS = 16
        HEAD_DIM = D_MODEL // N_HEADS
        FFN_DIM = 512
        N_EXPERTS = 8
        TOP_K = 2
        BATCH = 4
        SEQ = 128

        def _layernorm(x, w, b, eps=1e-05):
            mu = jnp.mean(x, axis=-1, keepdims=True)
            var = jnp.mean(jnp.square(x - mu), axis=-1, keepdims=True)
            return (x - mu) * jax.lax.rsqrt(var + eps) * w + b

        def _causal_attention(nx, Wqkv, bqkv, Wo, bo):
            B, S, D = nx.shape
            qkv = nx @ Wqkv + bqkv
            q, k, v = jnp.split(qkv, 3, axis=-1)
            q = q.reshape(B, S, N_HEADS, HEAD_DIM)
            k = k.reshape(B, S, N_HEADS, HEAD_DIM)
            v = v.reshape(B, S, N_HEADS, HEAD_DIM)
            scores = jnp.einsum('bqhd,bkhd->bhqk', q, k) / jnp.sqrt(jnp.float32(HEAD_DIM))
            causal = jnp.tril(jnp.ones((S, S), bool))
            scores = jnp.where(causal, scores, jnp.finfo(scores.dtype).min)
            attn = jax.nn.softmax(scores, axis=-1)
            out = jnp.einsum('bhqk,bkhd->bqhd', attn, v).reshape(B, S, D)
            return out @ Wo + bo

        def _moe_ffn(nx, gate_W, fc1_w, fc1_b, fc2_w, fc2_b):
            gate_logits = nx @ gate_W
            topk_vals, topk_idx = jax.lax.top_k(gate_logits, TOP_K)
            gate_w = jax.nn.softmax(topk_vals, axis=-1)
            dense_gates = jnp.sum(jax.nn.one_hot(topk_idx, N_EXPERTS, dtype=nx.dtype) * gate_w[..., None], axis=-2)
            moe_out = jnp.zeros_like(nx)
            for e in range(N_EXPERTS):
                h = jax.nn.gelu(jnp.einsum('bsd,fd->bsf', nx, fc1_w[e]) + fc1_b[e], approximate=False)
                y = jnp.einsum('bsf,df->bsd', h, fc2_w[e]) + fc2_b[e]
                moe_out = moe_out + y * dense_gates[..., e:e + 1]
            return moe_out
        nx = _layernorm(x, ln1_w, ln1_b)
        attn_out = _causal_attention(nx, Wqkv, bqkv, Wo, bo)
        x = x + attn_out
        nx2 = _layernorm(x, ln2_w, ln2_b)
        moe_out = _moe_ffn(nx2, gate_W, fc1_w, fc1_b, fc2_w, fc2_b)
        return x + moe_out
    x = x + _L0_xattn_ref(_layernorm(x, axis=-1), ctx_1024, ctx_1024, L0_xattn_Wq, L0_xattn_bq, L0_xattn_Wk, L0_xattn_bk, L0_xattn_Wv, L0_xattn_bv, L0_xattn_Wo, L0_xattn_bo)
    x = x + _L0_ffn_ref(_layernorm(x, axis=-1), L0_ffn_ln1_w, L0_ffn_ln1_b, L0_ffn_ln2_w, L0_ffn_ln2_b, L0_ffn_Wqkv, L0_ffn_bqkv, L0_ffn_Wo, L0_ffn_bo, L0_ffn_gate_W, L0_ffn_fc1_w, L0_ffn_fc1_b, L0_ffn_fc2_w, L0_ffn_fc2_b)
    return x

_drawn_inputs = setup_inputs


def setup_inputs(seed=0):
    import zlib

    import numpy as np

    out = dict(_drawn_inputs(seed))
    spreads = {'L0_xattn_bq': (0.0, 0.8),
     'L0_xattn_bk': (0.0, 0.8),
     'L0_xattn_bv': (0.0, 0.1),
     'L0_xattn_bo': (0.0, 0.1),
     'L0_ffn_ln1_w': (1.0, 0.6),
     'L0_ffn_ln1_b': (0.0, 0.307),
     'L0_ffn_ln2_w': (1.0, 0.2),
     'L0_ffn_ln2_b': (0.0, 0.1),
     'L0_ffn_bqkv': (0.0, 0.1),
     'L0_ffn_bo': (0.0, 0.1),
     'L0_ffn_fc1_b': (0.0, 0.345),
     'L0_ffn_fc2_b': (0.0, 0.1)}
    factors = {'L0_xattn_Wq': 6.044, 'L0_xattn_Wk': 8.0}
    for name, (base, spread) in spreads.items():
        noise = np.random.default_rng([zlib.crc32(name.encode()), seed]).standard_normal(out[name].shape)
        drawn = base * np.exp(spread * noise) if base else spread * noise
        out[name] = jnp.asarray(drawn.astype(out[name].dtype))
    for name, factor in factors.items():
        out[name] = (out[name] * factor).astype(out[name].dtype)
    return out
```

```python
from contextlib import ExitStack

import numpy as np

import concourse.bass as bass
from concourse import mybir

F32 = mybir.dt.float32
BF16 = mybir.dt.bfloat16
U32 = mybir.dt.uint32
ALU = mybir.AluOpType
ACT = mybir.ActivationFunctionType
AX = mybir.AxisListType

P = 128
D = 128
H, HD = 16, 8
N = 1024
NB = N // P
SK = 6404
KT = SK // P
TAIL = SK - KT * P
SKP = KT * P + 32
HG = 4
NG = H // HG
QH = 512
NHALF = N // QH
UNITS = NG * NHALF
QB = QH // P
PARTS = 3
PROD = PARTS * PARTS * HD
ROWS1 = 96
ROWS2 = ROWS1 + PARTS
VC = HD + 1
STEP = 3
TURNS = (KT - 2) // STEP
LOOPK = TURNS * STEP * P
RESTK = SK - LOOPK
CW = 512
CHUNKS = -(-SK // CW)
VG = -(-KT // 4)
E, F, FC = 8, 512, 4
SCALE = float(np.float32(1.0) / np.sqrt(np.float32(HD)))
EPS = 1e-5

TILES1 = 2 * HG * TURNS + 2 * HG
SPU = 1 + HG * KT
APU = 1 + KT
assert RESTK <= 512 // 2 + P and SPU % 3 == 0 and TURNS * STEP == KT - 2


def slot_base(step):
    return (TILES1 + 1) * step + max(0, step - 1)


def build(nc, A):
    ctx = ExitStack()
    with ctx:
        def sb(name, shape, dt=F32):
            return ctx.enter_context(nc.sbuf_tensor(name, shape, dt))

        def sem(name):
            return ctx.enter_context(nc.semaphore(name))

        ps = ctx.enter_context(nc.psum_tensor("ps", [P, 8, 512], F32))
        ACC = 7
        score_bank = lambda n: 4 + n % 3

        kparts = nc.dram_tensor("kparts", [PARTS, P, SKP], BF16, kind="Internal").ap()
        qparts = nc.dram_tensor("qparts", [PARTS, P, N], BF16, kind="Internal").ap()
        k2parts = nc.dram_tensor("k2parts", [PARTS, P, N], BF16, kind="Internal").ap()
        q2parts = nc.dram_tensor("q2parts", [PARTS, P, N], BF16, kind="Internal").ap()

        KS = sb("KS", [P, 2, HG * SKP], BF16)
        keys = [KS[:, p, :].rearrange("r (h n) -> r h n", h=HG) for p in range(2)]
        ctxT = KS[:, 1, 0:2 * SK].bitcast(F32)
        flat = KS[:, :, :].rearrange("r a n -> r (a n)")
        q2s = flat[:, 0:H * N].rearrange("r (h n) -> r h n", h=H)
        k2s = flat[:, H * N:2 * H * N].rearrange("r (h n) -> r h n", h=H)
        w0 = 2 * H * N
        fc1 = flat[:, w0:w0 + 2 * E * F].bitcast(F32).rearrange("d (e f) -> d e f", e=E)
        fc2 = flat[:, w0 + 2 * E * F:w0 + 4 * E * F].bitcast(F32).rearrange(
            "f (e c d) -> f e c d", e=E, c=FC)
        QU = sb("QU", [P, 3, HG, QH], BF16)
        V = sb("V", [P, KT, H, VC])
        V2 = V[:, :, :, :].rearrange("k t h c -> k (t h c)")[:, 0:NB * H * VC].rearrange(
            "k (t h c) -> k t h c", t=NB, h=H)
        VTAIL = sb("VTAIL", [P, NG, P])
        VST = sb("VST", [P, STEP, HG, 32])
        PR = sb("PR", [P, STEP, HG, QH])
        PRf = PR[:, :, :, :].rearrange("k a h q -> k (a h q)")
        PTAIL = sb("PTAIL", [P, QH])
        OA = sb("OA", [P, QH])
        OX = sb("OX", [P, NB, D])
        X = sb("X", [P, NB, D])
        Z = sb("Z", [P, NB, D])
        NX = sb("NX", [P, NB, D])
        XT = sb("XT", [P, N])
        PM = sb("PM", [P, HG, QB, TURNS + 1])
        C32 = sb("C32", [P, HG, QB])
        C3 = sb("C3", [P, HG, QB, PARTS], BF16)
        RD = sb("RD", [P, QB, HG])
        st = sb("st", [P, NB, 6])
        mv = sb("mv", [P, NB, 2])
        ve = sb("ve", [P, NB])
        sd = sb("sd", [P, NB])
        rs = sb("rs", [P, NB])
        nt = sb("nt", [P, NB])
        ident = sb("ident", [P, P])
        identb = sb("identb", [P, P], BF16)
        maskk = sb("maskk", [P, P], BF16)
        maskq = sb("maskq", [P, P], BF16)
        iota = sb("iota", [P, E])
        sel = sb("sel", [PARTS * E, E, P], BF16)
        wq, wk, wv, wo, wo2 = (sb(n, [P, D]) for n in ("wq", "wk", "wv", "wo", "wo2"))
        wqkv = sb("wqkv", [P, 3 * D])
        gw = sb("gw", [P, E])
        cols = sb("cols", [P, 4])
        b1c = sb("b1c", [P, E * FC])
        fc2b = sb("fc2b", [E, D])
        rows = {n: sb("r_" + n, [P, D]) for n in ("bv", "bo", "l1w", "l1b", "l2w", "l2b", "bv2", "bo2")}
        top = sb("top", [P, NB, E])
        topi = sb("topi", [P, NB, E], U32)
        topf = sb("topf", [P, NB, 2])
        gts = sb("gts", [P, 4, NB])
        dg = sb("dg", [P, 2, NB, E])
        dg3 = sb("dg3", [P, NB, PARTS, E], BF16)
        dgr = sb("dgr", [P, NB, E])
        QUf = QU[:, :, :, :].rearrange("r a h n -> r (a h n)")
        gT = QUf[0:E, 0:2 * N].bitcast(F32)
        gT3 = QUf[0:PARTS * E, 2 * N:3 * N]

        kf = PRf[:, 0:2 * CW].rearrange("p (a n) -> p a n", a=2)
        kr = PRf[:, 2 * CW:4 * CW].rearrange("p (a n) -> p a n", a=2)
        qf = PRf[:, 4 * CW:4 * CW + N]
        qr = PRf[:, 4 * CW + N:4 * CW + 2 * N]
        s0 = 4 * CW + 2 * N
        q3 = PRf[:, s0:s0 + PARTS * N // 2].bitcast(BF16).rearrange("p (j n) -> p j n", j=PARTS)
        K3 = KS[:, 1, 2 * SK:2 * SK + 2 * PARTS * CW].rearrange("p (a j n) -> p a j n", a=2, j=PARTS)
        k2f, k2r = PRf[:, 0:N], PRf[:, N:2 * N]
        v0 = NB * H * VC
        k23 = V[:, :, :, :].rearrange("k t h c -> k (t h c)")[:, v0:v0 + PARTS * N // 2].bitcast(BF16).rearrange(
            "p (j n) -> p j n", j=PARTS)

        ctx_in = [sem(f"ctx_in{c}") for c in range(CHUNKS)]
        names = """x_in wkv_in wq_in par_in const_in late_in pad_in
            kstored0 kstored1 qstored keys_in0 keys_in1 qu_in0 qu_in1 qu_in2 zrows_in
            k_proj k_f32 k_p1 k_r1 k_p2 k_p3 v_proj v_out ones_set
            ln_var ln_sqrt xn_ready xt_psum xt_ready q_proj q_f32 q_p1 q_r1 q_p2 q_p3
            p1_ready p1_free max_parts shift_rows s_ready exp_done av_done acc_copied
            vst_ready ox_ready chain
            ot_psum ot_ready y_ready nx_ready nxt_psum nxt_ready q2_proj k2_proj v2_proj
            q2_f32 q2_p1 q2_r1 q2_p2 q2_p3 k2_f32 k2_p1 k2_r1 k2_p2 k2_p3 v2_out
            q2stored k2stored q2_in k2_in moe_in k2r_free
            o2t_psum o2t_ready y2_ready n2_ready n2t_psum n2t_ready gl_ready gate_d gate_e
            dg_ready gt_psum gt_ready h_psum h_gelu g_psum h_gated h_used yt_copied
            yo_psum out_ready out_done""".split()
        S = {n: sem(n) for n in names}
        kstored = [S["kstored0"], S["kstored1"]]
        keys_in = [S["keys_in0"], S["keys_in1"]]
        qu_in = [S["qu_in0"], S["qu_in1"], S["qu_in2"]]

        cwidth = lambda c: min(CW, SK - c * CW)
        PLAN = [("k", 0), ("k", 1), ("k", 2), ("q", 0)]
        PLAN += [x for n in range(VG) for x in ([("k", n + 3)] if n + 3 < CHUNKS else []) + [("v", n)]]
        PLAN += [("vt", 0)]

        def kts2(half):
            return (half + 1) * QB

        def cols2(half, kt):
            return max(0, kt - half * QB) * P

        BASE1 = slot_base(UNITS + 1) - (TILES1 + 1)
        TILES2 = HG * QB
        def base2(step):
            return BASE1 + (TILES2 + 1) * step + max(0, step - 1)
        SBASE2 = [SPU * UNITS]
        ABASE2 = [APU * UNITS]
        for u in range(UNITS):
            SBASE2.append(SBASE2[-1] + HG * kts2(u % NHALF))
            ABASE2.append(ABASE2[-1] + kts2(u % NHALF))

        block = ctx.enter_context(nc.Block())

        @block.sync
        def _(sp):
            def put(dst, src, s):
                sp.dma_start(dst, src).then_inc(s, 16)

            put(wk[:, :], A["Wk"], S["wkv_in"])
            put(cols[:, :], A["cols"], S["wkv_in"])
            put(X[:, :, :], A["x"].rearrange("a (b p) d -> p (a b) d", p=P), S["x_in"])
            for c in range(CHUNKS):
                a, w = c * CW, cwidth(c)
                put(ctxT[:, a:a + w], A["ctxT"][:, a:a + w], ctx_in[c])
                if c == 0:
                    put(ident[:, :], A["ident"], S["const_in"])
                    put(wq[:, :], A["Wq"], S["wq_in"])
                    put(wv[:, :], A["Wv"], S["wq_in"])
                    put(rows["bv"][:, :], A["bv"].to_broadcast([P, D]), S["wq_in"])
            put(kparts[:, :, SK:SKP], A["zeros"].rearrange("j p n -> j p n"), S["pad_in"])
            put(keys[0][PROD:ROWS2, :, :], A["padrows"][:, None, :].to_broadcast([ROWS2 - PROD, HG, SKP]),
                S["keys_in0"])
            put(QU[PROD:ROWS1, :, :, :].rearrange("r a h n -> r (a h n)"), A["zrows"], S["zrows_in"])
            put(identb[:, :], A["identb"], S["const_in"])

            for kind, c in PLAN:
                if kind == "k":
                    sp.wait_ge(S["k_p3"], c + 1)
                    a, w = c * CW, cwidth(c)
                    put(kparts[:, :, a:a + w].rearrange("j p n -> p j n"), K3[:, c % 2, :, 0:w], kstored[c % 2])
                if kind == "q":
                    sp.wait_ge(S["q_p3"], 1)
                    put(qparts.rearrange("j p n -> p j n"), q3, S["qstored"])

            def stage_queries(u):
                g, half = divmod(u, NHALF)
                src = qparts[:, :, half * QH:(half + 1) * QH].rearrange("j (h d) n -> j d h n", d=HD)
                for j in range(PARTS):
                    for i in range(PARTS):
                        r = (PARTS * j + i) * HD
                        put(QU[r:r + HD, u % 3, :, :], src[i, :, g * HG:(g + 1) * HG, :], qu_in[u % 3])

            def stage_keys(g):
                src = kparts.rearrange("j (h d) n -> j d h n", d=HD)
                for j in range(PARTS):
                    for i in range(PARTS):
                        r = (PARTS * j + i) * HD
                        put(keys[g % 2][r:r + HD, :, :], src[j, :, g * HG:(g + 1) * HG, :], keys_in[g % 2])

            sp.wait_ge(S["qstored"], 16)
            stage_queries(0)
            sp.wait_ge(kstored[0], 16 * ((CHUNKS + 1) // 2))
            sp.wait_ge(kstored[1], 16 * (CHUNKS // 2))
            sp.wait_ge(S["pad_in"], 16)
            stage_keys(0)
            stage_queries(1)
            stage_queries(2)
            for n in ("bo", "l1w", "l1b", "l2w", "l2b", "bv2", "bo2"):
                put(rows[n][:, :], A[n].to_broadcast([P, D]), S["late_in"])
            for dst, n in ((wo, "Wo"), (wo2, "Wo2"), (wqkv, "Wqkv"), (gw, "gw"), (b1c, "b1c"), (fc2b, "fc2b"),
                           (maskk, "maskk"), (maskq, "maskq"), (iota, "iota")):
                put(dst[:, :], A[n], S["late_in"])
            put(sel[:, :, :], A["sel"], S["late_in"])
            sp.wait_ge(S["av_done"], 1)
            put(keys[1][PROD:ROWS2, :, :], A["padrows"][:, None, :].to_broadcast([ROWS2 - PROD, HG, SKP]),
                S["keys_in1"])
            stage_keys(1)
            for u in range(UNITS):
                sp.wait_ge(S["av_done"], 1 + APU * (u + 1))
                if u + 3 < UNITS:
                    stage_queries(u + 3)
                if u % NHALF == NHALF - 1 and u // NHALF + 2 < NG:
                    stage_keys(u // NHALF + 2)
            put(fc1, A["fc1T"], S["moe_in"])
            put(fc2, A["fc2T"], S["moe_in"])
            put(q2s[PROD:ROWS1, :, :], A["zrows"][:, None, 0:N].to_broadcast([ROWS1 - PROD, H, N]), S["q2_in"])
            put(k2s[PROD:ROWS2, :, :], A["padrows"][:, None, 0:N].to_broadcast([ROWS2 - PROD, H, N]), S["k2_in"])
            sp.wait_ge(S["q2_p3"], 1)
            put(q2parts.rearrange("j p n -> p j n"), q3, S["q2stored"])
            sp.wait_ge(S["k2_p3"], 1)
            put(k2parts.rearrange("j p n -> p j n"), k23, S["k2stored"])
            sp.wait_ge(S["q2stored"], 16)
            srcq = q2parts.rearrange("j (h d) n -> j d h n", d=HD)
            srck = k2parts.rearrange("j (h d) n -> j d h n", d=HD)
            for j in range(PARTS):
                for i in range(PARTS):
                    r = (PARTS * j + i) * HD
                    put(q2s[r:r + HD, :, :], srcq[i], S["q2_in"])
            sp.wait_ge(S["k2stored"], 16)
            for j in range(PARTS):
                for i in range(PARTS):
                    r = (PARTS * j + i) * HD
                    put(k2s[r:r + HD, :, :], srck[j], S["k2_in"])
            for half in range(NHALF):
                sp.wait_ge(S["out_ready"], half + 1)
                put(A["out"].rearrange("a (b p) d -> p (a b) d", p=P)[:, half * QB:(half + 1) * QB, :],
                    NX[:, half * QB:(half + 1) * QB, :], S["out_done"])
            sp.wait_ge(S["out_done"], 16 * NHALF)

        @block.gpsimd
        def _(pool):
            pool.memset(V[:, :, :, HD:VC], 1.0).then_inc(S["ones_set"], 1)
            pool.memset(VTAIL[:, :, :], 0.0).then_inc(S["ones_set"], 1)
            pool.memset(VST[:, :, :, :], 0.0).then_inc(S["ones_set"], 1)
            pool.wait_ge(S["ones_set"], 3)
            for h in range(HG):
                pool.memset(VTAIL[32 * h:32 * h + TAIL, :, 32 * h + HD:32 * h + VC], 1.0).then_inc(S["ones_set"], 1)
            pool.wait_ge(S["ones_set"], 3 + HG)
            pool.wait_ge(S["v_out"], VG)

            def stage(u, kt, slot):
                if not (isinstance(kt, int) and kt == 0):
                    pool.wait_ge(S["av_done"], APU * u + kt)
                elif u:
                    pool.wait_ge(S["av_done"], 1 + APU * u)
                g = u // NHALF
                pool.tensor_copy(VST[:, slot, :, 0:VC], V[:, bass.ds(kt, 1), g * HG:(g + 1) * HG, :]
                                 .rearrange("k a h c -> k (a h) c")).then_inc(S["vst_ready"], 1)

            for u in range(UNITS):
                stage(u, 0, 0)
                with pool.Fori(0, TURNS) as i:
                    for j in range(STEP):
                        stage(u, i * STEP + (j + 1), (j + 1) % STEP)
                stage(u, KT - 1, (KT - 1) % STEP)
            pool.wait_ge(S["v2_out"], 1)
            pool.memset(V2[:, :, :, HD:VC], 1.0).then_inc(S["ones_set"], 1)

        @block.scalar
        def _(act):
            def ln_sqrt(n):
                act.wait_ge(S["ln_var"], n)
                act.activation(sd[:, :], ve[:, :], ACT.Sqrt).then_inc(S["ln_sqrt"], 1)

            act.wait_ge(S["wkv_in"], 32)
            ln_sqrt(1)

            for kind, c in PLAN:
                if kind == "k":
                    w = cwidth(c)
                    act.wait_ge(S["k_proj"], c + 1)
                    if c >= 2:
                        act.wait_ge(S["k_r1"], c - 1)
                    act.activation(kf[:, c % 2, 0:w], ps[:, score_bank(c), 0:w], ACT.Identity,
                                   bias=cols[:, 1:2]).then_inc(S["k_f32"], 1)
                    act.wait_ge(S["k_f32"], c + 1)
                    if c >= 2:
                        act.wait_ge(kstored[c % 2], 16 * (c // 2))
                    act.activation(K3[:, c % 2, 0, 0:w], kf[:, c % 2, 0:w], ACT.Copy).then_inc(S["k_p1"], 1)
                    act.wait_ge(S["k_r1"], c + 1)
                    act.activation(K3[:, c % 2, 1, 0:w], kr[:, c % 2, 0:w], ACT.Copy).then_inc(S["k_p2"], 1)
                if kind == "q":
                    for half in range(NHALF):
                        q = slice(half * QH, (half + 1) * QH)
                        act.wait_ge(S["q_f32"], half + 1)
                        act.activation(q3[:, 0, q], qf[:, q], ACT.Copy).then_inc(S["q_p1"], 1)
                    for half in range(NHALF):
                        q = slice(half * QH, (half + 1) * QH)
                        act.wait_ge(S["q_r1"], half + 1)
                        act.activation(q3[:, 1, q], qr[:, q], ACT.Copy).then_inc(S["q_p2"], 1)

            def exp_tile(n, dst, src):
                act.wait_ge(S["s_ready"], n + 1)
                act.activation(dst, src, ACT.Exp).then_inc(S["exp_done"], 1)

            def exp_keys(u, kt, slot):
                if not (isinstance(kt, int) and kt == 0):
                    act.wait_ge(S["av_done"], APU * u + kt)
                elif u:
                    act.wait_ge(S["av_done"], 1 + APU * u)
                for h in range(HG):
                    exp_tile(SPU * u + 1 + HG * kt + h, PR[:, slot, h, :],
                             ps[:, score_bank(1 + HG * slot + h), :])

            def shift_rows(u, dst, bank):
                for h in (2, 3):
                    act.activation(dst[:, h, :], ps[32 * h:32 * h + PARTS, bank, :], ACT.Copy)\
                       .then_inc(S["shift_rows"], 1)

            for step in range(UNITS + 1):
                u = step - 1
                if u >= 0:
                    if u:
                        act.wait_ge(S["av_done"], APU * (u - 1) + 2)
                    exp_tile(SPU * u, PTAIL[:, :], ps[:, score_bank(0), :])
                    exp_keys(u, 0, 0)
                    with act.Fori(0, TURNS) as i:
                        for j in range(STEP):
                            exp_keys(u, i * STEP + (j + 1), (j + 1) % STEP)
                    exp_keys(u, KT - 1, (KT - 1) % STEP)
                    act.wait_ge(S["av_done"], 1 + APU * (u + 1))
                    if u:
                        act.wait_ge(S["p1_free"], slot_base(u + 1) + 2)
                    act.activation(OA[:, :], ps[:, ACC, :], ACT.Copy).then_inc(S["acc_copied"], 1)
                if step < UNITS:
                    n = slot_base(step) + TILES1
                    act.wait_ge(S["p1_ready"], n + 1)
                    shift_rows(step, QU[ROWS1:ROWS2, step % 3, :, :], 2 * (n % 2))

            act.wait_ge(S["ot_psum"], 2)
            act.activation(XT[:, QH:N], ps[:, 1, :], ACT.Copy).then_inc(S["ot_ready"], 1)
            ln_sqrt(2)
            ln_sqrt(3)
            act.wait_ge(S["nxt_psum"], 2)
            act.activation(XT[:, QH:N], ps[:, 5, :], ACT.Copy).then_inc(S["nxt_ready"], 1)
            for t, f, r in (("q2", qf, qr), ("k2", k2f, k2r)):
                parts = q3 if t == "q2" else k23
                act.wait_ge(S[t + "_f32"], 1)
                act.activation(parts[:, 0, :], f, ACT.Copy).then_inc(S[t + "_p1"], 1)
                act.wait_ge(S[t + "_r1"], 1)
                act.activation(parts[:, 1, :], r, ACT.Copy).then_inc(S[t + "_p2"], 1)

            for step in range(UNITS + 1):
                u = step - 1
                if u >= 0:
                    half = u % NHALF
                    for kt in range(kts2(half)):
                        a = ABASE2[u] + kt
                        act.wait_ge(S["av_done"], a - STEP + 2)
                        if u == 0 and kt == 0:
                            act.wait_ge(S["k2_p3"], 1)
                            act.wait_ge(S["q2stored"], 16)
                        c0 = cols2(half, kt)
                        for h in range(HG):
                            n = SBASE2[u] + HG * kt + h
                            exp_tile(n, PR[:, a % STEP, h, c0:QH], ps[:, score_bank(n), c0:QH])
                    act.wait_ge(S["av_done"], 1 + ABASE2[u + 1])
                    act.wait_ge(S["p1_free"], (base2(u + 1) if u else BASE1) + 2)
                    act.activation(OA[:, :], ps[:, ACC, :], ACT.Copy).then_inc(S["acc_copied"], 1)
                if step < UNITS:
                    n = base2(step) + TILES2
                    g, half = divmod(step, NHALF)
                    act.wait_ge(S["p1_ready"], n + 1)
                    shift_rows(step, q2s[ROWS1:ROWS2, g * HG:(g + 1) * HG, half * QH:(half + 1) * QH], 2 * (n % 2))

            act.wait_ge(S["o2t_psum"], 2)
            act.activation(XT[:, QH:N], ps[:, 1, :], ACT.Copy).then_inc(S["o2t_ready"], 1)
            ln_sqrt(4)
            act.wait_ge(S["n2t_psum"], 2)
            act.activation(XT[:, QH:N], ps[:, 5, :], ACT.Copy).then_inc(S["n2t_ready"], 1)
            act.wait_ge(S["gate_d"], 1)
            act.activation(gts[:, 1, :], gts[:, 0, :], ACT.Exp).then_inc(S["gate_e"], 1)
            for m in range(NHALF * E * FC):
                e, c = (m // FC) % E, m % FC
                act.wait_ge(S["h_psum"], m + 1)
                if m >= 4:
                    act.wait_ge(S["h_gated"], m - 3)
                act.activation(PRf[:, (m % 4) * QH:(m % 4 + 1) * QH], ps[:, m % 4, :], ACT.Gelu,
                               bias=b1c[:, e * FC + c:e * FC + c + 1]).then_inc(S["h_gelu"], 1)
            for half in range(NHALF):
                act.wait_ge(S["h_used"], (half + 1) * E * FC)
                act.activation(XT[:, half * QH:(half + 1) * QH], ps[:, 6 + half, :], ACT.Copy)\
                   .then_inc(S["yt_copied"], 1)

        @block.vector
        def _(dve):
            chained = [0]

            def link(ins):
                chained[0] += 1
                ins.then_inc(S["chain"], 1)
                dve.wait_ge(S["chain"], chained[0])

            lns = [0]

            def layernorm(src, dst, last):
                for b in range(NB):
                    i = dve.bn_stats(st[:, b, :], src[:, b, :])
                link(i)
                for b in range(NB):
                    i = dve.bn_aggr(mv[:, b, :], st[:, b, :])
                link(i)
                lns[0] += 1
                dve.tensor_scalar(ve[:, :], mv[:, :, 1], EPS, None, ALU.add).then_inc(S["ln_var"], 1)
                dve.wait_ge(S["ln_sqrt"], lns[0])
                link(dve.reciprocal(rs[:, :], sd[:, :]))
                link(dve.tensor_tensor(nt[:, :], rs[:, :], rs[:, :], ALU.mult))
                link(dve.tensor_tensor(nt[:, :], nt[:, :], ve[:, :], ALU.mult))
                link(dve.tensor_scalar(nt[:, :], nt[:, :], -0.5, 1.5, ALU.mult, ALU.add))
                link(dve.tensor_tensor(rs[:, :], rs[:, :], nt[:, :], ALU.mult))
                for b in range(NB):
                    i = dve.tensor_scalar(dst[:, b, :], src[:, b, :], mv[:, b, 0:1], rs[:, b:b + 1],
                                          ALU.subtract, ALU.mult)
                last(i)

            def over_rows(dst, in0, row, op):
                return dve.tensor_tensor(dst, in0, row[:, None, :].to_broadcast([P, NB, D]), op)

            dve.wait_ge(S["x_in"], 16)
            layernorm(X, NX, lambda i: i.then_inc(S["xn_ready"], 1))

            vb = rows["bv"][:, :].rearrange("p (h d) -> p h d", d=HD)
            for kind, c in PLAN:
                if kind == "k":
                    w = cwidth(c)
                    dve.wait_ge(S["k_p1"], c + 1)
                    if c >= 2:
                        dve.wait_ge(S["k_p3"], c - 1)
                    dve.tensor_tensor(kr[:, c % 2, 0:w], kf[:, c % 2, 0:w], K3[:, c % 2, 0, 0:w],
                                      ALU.subtract).then_inc(S["k_r1"], 1)
                    dve.wait_ge(S["k_p2"], c + 1)
                    dve.tensor_tensor(K3[:, c % 2, 2, 0:w], kr[:, c % 2, 0:w], K3[:, c % 2, 1, 0:w],
                                      ALU.subtract).then_inc(S["k_p3"], 1)
                if kind == "q":
                    for half in range(NHALF):
                        dve.wait_ge(S["xt_psum"], half + 1)
                        dve.tensor_copy(XT[:, half * QH:(half + 1) * QH], ps[:, half, :]).then_inc(S["xt_ready"], 1)
                    dve.wait_ge(S["wkv_in"], 32)
                    for half in range(NHALF):
                        q = slice(half * QH, (half + 1) * QH)
                        dve.wait_ge(S["q_proj"], half + 1)
                        dve.tensor_scalar(qf[:, q], ps[:, 2 + half, :], cols[:, 0:1], SCALE,
                                          ALU.add, ALU.mult).then_inc(S["q_f32"], 1)
                    for half in range(NHALF):
                        q = slice(half * QH, (half + 1) * QH)
                        dve.wait_ge(S["q_p1"], half + 1)
                        dve.tensor_tensor(qr[:, q], qf[:, q], q3[:, 0, q], ALU.subtract).then_inc(S["q_r1"], 1)
                    for half in range(NHALF):
                        q = slice(half * QH, (half + 1) * QH)
                        dve.wait_ge(S["q_p2"], half + 1)
                        i = dve.tensor_tensor(q3[:, 2, q], qr[:, q], q3[:, 1, q], ALU.subtract)
                    i.then_inc(S["q_p3"], 1)
                if kind == "v":
                    n = min(4, KT - 4 * c)
                    dve.wait_ge(S["v_proj"], c + 1)
                    dve.wait_ge(S["wq_in"], 48)
                    dve.tensor_tensor(V[:, 4 * c:4 * c + n, :, 0:HD],
                                      ps[:, c % 2, 0:n * D].rearrange("p (t h d) -> p t h d", t=n, d=HD),
                                      vb[:, None, :, :].to_broadcast([P, n, H, HD]), ALU.add)\
                       .then_inc(S["v_out"], 1)
                if kind == "vt":
                    dve.wait_ge(S["av_done"], 1)
                    dve.wait_ge(S["ones_set"], 3 + HG)
                    for h in range(HG):
                        r = slice(32 * h, 32 * h + TAIL)
                        i = dve.tensor_tensor(
                            VTAIL[r, :, 32 * h:32 * h + HD],
                            ps[r, 2, 0:D].rearrange("p (g h d) -> p g h d", g=NG, d=HD)[:, :, h, :],
                            vb[r, :, :].rearrange("p (g h) d -> p g h d", g=NG)[:, :, h, :], ALU.add)
                        i.then_inc(S["p1_free"], 1) if h >= 2 else None

            def negated_maxima(partial, dst, bank, n):
                if partial is not None:
                    link(dve.tensor_reduce(C32[:, :, :], partial, AX.X, ALU.max, negate=True))
                for part in range(PARTS - 1):
                    link(dve.tensor_copy(C3[:, :, :, part], C32[:, :, :]))
                    link(dve.tensor_tensor(C32[:, :, :], C32[:, :, :], C3[:, :, :, part], ALU.subtract))
                dve.tensor_copy(C3[:, :, :, PARTS - 1], C32[:, :, :]).then_inc(S["max_parts"], 1)
                dve.wait_ge(S["p1_ready"], n + 1)
                dve.tensor_copy(dst[:, 0, :], ps[0:PARTS, bank, :]).then_inc(S["shift_rows"], 1)
                dve.tensor_copy(dst[:, 1, :], ps[32:32 + PARTS, bank, :]).then_inc(S["p1_free"], 1)

            def normalise(g, half, n):
                bank = 2 * (n % 2)
                dve.wait_ge(S["p1_ready"], n + 1)
                t = ps[:, bank, :].rearrange("p (b h c) -> p b h c", b=QB, c=32)
                link(dve.reciprocal(RD[:, :, :], t[:, :, :, HD]))
                o = OX[:, half * QB:(half + 1) * QB, g * HG * HD:(g + 1) * HG * HD]
                dve.tensor_tensor(o.rearrange("p b (h d) -> p b h d", d=HD), t[:, :, :, 0:HD],
                                  RD[:, :, :, None].to_broadcast([P, QB, HG, HD]), ALU.mult)\
                   .then_inc(S["p1_free"], 1)

            for step in range(UNITS + 1):
                n0 = slot_base(step)
                if step < UNITS:
                    def reduce_tile(n, t, slot, width, at):
                        h, qp = divmod(t, 2)
                        dve.wait_ge(S["p1_ready"], n + 1)
                        return dve.tensor_reduce(PM[:, h, 2 * qp:2 * qp + 2, at],
                                                 ps[:, 2 * slot:2 * slot + 2, 0:width], AX.X, ALU.max)

                    with dve.Fori(0, TURNS) as i:
                        for t in range(2 * HG):
                            reduce_tile(n0 + 2 * HG * i + t, t, (n0 + t) % 2, STEP * P, bass.ds(i, 1))\
                                .then_inc(S["p1_free"], 1)
                    for t in range(2 * HG):
                        n = n0 + 2 * HG * TURNS + t
                        i = reduce_tile(n, t, n % 2, RESTK, slice(TURNS, TURNS + 1))
                        i.then_inc(S["p1_free"], 1)
                    n = n0 + TILES1
                    dve.wait_ge(S["p1_free"], n + 2)
                    negated_maxima(PM[:, :, :, :], QU[ROWS1:ROWS2, step % 3, :, :], 2 * (n % 2), n)
                if step > 0:
                    n = n0 + (TILES1 + 1 if step < UNITS else 0)
                    normalise(*divmod(step - 1, NHALF), n)

            dve.wait_ge(S["late_in"], 16 * 17)
            over_rows(X[:, :, :], X[:, :, :], rows["bo"], ALU.add).then_inc(S["nx_ready"], 1)
            dve.wait_ge(S["ot_psum"], 1)
            dve.tensor_copy(XT[:, 0:QH], ps[:, 0, :]).then_inc(S["ot_ready"], 1)
            dve.wait_ge(S["nx_ready"], 1)
            for half in range(NHALF):
                dve.wait_ge(S["y_ready"], half + 1)
                xs = X[:, half * QB:(half + 1) * QB, :].rearrange("p b d -> p (b d)")
                i = dve.tensor_tensor(xs, xs, ps[:, 2 + half, :], ALU.add)
            link(i)
            layernorm(X, Z, link)
            layernorm(Z, NX, link)
            link(over_rows(NX[:, :, :], NX[:, :, :], rows["l1w"], ALU.mult))
            over_rows(NX[:, :, :], NX[:, :, :], rows["l1b"], ALU.add).then_inc(S["nx_ready"], 1)
            dve.wait_ge(S["nxt_psum"], 1)
            dve.tensor_copy(XT[:, 0:QH], ps[:, 4, :]).then_inc(S["nxt_ready"], 1)
            dve.wait_ge(S["q2_proj"], 1)
            dve.tensor_scalar(qf, ps[:, 6:8, :].rearrange("p a n -> p (a n)"), cols[:, 2:3], SCALE,
                              ALU.add, ALU.mult).then_inc(S["q2_f32"], 1)
            dve.wait_ge(S["k2_proj"], 1)
            dve.tensor_scalar(k2f, ps[:, 0:2, :].rearrange("p a n -> p (a n)"), cols[:, 3:4], None,
                              ALU.add).then_inc(S["k2_f32"], 1)
            dve.wait_ge(S["q2_p1"], 1)
            dve.tensor_tensor(qr, qf, q3[:, 0, :], ALU.subtract).then_inc(S["q2_r1"], 1)
            dve.wait_ge(S["k2_p1"], 1)
            dve.tensor_tensor(k2r, k2f, k23[:, 0, :], ALU.subtract).then_inc(S["k2_r1"], 1)
            dve.wait_ge(S["q2_p2"], 1)
            dve.tensor_tensor(q3[:, 2, :], qr, q3[:, 1, :], ALU.subtract).then_inc(S["q2_p3"], 1)
            dve.wait_ge(S["k2_p2"], 1)
            dve.tensor_tensor(k23[:, 2, :], k2r, k23[:, 1, :], ALU.subtract).then_inc(S["k2_p3"], 1)
            dve.wait_ge(S["v2_proj"], 1)
            v2b = rows["bv2"][:, :].rearrange("p (h d) -> p h d", d=HD)
            for half in range(NHALF):
                i = dve.tensor_tensor(V2[:, half * QB:(half + 1) * QB, :, 0:HD],
                                      ps[:, 2 + half, :].rearrange("p (t h d) -> p t h d", t=QB, d=HD),
                                      v2b[:, None, :, :].to_broadcast([P, QB, H, HD]), ALU.add)
            i.then_inc(S["v2_out"], 1)

            for step in range(UNITS + 1):
                n0 = base2(step)
                if step < UNITS:
                    g, half = divmod(step, NHALF)
                    for t in range(TILES2):
                        h, qb = divmod(t, QB)
                        w = (half * QB + qb + 1) * P
                        n = n0 + t
                        slot = n % 2
                        dve.wait_ge(S["p1_ready"], n + 1)
                        tile = ps[:, 2 * slot:2 * slot + 2, :].rearrange("p a n -> p (a n)")
                        dve.tensor_reduce(C32[:, h, qb:qb + 1], tile[:, 0:w], AX.X, ALU.max, negate=True)\
                           .then_inc(S["p1_free"], 1)
                    n = n0 + TILES2
                    dve.wait_ge(S["p1_free"], n + 2)
                    negated_maxima(None, q2s[ROWS1:ROWS2, g * HG:(g + 1) * HG, half * QH:(half + 1) * QH],
                                   2 * (n % 2), n)
                if step > 0:
                    n = n0 + (TILES2 + 1 if step < UNITS else 0)
                    normalise(*divmod(step - 1, NHALF), n)

            link(over_rows(Z[:, :, :], Z[:, :, :], rows["bo2"], ALU.add))
            dve.wait_ge(S["o2t_psum"], 1)
            dve.tensor_copy(XT[:, 0:QH], ps[:, 0, :]).then_inc(S["o2t_ready"], 1)
            for half in range(NHALF):
                dve.wait_ge(S["y2_ready"], half + 1)
                zs = Z[:, half * QB:(half + 1) * QB, :].rearrange("p b d -> p (b d)")
                i = dve.tensor_tensor(zs, zs, ps[:, 2 + half, :], ALU.add)
            link(i)
            layernorm(Z, NX, link)
            link(over_rows(NX[:, :, :], NX[:, :, :], rows["l2w"], ALU.mult))
            over_rows(NX[:, :, :], NX[:, :, :], rows["l2b"], ALU.add).then_inc(S["n2_ready"], 1)
            dve.wait_ge(S["n2t_psum"], 1)
            dve.tensor_copy(XT[:, 0:QH], ps[:, 4, :]).then_inc(S["n2t_ready"], 1)
            link(dve.tensor_tensor(X[:, :, :], X[:, :, :], Z[:, :, :], ALU.add))
            dve.wait_ge(S["gl_ready"], 1)
            link(dve.tensor_copy(dgr[:, :, :], ps[:, 6, 0:NB * E].rearrange("p (b e) -> p b e", e=E)))
            for b in range(NB):
                i = dve.max(top[:, b, :], dgr[:, b, :])
            link(i)
            for b in range(NB):
                i = dve.max_index(topi[:, b, :], top[:, b, :], dgr[:, b, :])
            link(i)
            dve.tensor_tensor(gts[:, 0, :], top[:, :, 1], top[:, :, 0], ALU.subtract).then_inc(S["gate_d"], 1)
            link(dve.tensor_copy(topf[:, :, :], topi[:, :, 0:2]))
            dve.wait_ge(S["gate_e"], 1)
            link(dve.tensor_scalar(gts[:, 2, :], gts[:, 1, :], 1.0, None, ALU.add))
            link(dve.reciprocal(gts[:, 2, :], gts[:, 2, :]))
            link(dve.tensor_tensor(gts[:, 3, :], gts[:, 1, :], gts[:, 2, :], ALU.mult))
            for r in range(2):
                for b in range(NB):
                    i = dve.tensor_scalar(dg[:, r, b, :], iota[:, :], topf[:, b, r:r + 1],
                                          gts[:, 2 + r, b:b + 1], ALU.is_equal, ALU.mult)
            link(i)
            link(dve.tensor_tensor(dg[:, 0, :, :], dg[:, 0, :, :], dg[:, 1, :, :], ALU.add))
            link(dve.tensor_copy(dg3[:, :, 0, :], dg[:, 0, :, :]))
            link(dve.tensor_tensor(dgr[:, :, :], dg[:, 0, :, :], dg3[:, :, 0, :], ALU.subtract))
            link(dve.tensor_copy(dg3[:, :, 1, :], dgr[:, :, :]))
            dve.tensor_tensor(dg3[:, :, 2, :], dgr[:, :, :], dg3[:, :, 1, :], ALU.subtract)\
               .then_inc(S["dg_ready"], 1)
            dve.wait_ge(S["gt_psum"], 1)
            for half in range(NHALF):
                q = slice(half * QH, (half + 1) * QH)
                dve.tensor_copy(gT[:, q], ps[0:E, 4 + half, :])
                i = dve.tensor_copy(gT3[:, q], ps[0:PARTS * E, 2 + half, 0:QH // 2].bitcast(BF16))
            i.then_inc(S["gt_ready"], 1)
            for m in range(NHALF * E * FC):
                dve.wait_ge(S["h_gelu"], m + 1)
                dve.wait_ge(S["g_psum"], m // FC + 1)
                if m >= 4:
                    dve.wait_ge(S["h_used"], m - 3)
                dve.tensor_tensor(PRf[:, (4 + m % 4) * QH:(5 + m % 4) * QH],
                                  PRf[:, (m % 4) * QH:(m % 4 + 1) * QH],
                                  ps[:, 4 + (m // FC) % 2, :], ALU.mult).then_inc(S["h_gated"], 1)
            for half in range(NHALF):
                dve.wait_ge(S["yo_psum"], half + 1)
                xs = X[:, half * QB:(half + 1) * QB, :].rearrange("p b d -> p (b d)")
                os = NX[:, half * QB:(half + 1) * QB, :].rearrange("p b d -> p (b d)")
                dve.tensor_tensor(os, xs, ps[:, half, :], ALU.add).then_inc(S["out_ready"], 1)

        @block.tensor
        def _(pe):
            def transposes(src, banks, ready):
                for half, bank in enumerate(banks):
                    for b in range(QB):
                        i = pe.transpose(ps[:, bank, b * P:(b + 1) * P], src[:, half * QB + b, :], ident[:, :])
                    i.then_inc(ready, 1)

            pe.wait_ge(S["wkv_in"], 32)
            seen = 0
            for kind, c in PLAN:
                if kind == "k":
                    pe.wait_ge(ctx_in[c], 16)
                    if c >= 3:
                        pe.wait_ge(S["k_f32"], c - 2)
                    w = cwidth(c)
                    pe.matmul(ps[:, score_bank(c), 0:w], wk[:, :], ctxT[:, c * CW:c * CW + w],
                              start=True, stop=True).then_inc(S["k_proj"], 1)
                if kind == "q":
                    pe.wait_ge(S["xn_ready"], 1)
                    pe.wait_ge(S["const_in"], 32)
                    pe.wait_ge(S["wq_in"], 48)
                    transposes(NX, (0, 1), S["xt_psum"])
                    for half in range(NHALF):
                        pe.wait_ge(S["xt_ready"], half + 1)
                        pe.matmul(ps[:, 2 + half, :], wq[:, :], XT[:, half * QH:(half + 1) * QH],
                                  start=True, stop=True).then_inc(S["q_proj"], 1)
                if kind == "v":
                    if c >= 2:
                        pe.wait_ge(S["v_out"], c - 1)
                    for t in range(4 * c, min(4 * c + 4, KT)):
                        i = pe.matmul(ps[:, c % 2, (t % 4) * D:(t % 4 + 1) * D], ctxT[:, t * P:(t + 1) * P],
                                      wv[:, :], start=True, stop=True)
                    i.then_inc(S["v_proj"], 1)
                if kind == "vt":
                    pe.wait_ge(S["q_f32"], NHALF)
                    for h in range(HG):
                        i = pe.matmul(ps[32 * h:32 * h + TAIL, 2, 0:D], ctxT[:, KT * P:SK], wv[:, :],
                                      start=True, stop=True, tile_position=(0, 32 * h))
                    i.then_inc(S["av_done"], 1)

            def fill(n):
                pe.wait_ge(S["p1_free"], n + 1)

            def max_tile(u, n, t, slot, k0, width):
                h, qp = divmod(t, 2)
                fill(n)
                for b in range(2):
                    q0 = (2 * qp + b) * P
                    i = pe.matmul(ps[:, 2 * slot + b, 0:width], QU[0:ROWS1, u % 3, h, q0:q0 + P],
                                  keys[(u // NHALF) % 2][0:ROWS1, h, bass.ds(k0, width)], start=True, stop=True)
                i.then_inc(S["p1_ready"], 1)

            def score_tile(u, kt, h, bank):
                n = SPU * u + 1 + HG * kt + h
                if not isinstance(n, int) or n >= 3:
                    pe.wait_ge(S["exp_done"], n - 2)
                pe.matmul(ps[:, bank, :], keys[(u // NHALF) % 2][0:ROWS2, h, bass.ds(kt * P, P)],
                          QU[0:ROWS2, u % 3, h, :], start=True, stop=True).then_inc(S["s_ready"], 1)

            def values(u, kt, slot, last=False):
                pe.wait_ge(S["exp_done"], SPU * u + 1 + HG * (kt + 1))
                pe.wait_ge(S["vst_ready"], KT * u + kt + 1)
                for h in range(HG):
                    i = pe.matmul(ps[32 * h:32 * h + 32, ACC, :], VST[:, slot, h, :],
                                  PR[:, slot, h, :], start=False, stop=last, skip_group_check=True,
                                  tile_position=(0, 32 * h))
                i.then_inc(S["av_done"], 1)
                return i

            def maxima_rows(n):
                fill(n)
                for h in range(HG):
                    for b in range(QB):
                        i = pe.matmul(ps[32 * h:32 * h + PARTS, 2 * (n % 2), b * P:(b + 1) * P],
                                      C3[:, h, b, :], identb[:, :], start=True, stop=True,
                                      tile_position=(0, 32 * h))
                i.then_inc(S["p1_ready"], 1)

            def output_blocks(n, copies):
                pe.wait_ge(S["acc_copied"], copies)
                fill(n)
                for b in range(QB):
                    i = pe.transpose(ps[:, 2 * (n % 2), b * P:(b + 1) * P], OA[:, b * P:(b + 1) * P], ident[:, :])
                i.then_inc(S["p1_ready"], 1)

            pe.wait_ge(S["zrows_in"], 16)
            pe.wait_ge(S["v_out"], VG)
            for step in range(UNITS + 1):
                u1, u2 = (step if step < UNITS else None), (step - 1 if step else None)
                n0 = slot_base(step)
                if u1 is not None:
                    g = u1 // NHALF
                    pe.wait_ge(qu_in[u1 % 3], 16 * 9 * (u1 // 3 + 1))
                    pe.wait_ge(keys_in[g % 2], 16 * (1 + 9 * (g // 2 + 1)))
                if u2 is not None:
                    pe.wait_ge(S["shift_rows"], 3 * (u2 + 1))
                    pe.wait_ge(S["p1_free"], slot_base(u2) + TILES1 + 1 + 2)
                    par = (u2 // NHALF) % 2
                    if u2:
                        pe.wait_ge(S["exp_done"], SPU * u2 - 2)
                    for h in range(HG):
                        i = pe.matmul(ps[32 * h:32 * h + 32, score_bank(0), :], keys[par][0:ROWS2, h, KT * P:SKP],
                                      QU[0:ROWS2, u2 % 3, h, :], start=True, stop=True, tile_position=(0, 32 * h))
                    i.then_inc(S["s_ready"], 1)
                    for h in range(HG):
                        score_tile(u2, 0, h, score_bank(1 + h))
                    pe.wait_ge(S["exp_done"], SPU * u2 + 1)
                    if u2:
                        pe.wait_ge(S["acc_copied"], u2)
                    pe.matmul(ps[:, ACC, :], VTAIL[:, u2 // NHALF, :], PTAIL[:, :], start=True, stop=False,
                              skip_group_check=True).then_inc(S["av_done"], 1)

                with pe.Fori(0, TURNS) as i:
                    t = 0
                    for j in range(STEP):
                        tiles = [3, 3, 2][j]
                        for h in range(HG):
                            if u2 is not None:
                                score_tile(u2, i * STEP + (j + 1), h, score_bank(1 + HG * (j + 1) + h))
                            if u1 is not None and h < tiles:
                                max_tile(u1, n0 + 2 * HG * i + t, t, (n0 + t) % 2, i * (STEP * P), STEP * P)
                                t += 1
                        if u2 is not None:
                            values(u2, i * STEP + j, j)
                if u1 is not None:
                    for t in range(2 * HG):
                        n = n0 + 2 * HG * TURNS + t
                        max_tile(u1, n, t, n % 2, LOOPK, RESTK)
                if u2 is not None:
                    for h in range(HG):
                        score_tile(u2, KT - 1, h, score_bank(1 + HG * (KT - 1) + h))
                    values(u2, KT - 2, (KT - 2) % STEP)
                    values(u2, KT - 1, (KT - 1) % STEP, last=True)
                if u1 is not None:
                    pe.wait_ge(S["max_parts"], u1 + 1)
                    maxima_rows(n0 + TILES1)
                if u2 is not None:
                    output_blocks(n0 + (TILES1 + 1 if u1 is not None else 0), u2 + 1)

            pe.wait_ge(S["late_in"], 16 * 17)
            pe.wait_ge(S["p1_free"], BASE1 + 2)
            transposes(OX, (0, 1), S["ot_psum"])
            pe.wait_ge(S["ot_ready"], 2)
            for half in range(NHALF):
                for b in range(QB):
                    t = half * QB + b
                    i = pe.matmul(ps[:, 2 + half, b * D:(b + 1) * D], XT[:, t * P:(t + 1) * P], wo[:, :],
                                  start=True, stop=True)
                i.then_inc(S["y_ready"], 1)
            pe.wait_ge(S["nx_ready"], 2)
            transposes(NX, (4, 5), S["nxt_psum"])
            pe.wait_ge(S["nxt_ready"], 2)
            for bank, w, s in ((6, 0, "q2_proj"), (0, D, "k2_proj")):
                for half in range(NHALF):
                    i = pe.matmul(ps[:, bank + half, :], wqkv[:, w:w + D], XT[:, half * QH:(half + 1) * QH],
                                  start=True, stop=True)
                i.then_inc(S[s], 1)
            for t in range(NB):
                i = pe.matmul(ps[:, 2 + t // QB, (t % QB) * D:(t % QB + 1) * D], XT[:, t * P:(t + 1) * P],
                              wqkv[:, 2 * D:3 * D], start=True, stop=True)
            i.then_inc(S["v2_proj"], 1)

            pe.wait_ge(S["v2_out"], 1)
            pe.wait_ge(S["q2_in"], 16 * 10)
            pe.wait_ge(S["k2_in"], 16 * 10)
            pe.wait_ge(S["ones_set"], 4 + HG)
            for step in range(UNITS + 1):
                n0 = base2(step)
                u1, u2 = (step if step < UNITS else None), (step - 1 if step else None)

                def max_tiles(tiles):
                    g, half = divmod(u1, NHALF)
                    for t in tiles:
                        h, qb = divmod(t, QB)
                        head = g * HG + h
                        q0 = (half * QB + qb) * P
                        n = n0 + t
                        slot = n % 2
                        fill(n)
                        w = q0 + P
                        for a in range(0, w, 512):
                            b = min(512, w - a)
                            i = pe.matmul(ps[:, 2 * slot + a // 512, 0:b], q2s[0:ROWS1, head, q0:q0 + P],
                                          k2s[0:ROWS1, head, a:a + b], start=True, stop=True)
                        i = pe.matmul(ps[:, 2 * slot + q0 // 512, q0 % 512:q0 % 512 + P], identb[:, :], maskq[:, :],
                                      start=False, stop=True, skip_group_check=True)
                        i.then_inc(S["p1_ready"], 1)

                def values2(u, kt):
                    g, half = divmod(u, NHALF)
                    a = ABASE2[u] + kt
                    c0 = cols2(half, kt)
                    pe.wait_ge(S["exp_done"], SBASE2[u] + HG * (kt + 1))
                    if kt == 0:
                        pe.wait_ge(S["acc_copied"], UNITS + u)
                    for h in range(HG):
                        i = pe.matmul(ps[32 * h:32 * h + VC, ACC, c0:QH], V2[:, kt, g * HG + h, :],
                                      PR[:, a % STEP, h, c0:QH], start=(kt == 0), stop=(kt == kts2(half) - 1),
                                      skip_group_check=True, tile_position=(0, 32 * h))
                    i.then_inc(S["av_done"], 1)

                if u2 is not None:
                    g, half = divmod(u2, NHALF)
                    pe.wait_ge(S["shift_rows"], 3 * (UNITS + u2 + 1))
                    pe.wait_ge(S["p1_free"], base2(u2) + TILES2 + 1 + 2)
                    todo = list(range(TILES2)) if u1 is not None else []
                    per = -(-TILES2 // kts2(half))
                    for kt in range(kts2(half)):
                        c0 = cols2(half, kt)
                        masked = kt >= half * QB
                        for h in range(HG):
                            n = SBASE2[u2] + HG * kt + h
                            pe.wait_ge(S["exp_done"], n - 2)
                            i = pe.matmul(ps[:, score_bank(n), c0:QH], k2s[0:ROWS2, g * HG + h, kt * P:(kt + 1) * P],
                                          q2s[0:ROWS2, g * HG + h, half * QH + c0:(half + 1) * QH],
                                          start=True, stop=True)
                            if masked:
                                i = pe.matmul(ps[:, score_bank(n), c0:c0 + P], identb[:, :], maskk[:, :],
                                              start=False, stop=True, skip_group_check=True)
                            i.then_inc(S["s_ready"], 1)
                            if u1 is not None and todo and h < per:
                                max_tiles([todo.pop(0)])
                        if kt:
                            values2(u2, kt - 1)
                    if u1 is not None:
                        max_tiles(todo)
                    values2(u2, kts2(half) - 1)
                else:
                    max_tiles(range(TILES2))
                if u1 is not None:
                    pe.wait_ge(S["max_parts"], UNITS + u1 + 1)
                    maxima_rows(n0 + TILES2)
                if u2 is not None:
                    output_blocks(n0 + (TILES2 + 1 if u1 is not None else 0), UNITS + u2 + 1)

            pe.wait_ge(S["p1_free"], base2(UNITS) + 1 + 2)
            transposes(OX, (0, 1), S["o2t_psum"])
            pe.wait_ge(S["o2t_ready"], 2)
            for half in range(NHALF):
                for b in range(QB):
                    t = half * QB + b
                    i = pe.matmul(ps[:, 2 + half, b * D:(b + 1) * D], XT[:, t * P:(t + 1) * P], wo2[:, :],
                                  start=True, stop=True)
                i.then_inc(S["y2_ready"], 1)
            pe.wait_ge(S["n2_ready"], 1)
            transposes(NX, (4, 5), S["n2t_psum"])
            pe.wait_ge(S["n2t_ready"], 2)
            for t in range(NB):
                i = pe.matmul(ps[:, 6, t * E:(t + 1) * E], XT[:, t * P:(t + 1) * P], gw[:, :], start=True, stop=True)
            i.then_inc(S["gl_ready"], 1)

            def up(m):
                half, e, c = m // (E * FC), (m // FC) % E, m % FC
                if m >= 4:
                    pe.wait_ge(S["h_gelu"], m - 3)
                pe.matmul(ps[:, m % 4, :], fc1[:, e, c * P:(c + 1) * P], XT[:, half * QH:(half + 1) * QH],
                          start=True, stop=True).then_inc(S["h_psum"], 1)

            def gate(k):
                half, e = divmod(k, E)
                if k >= 2:
                    pe.wait_ge(S["h_gated"], FC * (k - 1))
                pe.matmul(ps[:, 4 + k % 2, :], sel[:, e, :], gT3[:, half * QH:(half + 1) * QH],
                          start=True, stop=True).then_inc(S["g_psum"], 1)

            pe.wait_ge(S["moe_in"], 32)
            pe.wait_ge(S["dg_ready"], 1)
            for t in range(NB):
                half, b = divmod(t, QB)
                pe.transpose(ps[0:E, 4 + half, b * P:(b + 1) * P], dg[:, 0, t, :], ident[:, :])
                i = pe.transpose(ps[0:PARTS * E, 2 + half, b * P // 2:(b + 1) * P // 2].bitcast(BF16),
                                 dg3[:, t, :, :].rearrange("p j e -> p (j e)"), identb[:, :])
            i.then_inc(S["gt_psum"], 1)
            pe.wait_ge(S["gt_ready"], 1)
            gate(0)
            up(0)
            up(1)
            MM = NHALF * E * FC
            for m in range(MM):
                half, e, c = m // (E * FC), (m // FC) % E, m % FC
                if m % FC == 1 and m // FC + 1 < NHALF * E:
                    gate(m // FC + 1)
                if m + 2 < MM:
                    up(m + 2)
                if e == 0 and c == 0:
                    pe.matmul(ps[:, 6 + half, :], fc2b[:, :], gT[:, half * QH:(half + 1) * QH],
                              start=True, stop=False, skip_group_check=True)
                pe.wait_ge(S["h_gated"], m + 1)
                i = pe.matmul(ps[:, 6 + half, :], fc2[:, e, c, :], PRf[:, (4 + m % 4) * QH:(5 + m % 4) * QH],
                              start=False, stop=(e == E - 1 and c == FC - 1), skip_group_check=True)
                i.then_inc(S["h_used"], 1)
            for half in range(NHALF):
                pe.wait_ge(S["yt_copied"], half + 1)
                if half == 0:
                    pe.wait_ge(S["h_gelu"], MM)
                for b in range(QB):
                    t = half * QB + b
                    i = pe.transpose(ps[:, half, b * P:(b + 1) * P], XT[:, t * P:(t + 1) * P], ident[:, :])
                i.then_inc(S["yo_psum"], 1)


def kernel(**inputs):
    import ml_dtypes
    import concourse.bacc as bacc
    from concourse.bass_utils import run_bass_kernel_spmd

    a = {k: np.asarray(v) for k, v in inputs.items()}
    bf = ml_dtypes.bfloat16
    f = lambda n: a["L0_ffn_" + n]
    xa = lambda n: a["L0_xattn_" + n]
    col = lambda v: v.reshape(D, 1)
    row = lambda v: v.reshape(1, D)
    padrows = np.zeros((ROWS2 - PROD, SKP), bf)
    padrows[ROWS1 - PROD:, :SK] = 1
    masked = np.triu(np.ones((P, P), bool), 1)
    sel = np.zeros((PARTS * E, E, P), bf)
    for j in range(PARTS):
        for e in range(E):
            sel[j * E + e, e, :] = 1
    arrays = {
        "x": a["x"], "ctxT": np.ascontiguousarray(a["ctx_1024"][0].T),
        "Wq": xa("Wq"), "Wk": xa("Wk"), "Wv": xa("Wv"), "Wo": xa("Wo"), "Wqkv": f("Wqkv"), "Wo2": f("Wo"),
        "gw": f("gate_W"),
        "cols": np.concatenate([col(xa("bq")), col(xa("bk")), col(f("bqkv")[:D]), col(f("bqkv")[D:2 * D])], 1),
        "bv": row(xa("bv")), "bo": row(xa("bo")), "bv2": row(f("bqkv")[2 * D:]), "bo2": row(f("bo")),
        "l1w": row(f("ln1_w")), "l1b": row(f("ln1_b")), "l2w": row(f("ln2_w")), "l2b": row(f("ln2_b")),
        "fc1T": np.ascontiguousarray(f("fc1_w").transpose(2, 0, 1)),
        "fc2T": np.ascontiguousarray(f("fc2_w").reshape(E, D, FC, P).transpose(3, 0, 2, 1)),
        "b1c": np.ascontiguousarray(f("fc1_b").reshape(E * FC, P).T), "fc2b": f("fc2_b"),
        "ident": np.eye(P, dtype=np.float32), "identb": np.eye(P, dtype=bf),
        "maskq": np.where(masked, -1e30, 0.0).astype(bf), "maskk": np.where(masked.T, -1e30, 0.0).astype(bf),
        "iota": np.tile(np.arange(E, dtype=np.float32), (P, 1)), "sel": sel,
        "zeros": np.zeros((PARTS, P, SKP - SK), bf), "padrows": padrows,
        "zrows": np.zeros((ROWS1 - PROD, 3 * HG * QH), bf),
    }
    nc = bacc.Bacc("TRN2", target_bir_lowering=False, num_devices=1)
    dram = {n: nc.dram_tensor("in_" + n, v.shape, mybir.dt.from_np(v.dtype), kind="ExternalInput").ap()
            for n, v in arrays.items()}
    dram["out"] = nc.dram_tensor("out", (1, N, D), F32, kind="ExternalOutput").ap()
    build(nc, dram)
    r = run_bass_kernel_spmd(nc, [{"in_" + n: v for n, v in arrays.items()}], core_ids=[0])
    return r.results[0]["out"]
```

```python
from contextlib import ExitStack

import numpy as np

import concourse.bass as bass
from concourse import mybir

F32 = mybir.dt.float32
BF16 = mybir.dt.bfloat16
U32 = mybir.dt.uint32
ALU = mybir.AluOpType
ACT = mybir.ActivationFunctionType
AX = mybir.AxisListType

P = 128
D = 128
H, HD = 16, 8
N = 1024
NB = N // P
SK = 6404
KT = SK // P
TAIL = SK - KT * P
SKP = KT * P + 32
HG = 4
NG = H // HG
QH = 512
NHALF = N // QH
UNITS = NG * NHALF
QB = QH // P
PARTS = 3
PROD = PARTS * PARTS * HD
ROWS1 = 96
ROWS2 = ROWS1 + PARTS
VC = HD + 1
STEP = 3
TURNS = (KT - 2) // STEP
MCH = TURNS + 1
MK = SK // MCH
MW = SK - (MCH - 1) * MK
CW = 512
CHUNKS = -(-SK // CW)
VG = -(-KT // 4)
E, F, FC = 8, 512, 4
SCALE = float(np.float32(1.0) / np.sqrt(np.float32(HD)))
EPS = 1e-5

TILES = HG * QB
SLOTS = 4
AHEAD = 2
SPU = 1 + HG * KT
APU = 1 + KT
ORDER = ((0, "max", 1, "max", 2, "max", "values", "max", 3, "max"),
         (0, "max", 1, "max", 2, "max", "values", "max", 3, "max"),
         (0, "max", 1, "max", "max", 2, "max", "values", "max", 3, "max"))
assert MW <= 512 and SPU % 3 == 0 and TURNS * STEP == KT - 2
assert TILES % SLOTS == 0 and sum(o.count("max") for o in ORDER) == TILES


def with_output(step):
    return 1 if 2 <= step < UNITS else 0


def first_use(step):
    n = AHEAD
    for s in range(step):
        n += TILES * MCH + with_output(s) + 1 - (AHEAD if s == UNITS - 1 else 0)
    return n


def loop_use(step):
    return first_use(step) + with_output(step) + TILES - AHEAD


def tile_use(u, t):
    if t < AHEAD:
        return t if u == 0 else maxima_use(u - 1) - AHEAD + t
    return first_use(u) + t - AHEAD if t < 2 * AHEAD else loop_use(u) - TILES + t


def maxima_use(step):
    return first_use(step + 1) - 1


def output_use(u):
    return first_use(u + 2) + AHEAD if u + 2 < UNITS else first_use(UNITS) + u + 2 - UNITS


def build(nc, A):
    ctx = ExitStack()
    with ctx:
        def sb(name, shape, dt=F32):
            return ctx.enter_context(nc.sbuf_tensor(name, shape, dt))

        def sem(name):
            return ctx.enter_context(nc.semaphore(name))

        ps = ctx.enter_context(nc.psum_tensor("ps", [P, 8, 512], F32))
        ACC = 7
        score_bank = lambda n: 4 + n % 3

        kparts = nc.dram_tensor("kparts", [PARTS, P, SKP], BF16, kind="Internal").ap()
        qparts = nc.dram_tensor("qparts", [PARTS, P, N], BF16, kind="Internal").ap()
        k2parts = nc.dram_tensor("k2parts", [PARTS, P, N], BF16, kind="Internal").ap()
        q2parts = nc.dram_tensor("q2parts", [PARTS, P, N], BF16, kind="Internal").ap()

        KS = sb("KS", [P, 2, HG * SKP], BF16)
        keys = [KS[:, p, :].rearrange("r (h n) -> r h n", h=HG) for p in range(2)]
        ctxT = KS[:, 1, 0:2 * SK].bitcast(F32)
        flat = KS[:, :, :].rearrange("r a n -> r (a n)")
        q2s = flat[:, 0:H * N].rearrange("r (h n) -> r h n", h=H)
        k2s = flat[:, H * N:2 * H * N].rearrange("r (h n) -> r h n", h=H)
        w0 = 2 * H * N
        fc1 = flat[:, w0:w0 + 2 * E * F].bitcast(F32).rearrange("d (e f) -> d e f", e=E)
        fc2 = flat[:, w0 + 2 * E * F:w0 + 4 * E * F].bitcast(F32).rearrange(
            "f (e c d) -> f e c d", e=E, c=FC)
        QU = sb("QU", [P, 3, HG, QH], BF16)
        V = sb("V", [P, KT, H, VC])
        V2 = V[:, :, :, :].rearrange("k t h c -> k (t h c)")[:, 0:NB * H * VC].rearrange(
            "k (t h c) -> k t h c", t=NB, h=H)
        VTAIL = sb("VTAIL", [P, NG, P])
        VST = sb("VST", [P, STEP, HG, 32])
        PR = sb("PR", [P, STEP, HG, QH])
        PRf = PR[:, :, :, :].rearrange("k a h q -> k (a h q)")
        PTAIL = sb("PTAIL", [P, QH])
        OA = sb("OA", [P, QH])
        OX = sb("OX", [P, NB, D])
        X = sb("X", [P, NB, D])
        Z = sb("Z", [P, NB, D])
        NX = sb("NX", [P, NB, D])
        XT = sb("XT", [P, N])
        PM = sb("PM", [P, HG, QB, MCH])
        C32 = sb("C32", [P, HG, QB])
        C3 = sb("C3", [P, HG, QB, PARTS], BF16)
        RD = sb("RD", [P, QB, HG])
        st = sb("st", [P, NB, 6])
        mv = sb("mv", [P, NB, 2])
        ve = sb("ve", [P, NB])
        sd = sb("sd", [P, NB])
        rs = sb("rs", [P, NB])
        nt = sb("nt", [P, NB])
        ident = sb("ident", [P, P])
        identb = sb("identb", [P, P], BF16)
        maskk = sb("maskk", [P, P], BF16)
        maskq = sb("maskq", [P, P], BF16)
        iota = sb("iota", [P, E])
        sel = sb("sel", [PARTS * E, E, P], BF16)
        wq, wk, wv, wo, wo2 = (sb(n, [P, D]) for n in ("wq", "wk", "wv", "wo", "wo2"))
        wqkv = sb("wqkv", [P, 3 * D])
        gw = sb("gw", [P, E])
        cols = sb("cols", [P, 4])
        b1c = sb("b1c", [P, E * FC])
        fc2b = sb("fc2b", [E, D])
        rows = {n: sb("r_" + n, [P, D]) for n in ("bv", "bo", "l1w", "l1b", "l2w", "l2b", "bv2", "bo2")}
        top = sb("top", [P, NB, E])
        topi = sb("topi", [P, NB, E], U32)
        topf = sb("topf", [P, NB, 2])
        gts = sb("gts", [P, 4, NB])
        dg = sb("dg", [P, 2, NB, E])
        dg3 = sb("dg3", [P, NB, PARTS, E], BF16)
        dgr = sb("dgr", [P, NB, E])
        QUf = QU[:, :, :, :].rearrange("r a h n -> r (a h n)")
        gT = QUf[0:E, 0:2 * N].bitcast(F32)
        gT3 = QUf[0:PARTS * E, 2 * N:3 * N]

        kf = PRf[:, 0:2 * CW].rearrange("p (a n) -> p a n", a=2)
        kr = PRf[:, 2 * CW:4 * CW].rearrange("p (a n) -> p a n", a=2)
        qf = PRf[:, 4 * CW:4 * CW + N]
        qr = PRf[:, 4 * CW + N:4 * CW + 2 * N]
        s0 = 4 * CW + 2 * N
        q3 = PRf[:, s0:s0 + PARTS * N // 2].bitcast(BF16).rearrange("p (j n) -> p j n", j=PARTS)
        K3 = KS[:, 1, 2 * SK:2 * SK + 2 * PARTS * CW].rearrange("p (a j n) -> p a j n", a=2, j=PARTS)
        k2f, k2r = PRf[:, 0:N], PRf[:, N:2 * N]
        v0 = NB * H * VC
        k23 = V[:, :, :, :].rearrange("k t h c -> k (t h c)")[:, v0:v0 + PARTS * N // 2].bitcast(BF16).rearrange(
            "p (j n) -> p j n", j=PARTS)

        ctx_in = [sem(f"ctx_in{c}") for c in range(CHUNKS)]
        names = """x_in wkv_in wq_in par_in const_in late_in pad_in
            kstored0 kstored1 qstored keys_in0 keys_in1 qu_in0 qu_in1 qu_in2 zrows_in
            k_proj k_f32 k_p1 k_r1 k_p2 k_p3 v_proj v_out ones_set
            ln_var ln_sqrt xn_ready xt_psum xt_ready q_proj q_f32 q_p1 q_r1 q_p2 q_p3
            p1_ready p1_free max_parts shift_rows shift_rows2 s_ready exp_done av_done acc_copied
            vst_ready ox_ready chain
            ot_psum ot_ready y_ready nx_ready nxt_psum nxt_ready q2_proj k2_proj v2_proj
            q2_f32 q2_p1 q2_r1 q2_p2 q2_p3 k2_f32 k2_p1 k2_r1 k2_p2 k2_p3 v2_out
            q2stored k2stored q2_in k2_in moe_in k2r_free
            o2t_psum o2t_ready y2_ready n2_ready n2t_psum n2t_ready gl_ready gate_d gate_e
            dg_ready gt_psum gt_ready h_psum h_gelu g_psum h_gated h_used yt_copied
            yo_psum out_ready out_done""".split()
        S = {n: sem(n) for n in names}
        kstored = [S["kstored0"], S["kstored1"]]
        keys_in = [S["keys_in0"], S["keys_in1"]]
        qu_in = [S["qu_in0"], S["qu_in1"], S["qu_in2"]]

        cwidth = lambda c: min(CW, SK - c * CW)
        PLAN = [("k", 0), ("k", 1), ("k", 2), ("q", 0)]
        PLAN += [x for n in range(VG) for x in ([("k", n + 3)] if n + 3 < CHUNKS else []) + [("v", n)]]
        PLAN += [("vt", 0)]

        def kts2(half):
            return (half + 1) * QB

        def cols2(half, kt):
            return max(0, kt - half * QB) * P

        BASE1 = output_use(UNITS - 1) + 1 + SLOTS - 2
        READY2 = 1 - (SLOTS - 2)
        TILES2 = HG * QB
        def base2(step):
            return BASE1 + (TILES2 + 1) * step + max(0, step - 1)
        SBASE2 = [SPU * UNITS]
        ABASE2 = [APU * UNITS]
        for u in range(UNITS):
            SBASE2.append(SBASE2[-1] + HG * kts2(u % NHALF))
            ABASE2.append(ABASE2[-1] + kts2(u % NHALF))

        block = ctx.enter_context(nc.Block())

        @block.sync
        def _(sp):
            def put(dst, src, s):
                sp.dma_start(dst, src).then_inc(s, 16)

            put(wk[:, :], A["Wk"], S["wkv_in"])
            put(cols[:, :], A["cols"], S["wkv_in"])
            put(X[:, :, :], A["x"].rearrange("a (b p) d -> p (a b) d", p=P), S["x_in"])
            for c in range(CHUNKS):
                a, w = c * CW, cwidth(c)
                put(ctxT[:, a:a + w], A["ctxT"][:, a:a + w], ctx_in[c])
                if c == 0:
                    put(ident[:, :], A["ident"], S["const_in"])
                    put(wq[:, :], A["Wq"], S["wq_in"])
                    put(wv[:, :], A["Wv"], S["wq_in"])
                    put(rows["bv"][:, :], A["bv"].to_broadcast([P, D]), S["wq_in"])
            put(kparts[:, :, SK:SKP], A["zeros"].rearrange("j p n -> j p n"), S["pad_in"])
            put(keys[0][PROD:ROWS2, :, :], A["padrows"][:, None, :].to_broadcast([ROWS2 - PROD, HG, SKP]),
                S["keys_in0"])
            put(QU[PROD:ROWS1, :, :, :].rearrange("r a h n -> r (a h n)"), A["zrows"], S["zrows_in"])
            put(identb[:, :], A["identb"], S["const_in"])

            for kind, c in PLAN:
                if kind == "k":
                    sp.wait_ge(S["k_p3"], c + 1)
                    a, w = c * CW, cwidth(c)
                    put(kparts[:, :, a:a + w].rearrange("j p n -> p j n"), K3[:, c % 2, :, 0:w], kstored[c % 2])
                if kind == "q":
                    sp.wait_ge(S["q_p3"], 1)
                    put(qparts.rearrange("j p n -> p j n"), q3, S["qstored"])

            def stage_queries(u):
                g, half = divmod(u, NHALF)
                src = qparts[:, :, half * QH:(half + 1) * QH].rearrange("j (h d) n -> j d h n", d=HD)
                for j in range(PARTS):
                    for i in range(PARTS):
                        r = (PARTS * j + i) * HD
                        put(QU[r:r + HD, u % 3, :, :], src[i, :, g * HG:(g + 1) * HG, :], qu_in[u % 3])

            def stage_keys(g):
                src = kparts.rearrange("j (h d) n -> j d h n", d=HD)
                for j in range(PARTS):
                    for i in range(PARTS):
                        r = (PARTS * j + i) * HD
                        put(keys[g % 2][r:r + HD, :, :], src[j, :, g * HG:(g + 1) * HG, :], keys_in[g % 2])

            sp.wait_ge(S["qstored"], 16)
            stage_queries(0)
            sp.wait_ge(kstored[0], 16 * ((CHUNKS + 1) // 2))
            sp.wait_ge(kstored[1], 16 * (CHUNKS // 2))
            sp.wait_ge(S["pad_in"], 16)
            stage_keys(0)
            stage_queries(1)
            stage_queries(2)
            for n in ("bo", "l1w", "l1b", "l2w", "l2b", "bv2", "bo2"):
                put(rows[n][:, :], A[n].to_broadcast([P, D]), S["late_in"])
            for dst, n in ((wo, "Wo"), (wo2, "Wo2"), (wqkv, "Wqkv"), (gw, "gw"), (b1c, "b1c"), (fc2b, "fc2b"),
                           (maskk, "maskk"), (maskq, "maskq"), (iota, "iota")):
                put(dst[:, :], A[n], S["late_in"])
            put(sel[:, :, :], A["sel"], S["late_in"])
            sp.wait_ge(S["av_done"], 1)
            put(keys[1][PROD:ROWS2, :, :], A["padrows"][:, None, :].to_broadcast([ROWS2 - PROD, HG, SKP]),
                S["keys_in1"])
            stage_keys(1)
            for u in range(UNITS):
                sp.wait_ge(S["av_done"], 1 + APU * (u + 1))
                if u + 3 < UNITS:
                    stage_queries(u + 3)
                if u % NHALF == NHALF - 1 and u // NHALF + 2 < NG:
                    stage_keys(u // NHALF + 2)
            put(fc1, A["fc1T"], S["moe_in"])
            put(fc2, A["fc2T"], S["moe_in"])
            put(q2s[PROD:ROWS1, :, :], A["zrows"][:, None, 0:N].to_broadcast([ROWS1 - PROD, H, N]), S["q2_in"])
            put(k2s[PROD:ROWS2, :, :], A["padrows"][:, None, 0:N].to_broadcast([ROWS2 - PROD, H, N]), S["k2_in"])
            sp.wait_ge(S["q2_p3"], 1)
            put(q2parts.rearrange("j p n -> p j n"), q3, S["q2stored"])
            sp.wait_ge(S["k2_p3"], 1)
            put(k2parts.rearrange("j p n -> p j n"), k23, S["k2stored"])
            sp.wait_ge(S["q2stored"], 16)
            srcq = q2parts.rearrange("j (h d) n -> j d h n", d=HD)
            srck = k2parts.rearrange("j (h d) n -> j d h n", d=HD)
            for j in range(PARTS):
                for i in range(PARTS):
                    r = (PARTS * j + i) * HD
                    put(q2s[r:r + HD, :, :], srcq[i], S["q2_in"])
            sp.wait_ge(S["k2stored"], 16)
            for j in range(PARTS):
                for i in range(PARTS):
                    r = (PARTS * j + i) * HD
                    put(k2s[r:r + HD, :, :], srck[j], S["k2_in"])
            for half in range(NHALF):
                sp.wait_ge(S["out_ready"], half + 1)
                put(A["out"].rearrange("a (b p) d -> p (a b) d", p=P)[:, half * QB:(half + 1) * QB, :],
                    NX[:, half * QB:(half + 1) * QB, :], S["out_done"])
            sp.wait_ge(S["out_done"], 16 * NHALF)

        @block.gpsimd
        def _(pool):
            pool.memset(V[:, :, :, HD:VC], 1.0).then_inc(S["ones_set"], 1)
            pool.memset(VTAIL[:, :, :], 0.0).then_inc(S["ones_set"], 1)
            pool.memset(VST[:, :, :, :], 0.0).then_inc(S["ones_set"], 1)
            pool.wait_ge(S["ones_set"], 3)
            for h in range(HG):
                pool.memset(VTAIL[32 * h:32 * h + TAIL, :, 32 * h + HD:32 * h + VC], 1.0).then_inc(S["ones_set"], 1)
            pool.wait_ge(S["ones_set"], 3 + HG)
            pool.wait_ge(S["v_out"], VG)

            def stage(u, kt, slot):
                if u or not (isinstance(kt, int) and kt < STEP):
                    pool.wait_ge(S["av_done"], APU * u + kt - 1)
                g = u // NHALF
                pool.tensor_copy(VST[:, slot, :, 0:VC], V[:, bass.ds(kt, 1), g * HG:(g + 1) * HG, :]
                                 .rearrange("k a h c -> k (a h) c")).then_inc(S["vst_ready"], 1)

            for u in range(UNITS):
                stage(u, 0, 0)
                stage(u, 1, 1)
                with pool.Fori(0, TURNS) as i:
                    for j in range(STEP):
                        stage(u, i * STEP + (j + 2), (j + 2) % STEP)
            pool.wait_ge(S["v2_out"], 1)
            pool.memset(V2[:, :, :, HD:VC], 1.0).then_inc(S["ones_set"], 1)

        @block.scalar
        def _(act):
            def ln_sqrt(n):
                act.wait_ge(S["ln_var"], n)
                act.activation(sd[:, :], ve[:, :], ACT.Sqrt).then_inc(S["ln_sqrt"], 1)

            act.wait_ge(S["wkv_in"], 32)
            ln_sqrt(1)

            for kind, c in PLAN:
                if kind == "k":
                    w = cwidth(c)
                    act.wait_ge(S["k_proj"], c + 1)
                    if c >= 2:
                        act.wait_ge(S["k_r1"], c - 1)
                    act.activation(kf[:, c % 2, 0:w], ps[:, score_bank(c), 0:w], ACT.Identity,
                                   bias=cols[:, 1:2]).then_inc(S["k_f32"], 1)
                    act.wait_ge(S["k_f32"], c + 1)
                    if c >= 2:
                        act.wait_ge(kstored[c % 2], 16 * (c // 2))
                    act.activation(K3[:, c % 2, 0, 0:w], kf[:, c % 2, 0:w], ACT.Copy).then_inc(S["k_p1"], 1)
                    act.wait_ge(S["k_r1"], c + 1)
                    act.activation(K3[:, c % 2, 1, 0:w], kr[:, c % 2, 0:w], ACT.Copy).then_inc(S["k_p2"], 1)
                if kind == "q":
                    for half in range(NHALF):
                        q = slice(half * QH, (half + 1) * QH)
                        act.wait_ge(S["q_f32"], half + 1)
                        act.activation(q3[:, 0, q], qf[:, q], ACT.Copy).then_inc(S["q_p1"], 1)
                    for half in range(NHALF):
                        q = slice(half * QH, (half + 1) * QH)
                        act.wait_ge(S["q_r1"], half + 1)
                        act.activation(q3[:, 1, q], qr[:, q], ACT.Copy).then_inc(S["q_p2"], 1)

            def exp_tile(n, dst, src):
                act.wait_ge(S["s_ready"], n + 1)
                act.activation(dst, src, ACT.Exp).then_inc(S["exp_done"], 1)

            def exp_keys(u, kt, slot):
                if u or not (isinstance(kt, int) and kt < STEP):
                    act.wait_ge(S["av_done"], APU * u + kt - 1)
                for h in range(HG):
                    first = isinstance(kt, int) and kt == 0
                    n = h if first else 1 + HG * kt + h
                    bank = score_bank(h if first else 1 + HG * slot + h)
                    exp_tile(SPU * u + n, PR[:, slot, h, :], ps[:, bank, :])

            def shift_rows(u, dst, bank):
                for h in (0, 1):
                    act.activation(dst[:, h, :], ps[32 * h:32 * h + PARTS, bank, :], ACT.Copy)\
                       .then_inc(S["shift_rows"], 1)

            for step in range(UNITS + 1):
                u = step - 1
                if u >= 0:
                    exp_keys(u, 0, 0)
                    if u:
                        act.wait_ge(S["av_done"], 1 + APU * u)
                    exp_tile(SPU * u + HG, PTAIL[:, :], ps[:, score_bank(HG), :])
                    exp_keys(u, 1, 1)
                    with act.Fori(0, TURNS) as i:
                        for j in range(STEP):
                            exp_keys(u, i * STEP + (j + 2), (j + 2) % STEP)
                if step < UNITS:
                    n = maxima_use(step)
                    act.wait_ge(S["p1_ready"], n + 1)
                    shift_rows(step, QU[ROWS1:ROWS2, step % 3, :, :], n % SLOTS)
                if u >= 0:
                    act.wait_ge(S["av_done"], 1 + APU * (u + 1))
                    if u:
                        act.wait_ge(S["p1_free"], output_use(u - 1) + 1 + SLOTS)
                    act.activation(OA[:, :], ps[:, ACC, :], ACT.Copy).then_inc(S["acc_copied"], 1)

            act.wait_ge(S["ot_psum"], 2)
            act.activation(XT[:, QH:N], ps[:, 1, :], ACT.Copy).then_inc(S["ot_ready"], 1)
            ln_sqrt(2)
            ln_sqrt(3)
            act.wait_ge(S["nxt_psum"], 2)
            act.activation(XT[:, QH:N], ps[:, 5, :], ACT.Copy).then_inc(S["nxt_ready"], 1)
            for t, f, r in (("q2", qf, qr), ("k2", k2f, k2r)):
                parts = q3 if t == "q2" else k23
                act.wait_ge(S[t + "_f32"], 1)
                act.activation(parts[:, 0, :], f, ACT.Copy).then_inc(S[t + "_p1"], 1)
                act.wait_ge(S[t + "_r1"], 1)
                act.activation(parts[:, 1, :], r, ACT.Copy).then_inc(S[t + "_p2"], 1)

            for step in range(UNITS + 1):
                u = step - 1
                if u >= 0:
                    half = u % NHALF
                    for kt in range(kts2(half)):
                        a = ABASE2[u] + kt
                        act.wait_ge(S["av_done"], a - STEP + 2)
                        if u == 0 and kt == 0:
                            act.wait_ge(S["k2_p3"], 1)
                            act.wait_ge(S["q2stored"], 16)
                        c0 = cols2(half, kt)
                        for h in range(HG):
                            n = SBASE2[u] + HG * kt + h
                            exp_tile(n, PR[:, a % STEP, h, c0:QH], ps[:, score_bank(n), c0:QH])
                    act.wait_ge(S["av_done"], 1 + ABASE2[u + 1])
                    act.wait_ge(S["p1_free"], (base2(u + 1) if u else BASE1) + 2)
                    act.activation(OA[:, :], ps[:, ACC, :], ACT.Copy).then_inc(S["acc_copied"], 1)
                if step < UNITS:
                    n = base2(step) + TILES2
                    g, half = divmod(step, NHALF)
                    act.wait_ge(S["p1_ready"], n + READY2)
                    shift_rows(step, q2s[ROWS1:ROWS2, g * HG:(g + 1) * HG, half * QH:(half + 1) * QH], 2 * (n % 2))

            act.wait_ge(S["o2t_psum"], 2)
            act.activation(XT[:, QH:N], ps[:, 1, :], ACT.Copy).then_inc(S["o2t_ready"], 1)
            ln_sqrt(4)
            act.wait_ge(S["n2t_psum"], 2)
            act.activation(XT[:, QH:N], ps[:, 5, :], ACT.Copy).then_inc(S["n2t_ready"], 1)
            act.wait_ge(S["gate_d"], 1)
            act.activation(gts[:, 1, :], gts[:, 0, :], ACT.Exp).then_inc(S["gate_e"], 1)
            for m in range(NHALF * E * FC):
                e, c = (m // FC) % E, m % FC
                act.wait_ge(S["h_psum"], m + 1)
                if m >= 4:
                    act.wait_ge(S["h_gated"], m - 3)
                act.activation(PRf[:, (m % 4) * QH:(m % 4 + 1) * QH], ps[:, m % 4, :], ACT.Gelu,
                               bias=b1c[:, e * FC + c:e * FC + c + 1]).then_inc(S["h_gelu"], 1)
            for half in range(NHALF):
                act.wait_ge(S["h_used"], (half + 1) * E * FC)
                act.activation(XT[:, half * QH:(half + 1) * QH], ps[:, 6 + half, :], ACT.Copy)\
                   .then_inc(S["yt_copied"], 1)

        @block.vector
        def _(dve):
            chained = [0]

            def link(ins):
                chained[0] += 1
                ins.then_inc(S["chain"], 1)
                dve.wait_ge(S["chain"], chained[0])

            lns = [0]

            def layernorm(src, dst, last):
                for b in range(NB):
                    i = dve.bn_stats(st[:, b, :], src[:, b, :])
                link(i)
                for b in range(NB):
                    i = dve.bn_aggr(mv[:, b, :], st[:, b, :])
                link(i)
                lns[0] += 1
                dve.tensor_scalar(ve[:, :], mv[:, :, 1], EPS, None, ALU.add).then_inc(S["ln_var"], 1)
                dve.wait_ge(S["ln_sqrt"], lns[0])
                link(dve.reciprocal(rs[:, :], sd[:, :]))
                link(dve.tensor_tensor(nt[:, :], rs[:, :], rs[:, :], ALU.mult))
                link(dve.tensor_tensor(nt[:, :], nt[:, :], ve[:, :], ALU.mult))
                link(dve.tensor_scalar(nt[:, :], nt[:, :], -0.5, 1.5, ALU.mult, ALU.add))
                link(dve.tensor_tensor(rs[:, :], rs[:, :], nt[:, :], ALU.mult))
                for b in range(NB):
                    i = dve.tensor_scalar(dst[:, b, :], src[:, b, :], mv[:, b, 0:1], rs[:, b:b + 1],
                                          ALU.subtract, ALU.mult)
                last(i)

            def over_rows(dst, in0, row, op):
                return dve.tensor_tensor(dst, in0, row[:, None, :].to_broadcast([P, NB, D]), op)

            dve.wait_ge(S["x_in"], 16)
            layernorm(X, NX, lambda i: i.then_inc(S["xn_ready"], 1))

            vb = rows["bv"][:, :].rearrange("p (h d) -> p h d", d=HD)
            for kind, c in PLAN:
                if kind == "k":
                    w = cwidth(c)
                    dve.wait_ge(S["k_p1"], c + 1)
                    if c >= 2:
                        dve.wait_ge(S["k_p3"], c - 1)
                    dve.tensor_tensor(kr[:, c % 2, 0:w], kf[:, c % 2, 0:w], K3[:, c % 2, 0, 0:w],
                                      ALU.subtract).then_inc(S["k_r1"], 1)
                    dve.wait_ge(S["k_p2"], c + 1)
                    dve.tensor_tensor(K3[:, c % 2, 2, 0:w], kr[:, c % 2, 0:w], K3[:, c % 2, 1, 0:w],
                                      ALU.subtract).then_inc(S["k_p3"], 1)
                if kind == "q":
                    for half in range(NHALF):
                        dve.wait_ge(S["xt_psum"], half + 1)
                        dve.tensor_copy(XT[:, half * QH:(half + 1) * QH], ps[:, half, :]).then_inc(S["xt_ready"], 1)
                    dve.wait_ge(S["wkv_in"], 32)
                    for half in range(NHALF):
                        q = slice(half * QH, (half + 1) * QH)
                        dve.wait_ge(S["q_proj"], half + 1)
                        dve.tensor_scalar(qf[:, q], ps[:, 2 + half, :], cols[:, 0:1], SCALE,
                                          ALU.add, ALU.mult).then_inc(S["q_f32"], 1)
                    for half in range(NHALF):
                        q = slice(half * QH, (half + 1) * QH)
                        dve.wait_ge(S["q_p1"], half + 1)
                        dve.tensor_tensor(qr[:, q], qf[:, q], q3[:, 0, q], ALU.subtract).then_inc(S["q_r1"], 1)
                    for half in range(NHALF):
                        q = slice(half * QH, (half + 1) * QH)
                        dve.wait_ge(S["q_p2"], half + 1)
                        i = dve.tensor_tensor(q3[:, 2, q], qr[:, q], q3[:, 1, q], ALU.subtract)
                    i.then_inc(S["q_p3"], 1)
                if kind == "v":
                    n = min(4, KT - 4 * c)
                    dve.wait_ge(S["v_proj"], c + 1)
                    dve.wait_ge(S["wq_in"], 48)
                    dve.tensor_tensor(V[:, 4 * c:4 * c + n, :, 0:HD],
                                      ps[:, c % 2, 0:n * D].rearrange("p (t h d) -> p t h d", t=n, d=HD),
                                      vb[:, None, :, :].to_broadcast([P, n, H, HD]), ALU.add)\
                       .then_inc(S["v_out"], 1)
                if kind == "vt":
                    dve.wait_ge(S["av_done"], 1)
                    dve.wait_ge(S["ones_set"], 3 + HG)
                    for h in range(HG):
                        r = slice(32 * h, 32 * h + TAIL)
                        i = dve.tensor_tensor(
                            VTAIL[r, :, 32 * h:32 * h + HD],
                            ps[r, SLOTS - 1, 0:D].rearrange("p (g h d) -> p g h d", g=NG, d=HD)[:, :, h, :],
                            vb[r, :, :].rearrange("p (g h) d -> p g h d", g=NG)[:, :, h, :], ALU.add)
                        i.then_inc(S["p1_free"], 1)

            def negated_maxima_parts(partial):
                if partial is not None:
                    link(dve.tensor_reduce(C32[:, :, :], partial, AX.X, ALU.max, negate=True))
                for part in range(PARTS - 1):
                    link(dve.tensor_copy(C3[:, :, :, part], C32[:, :, :]))
                    link(dve.tensor_tensor(C32[:, :, :], C32[:, :, :], C3[:, :, :, part], ALU.subtract))
                dve.tensor_copy(C3[:, :, :, PARTS - 1], C32[:, :, :]).then_inc(S["max_parts"], 1)

            def negated_maxima_rows(dst, bank, n):
                dve.wait_ge(S["p1_ready"], n)
                dve.tensor_copy(dst[:, 2, :], ps[64:64 + PARTS, bank, :]).then_inc(S["shift_rows2"], 1)
                dve.tensor_copy(dst[:, 3, :], ps[96:96 + PARTS, bank, :]).then_inc(S["p1_free"], 1)

            def normalise(g, half, bank, n):
                dve.wait_ge(S["p1_ready"], n)
                t = ps[:, bank, :].rearrange("p (b h c) -> p b h c", b=QB, c=32)
                link(dve.reciprocal(RD[:, :, :], t[:, :, :, HD]))
                o = OX[:, half * QB:(half + 1) * QB, g * HG * HD:(g + 1) * HG * HD]
                dve.tensor_tensor(o.rearrange("p b (h d) -> p b h d", d=HD), t[:, :, :, 0:HD],
                                  RD[:, :, :, None].to_broadcast([P, QB, HG, HD]), ALU.mult)\
                   .then_inc(S["p1_free"], 1)

            def reduce_tile(n, t, bank, at):
                h, qb = divmod(t, QB)
                dve.wait_ge(S["p1_ready"], n + 1)
                dve.tensor_reduce(PM[:, h, qb, at], ps[:, bank, 0:MW], AX.X, ALU.max).then_inc(S["p1_free"], 1)

            def reduce_first(u, tiles):
                for t in tiles:
                    n = tile_use(u, t)
                    reduce_tile(n, t, n % SLOTS, slice(0, 1))

            reduce_first(0, range(AHEAD))
            for step in range(UNITS):
                reduce_first(step, range(AHEAD, 2 * AHEAD))
                if with_output(step):
                    n = output_use(step - 2)
                    normalise(*divmod(step - 2, NHALF), n % SLOTS, n + 1)
                reduce_first(step, range(2 * AHEAD, TILES))
                n0 = loop_use(step)
                with dve.Fori(0, TURNS) as i:
                    for t in range(TILES):
                        reduce_tile(n0 + TILES * i + t, t, (n0 + t) % SLOTS, bass.ds(i + 1, 1))
                dve.wait_ge(S["p1_free"], n0 + TILES * TURNS + SLOTS)
                negated_maxima_parts(PM[:, :, :, :])
                if step < UNITS - 1:
                    reduce_first(step + 1, range(AHEAD))
                n = maxima_use(step)
                negated_maxima_rows(QU[ROWS1:ROWS2, step % 3, :, :], n % SLOTS, n + 1)
            for u in range(UNITS - 2, UNITS):
                n = output_use(u)
                normalise(*divmod(u, NHALF), n % SLOTS, n + 1)

            dve.wait_ge(S["late_in"], 16 * 17)
            over_rows(X[:, :, :], X[:, :, :], rows["bo"], ALU.add).then_inc(S["nx_ready"], 1)
            dve.wait_ge(S["ot_psum"], 1)
            dve.tensor_copy(XT[:, 0:QH], ps[:, 0, :]).then_inc(S["ot_ready"], 1)
            dve.wait_ge(S["nx_ready"], 1)
            for half in range(NHALF):
                dve.wait_ge(S["y_ready"], half + 1)
                xs = X[:, half * QB:(half + 1) * QB, :].rearrange("p b d -> p (b d)")
                i = dve.tensor_tensor(xs, xs, ps[:, 2 + half, :], ALU.add)
            link(i)
            layernorm(X, Z, link)
            layernorm(Z, NX, link)
            link(over_rows(NX[:, :, :], NX[:, :, :], rows["l1w"], ALU.mult))
            over_rows(NX[:, :, :], NX[:, :, :], rows["l1b"], ALU.add).then_inc(S["nx_ready"], 1)
            dve.wait_ge(S["nxt_psum"], 1)
            dve.tensor_copy(XT[:, 0:QH], ps[:, 4, :]).then_inc(S["nxt_ready"], 1)
            dve.wait_ge(S["q2_proj"], 1)
            dve.tensor_scalar(qf, ps[:, 6:8, :].rearrange("p a n -> p (a n)"), cols[:, 2:3], SCALE,
                              ALU.add, ALU.mult).then_inc(S["q2_f32"], 1)
            dve.wait_ge(S["k2_proj"], 1)
            dve.tensor_scalar(k2f, ps[:, 0:2, :].rearrange("p a n -> p (a n)"), cols[:, 3:4], None,
                              ALU.add).then_inc(S["k2_f32"], 1)
            dve.wait_ge(S["q2_p1"], 1)
            dve.tensor_tensor(qr, qf, q3[:, 0, :], ALU.subtract).then_inc(S["q2_r1"], 1)
            dve.wait_ge(S["k2_p1"], 1)
            dve.tensor_tensor(k2r, k2f, k23[:, 0, :], ALU.subtract).then_inc(S["k2_r1"], 1)
            dve.wait_ge(S["q2_p2"], 1)
            dve.tensor_tensor(q3[:, 2, :], qr, q3[:, 1, :], ALU.subtract).then_inc(S["q2_p3"], 1)
            dve.wait_ge(S["k2_p2"], 1)
            dve.tensor_tensor(k23[:, 2, :], k2r, k23[:, 1, :], ALU.subtract).then_inc(S["k2_p3"], 1)
            dve.wait_ge(S["v2_proj"], 1)
            v2b = rows["bv2"][:, :].rearrange("p (h d) -> p h d", d=HD)
            for half in range(NHALF):
                i = dve.tensor_tensor(V2[:, half * QB:(half + 1) * QB, :, 0:HD],
                                      ps[:, 2 + half, :].rearrange("p (t h d) -> p t h d", t=QB, d=HD),
                                      v2b[:, None, :, :].to_broadcast([P, QB, H, HD]), ALU.add)
            i.then_inc(S["v2_out"], 1)

            for step in range(UNITS + 1):
                n0 = base2(step)
                if step < UNITS:
                    g, half = divmod(step, NHALF)
                    for t in range(TILES2):
                        h, qb = divmod(t, QB)
                        w = (half * QB + qb + 1) * P
                        n = n0 + t
                        slot = n % 2
                        dve.wait_ge(S["p1_ready"], n + READY2)
                        tile = ps[:, 2 * slot:2 * slot + 2, :].rearrange("p a n -> p (a n)")
                        dve.tensor_reduce(C32[:, h, qb:qb + 1], tile[:, 0:w], AX.X, ALU.max, negate=True)\
                           .then_inc(S["p1_free"], 1)
                    n = n0 + TILES2
                    dve.wait_ge(S["p1_free"], n + 2)
                    negated_maxima_parts(None)
                    negated_maxima_rows(q2s[ROWS1:ROWS2, g * HG:(g + 1) * HG, half * QH:(half + 1) * QH],
                                        2 * (n % 2), n + READY2)
                if step > 0:
                    n = n0 + (TILES2 + 1 if step < UNITS else 0)
                    normalise(*divmod(step - 1, NHALF), 2 * (n % 2), n + READY2)

            link(over_rows(Z[:, :, :], Z[:, :, :], rows["bo2"], ALU.add))
            dve.wait_ge(S["o2t_psum"], 1)
            dve.tensor_copy(XT[:, 0:QH], ps[:, 0, :]).then_inc(S["o2t_ready"], 1)
            for half in range(NHALF):
                dve.wait_ge(S["y2_ready"], half + 1)
                zs = Z[:, half * QB:(half + 1) * QB, :].rearrange("p b d -> p (b d)")
                i = dve.tensor_tensor(zs, zs, ps[:, 2 + half, :], ALU.add)
            link(i)
            layernorm(Z, NX, link)
            link(over_rows(NX[:, :, :], NX[:, :, :], rows["l2w"], ALU.mult))
            over_rows(NX[:, :, :], NX[:, :, :], rows["l2b"], ALU.add).then_inc(S["n2_ready"], 1)
            dve.wait_ge(S["n2t_psum"], 1)
            dve.tensor_copy(XT[:, 0:QH], ps[:, 4, :]).then_inc(S["n2t_ready"], 1)
            link(dve.tensor_tensor(X[:, :, :], X[:, :, :], Z[:, :, :], ALU.add))
            dve.wait_ge(S["gl_ready"], 1)
            link(dve.tensor_copy(dgr[:, :, :], ps[:, 6, 0:NB * E].rearrange("p (b e) -> p b e", e=E)))
            for b in range(NB):
                i = dve.max(top[:, b, :], dgr[:, b, :])
            link(i)
            for b in range(NB):
                i = dve.max_index(topi[:, b, :], top[:, b, :], dgr[:, b, :])
            link(i)
            dve.tensor_tensor(gts[:, 0, :], top[:, :, 1], top[:, :, 0], ALU.subtract).then_inc(S["gate_d"], 1)
            link(dve.tensor_copy(topf[:, :, :], topi[:, :, 0:2]))
            dve.wait_ge(S["gate_e"], 1)
            link(dve.tensor_scalar(gts[:, 2, :], gts[:, 1, :], 1.0, None, ALU.add))
            link(dve.reciprocal(gts[:, 2, :], gts[:, 2, :]))
            link(dve.tensor_tensor(gts[:, 3, :], gts[:, 1, :], gts[:, 2, :], ALU.mult))
            for r in range(2):
                for b in range(NB):
                    i = dve.tensor_scalar(dg[:, r, b, :], iota[:, :], topf[:, b, r:r + 1],
                                          gts[:, 2 + r, b:b + 1], ALU.is_equal, ALU.mult)
            link(i)
            link(dve.tensor_tensor(dg[:, 0, :, :], dg[:, 0, :, :], dg[:, 1, :, :], ALU.add))
            link(dve.tensor_copy(dg3[:, :, 0, :], dg[:, 0, :, :]))
            link(dve.tensor_tensor(dgr[:, :, :], dg[:, 0, :, :], dg3[:, :, 0, :], ALU.subtract))
            link(dve.tensor_copy(dg3[:, :, 1, :], dgr[:, :, :]))
            dve.tensor_tensor(dg3[:, :, 2, :], dgr[:, :, :], dg3[:, :, 1, :], ALU.subtract)\
               .then_inc(S["dg_ready"], 1)
            dve.wait_ge(S["gt_psum"], 1)
            for half in range(NHALF):
                q = slice(half * QH, (half + 1) * QH)
                dve.tensor_copy(gT[:, q], ps[0:E, 4 + half, :])
                i = dve.tensor_copy(gT3[:, q], ps[0:PARTS * E, 2 + half, 0:QH // 2].bitcast(BF16))
            i.then_inc(S["gt_ready"], 1)
            for m in range(NHALF * E * FC):
                dve.wait_ge(S["h_gelu"], m + 1)
                dve.wait_ge(S["g_psum"], m // FC + 1)
                if m >= 4:
                    dve.wait_ge(S["h_used"], m - 3)
                dve.tensor_tensor(PRf[:, (4 + m % 4) * QH:(5 + m % 4) * QH],
                                  PRf[:, (m % 4) * QH:(m % 4 + 1) * QH],
                                  ps[:, 4 + (m // FC) % 2, :], ALU.mult).then_inc(S["h_gated"], 1)
            for half in range(NHALF):
                dve.wait_ge(S["yo_psum"], half + 1)
                xs = X[:, half * QB:(half + 1) * QB, :].rearrange("p b d -> p (b d)")
                os = NX[:, half * QB:(half + 1) * QB, :].rearrange("p b d -> p (b d)")
                dve.tensor_tensor(os, xs, ps[:, half, :], ALU.add).then_inc(S["out_ready"], 1)

        @block.tensor
        def _(pe):
            def transposes(src, banks, ready):
                for half, bank in enumerate(banks):
                    for b in range(QB):
                        i = pe.transpose(ps[:, bank, b * P:(b + 1) * P], src[:, half * QB + b, :], ident[:, :])
                    i.then_inc(ready, 1)

            pe.wait_ge(S["wkv_in"], 32)
            seen = 0
            for kind, c in PLAN:
                if kind == "k":
                    pe.wait_ge(ctx_in[c], 16)
                    if c >= 3:
                        pe.wait_ge(S["k_f32"], c - 2)
                    w = cwidth(c)
                    pe.matmul(ps[:, score_bank(c), 0:w], wk[:, :], ctxT[:, c * CW:c * CW + w],
                              start=True, stop=True).then_inc(S["k_proj"], 1)
                if kind == "q":
                    pe.wait_ge(S["xn_ready"], 1)
                    pe.wait_ge(S["const_in"], 32)
                    pe.wait_ge(S["wq_in"], 48)
                    transposes(NX, (0, 1), S["xt_psum"])
                    for half in range(NHALF):
                        pe.wait_ge(S["xt_ready"], half + 1)
                        pe.matmul(ps[:, 2 + half, :], wq[:, :], XT[:, half * QH:(half + 1) * QH],
                                  start=True, stop=True).then_inc(S["q_proj"], 1)
                if kind == "v":
                    if c >= 2:
                        pe.wait_ge(S["v_out"], c - 1)
                    for t in range(4 * c, min(4 * c + 4, KT)):
                        i = pe.matmul(ps[:, c % 2, (t % 4) * D:(t % 4 + 1) * D], ctxT[:, t * P:(t + 1) * P],
                                      wv[:, :], start=True, stop=True)
                    i.then_inc(S["v_proj"], 1)
                if kind == "vt":
                    pe.wait_ge(S["q_f32"], NHALF)
                    for h in range(HG):
                        i = pe.matmul(ps[32 * h:32 * h + TAIL, SLOTS - 1, 0:D], ctxT[:, KT * P:SK], wv[:, :],
                                      start=True, stop=True, tile_position=(0, 32 * h))
                    i.then_inc(S["av_done"], 1)

            def fill(n):
                pe.wait_ge(S["p1_free"], n + 1)

            def max_tile(u, n, t, bank, k0):
                h, qb = divmod(t, QB)
                fill(n)
                pe.matmul(ps[:, bank, 0:MW], QU[0:ROWS1, u % 3, h, qb * P:(qb + 1) * P],
                          keys[(u // NHALF) % 2][0:ROWS1, h, bass.ds(k0, MW)],
                          start=True, stop=True).then_inc(S["p1_ready"], 1)

            def score_tile(u, kt, h, bank):
                n = SPU * u + (h if isinstance(kt, int) and kt == 0 else 1 + HG * kt + h)
                if not isinstance(n, int) or n >= 3:
                    pe.wait_ge(S["exp_done"], n - 2)
                pe.matmul(ps[:, bank, :], keys[(u // NHALF) % 2][0:ROWS2, h, bass.ds(kt * P, P)],
                          QU[0:ROWS2, u % 3, h, :], start=True, stop=True).then_inc(S["s_ready"], 1)

            def values(u, kt, slot):
                first = isinstance(kt, int) and kt == 0
                pe.wait_ge(S["exp_done"], SPU * u + (HG if first else 1 + HG * (kt + 1)))
                pe.wait_ge(S["vst_ready"], KT * u + kt + 1)
                if first and u:
                    pe.wait_ge(S["acc_copied"], u)
                for h in range(HG):
                    i = pe.matmul(ps[32 * h:32 * h + 32, ACC, :], VST[:, slot, h, :],
                                  PR[:, slot, h, :], start=first, stop=False, skip_group_check=True,
                                  tile_position=(0, 32 * h))
                i.then_inc(S["av_done"], 1)
                return i

            def maxima_rows(n, bank):
                fill(n)
                for h in range(HG):
                    for b in range(QB):
                        i = pe.matmul(ps[32 * h:32 * h + PARTS, bank, b * P:(b + 1) * P],
                                      C3[:, h, b, :], identb[:, :], start=True, stop=True,
                                      tile_position=(0, 32 * h))
                i.then_inc(S["p1_ready"], 1)

            def output_blocks(n, bank, copies):
                pe.wait_ge(S["acc_copied"], copies)
                fill(n)
                for b in range(QB):
                    i = pe.transpose(ps[:, bank, b * P:(b + 1) * P], OA[:, b * P:(b + 1) * P], ident[:, :])
                i.then_inc(S["p1_ready"], 1)

            pe.wait_ge(S["zrows_in"], 16)
            pe.wait_ge(S["v_out"], VG)
            def first_tiles(u, *tiles):
                for t in tiles if u < UNITS else ():
                    n = tile_use(u, t)
                    max_tile(u, n, t, n % SLOTS, 0)

            def staged(u):
                g = u // NHALF
                pe.wait_ge(qu_in[u % 3], 16 * 9 * (u // 3 + 1))
                pe.wait_ge(keys_in[g % 2], 16 * (1 + 9 * (g // 2 + 1)))

            staged(0)
            first_tiles(0, *range(AHEAD))
            for step in range(UNITS + 1):
                u1, u2 = (step if step < UNITS else None), (step - 1 if step else None)

                def score(kt, *heads):
                    for h in heads:
                        score_tile(u2, kt, h, score_bank(1 + HG * kt + h))

                first_tiles(step, *range(AHEAD, 2 * AHEAD))
                if u2 is None:
                    first_tiles(step, *range(2 * AHEAD, TILES))
                else:
                    if u2:
                        pe.wait_ge(S["exp_done"], SPU * u2 - 2)
                    for h in range(HG):
                        if h < 2:
                            pe.wait_ge(S["shift_rows"], 2 * u2 + h + 1)
                        elif h == 2:
                            pe.wait_ge(S["shift_rows2"], u2 + 1)
                        else:
                            pe.wait_ge(S["p1_free"], maxima_use(u2) + 1 + SLOTS)
                        score_tile(u2, 0, h, score_bank(h))
                    if step >= 2:
                        n = output_use(step - 2)
                        output_blocks(n, n % SLOTS, step - 1)
                    pe.wait_ge(S["exp_done"], SPU * u2 + 2)
                    for h in range(HG):
                        i = pe.matmul(ps[32 * h:32 * h + 32, score_bank(HG), :],
                                      keys[(u2 // NHALF) % 2][0:ROWS2, h, KT * P:SKP], QU[0:ROWS2, u2 % 3, h, :],
                                      start=True, stop=True, tile_position=(0, 32 * h))
                    i.then_inc(S["s_ready"], 1)
                    first_tiles(step, 4, 5)
                    score(1, 0)
                    first_tiles(step, 6, 7)
                    score(1, 1, 2)
                    first_tiles(step, 8, 9)
                    values(u2, 0, 0)
                    first_tiles(step, 10, 11)
                    score(1, 3)
                    first_tiles(step, 12, 13, 14, 15)

                n0 = loop_use(step)
                with pe.Fori(0, TURNS) as i:
                    t = 0
                    for j in range(STEP):
                        for what in ORDER[j]:
                            if what == "max" and u1 is not None:
                                max_tile(u1, n0 + TILES * i + t, t, (n0 + t) % SLOTS, i * MK + MK)
                                t += 1
                            if what == "values" and u2 is not None:
                                values(u2, i * STEP + (j + 1), (j + 1) % STEP)
                            if isinstance(what, int) and u2 is not None:
                                score_tile(u2, i * STEP + (j + 2), what, score_bank(1 + HG * (j + 2) + what))
                if u2 is not None:
                    values(u2, KT - 1, (KT - 1) % STEP)
                if u1 is not None:
                    if u1 < UNITS - 1:
                        staged(u1 + 1)
                        first_tiles(u1 + 1, *range(AHEAD))
                    pe.wait_ge(S["max_parts"], u1 + 1)
                    maxima_rows(maxima_use(u1), maxima_use(u1) % SLOTS)
                if u2 is not None:
                    pe.matmul(ps[:, ACC, :], VTAIL[:, u2 // NHALF, :], PTAIL[:, :], start=False, stop=True,
                              skip_group_check=True).then_inc(S["av_done"], 1)
            n = output_use(UNITS - 1)
            output_blocks(n, n % SLOTS, UNITS)

            pe.wait_ge(S["late_in"], 16 * 17)
            pe.wait_ge(S["p1_free"], BASE1 + 2)
            transposes(OX, (0, 1), S["ot_psum"])
            pe.wait_ge(S["ot_ready"], 2)
            for half in range(NHALF):
                for b in range(QB):
                    t = half * QB + b
                    i = pe.matmul(ps[:, 2 + half, b * D:(b + 1) * D], XT[:, t * P:(t + 1) * P], wo[:, :],
                                  start=True, stop=True)
                i.then_inc(S["y_ready"], 1)
            pe.wait_ge(S["nx_ready"], 2)
            transposes(NX, (4, 5), S["nxt_psum"])
            pe.wait_ge(S["nxt_ready"], 2)
            for bank, w, s in ((6, 0, "q2_proj"), (0, D, "k2_proj")):
                for half in range(NHALF):
                    i = pe.matmul(ps[:, bank + half, :], wqkv[:, w:w + D], XT[:, half * QH:(half + 1) * QH],
                                  start=True, stop=True)
                i.then_inc(S[s], 1)
            for t in range(NB):
                i = pe.matmul(ps[:, 2 + t // QB, (t % QB) * D:(t % QB + 1) * D], XT[:, t * P:(t + 1) * P],
                              wqkv[:, 2 * D:3 * D], start=True, stop=True)
            i.then_inc(S["v2_proj"], 1)

            pe.wait_ge(S["v2_out"], 1)
            pe.wait_ge(S["q2_in"], 16 * 10)
            pe.wait_ge(S["k2_in"], 16 * 10)
            pe.wait_ge(S["ones_set"], 4 + HG)
            for step in range(UNITS + 1):
                n0 = base2(step)
                u1, u2 = (step if step < UNITS else None), (step - 1 if step else None)

                def max_tiles(tiles):
                    g, half = divmod(u1, NHALF)
                    for t in tiles:
                        h, qb = divmod(t, QB)
                        head = g * HG + h
                        q0 = (half * QB + qb) * P
                        n = n0 + t
                        slot = n % 2
                        fill(n)
                        w = q0 + P
                        for a in range(0, w, 512):
                            b = min(512, w - a)
                            i = pe.matmul(ps[:, 2 * slot + a // 512, 0:b], q2s[0:ROWS1, head, q0:q0 + P],
                                          k2s[0:ROWS1, head, a:a + b], start=True, stop=True)
                        i = pe.matmul(ps[:, 2 * slot + q0 // 512, q0 % 512:q0 % 512 + P], identb[:, :], maskq[:, :],
                                      start=False, stop=True, skip_group_check=True)
                        i.then_inc(S["p1_ready"], 1)

                def values2(u, kt):
                    g, half = divmod(u, NHALF)
                    a = ABASE2[u] + kt
                    c0 = cols2(half, kt)
                    pe.wait_ge(S["exp_done"], SBASE2[u] + HG * (kt + 1))
                    if kt == 0:
                        pe.wait_ge(S["acc_copied"], UNITS + u)
                    for h in range(HG):
                        i = pe.matmul(ps[32 * h:32 * h + VC, ACC, c0:QH], V2[:, kt, g * HG + h, :],
                                      PR[:, a % STEP, h, c0:QH], start=(kt == 0), stop=(kt == kts2(half) - 1),
                                      skip_group_check=True, tile_position=(0, 32 * h))
                    i.then_inc(S["av_done"], 1)

                if u2 is not None:
                    g, half = divmod(u2, NHALF)
                    pe.wait_ge(S["shift_rows"], 2 * (UNITS + u2 + 1))
                    pe.wait_ge(S["p1_free"], base2(u2) + TILES2 + 1 + 2)
                    todo = list(range(TILES2)) if u1 is not None else []
                    per = -(-TILES2 // kts2(half))
                    for kt in range(kts2(half)):
                        c0 = cols2(half, kt)
                        masked = kt >= half * QB
                        for h in range(HG):
                            n = SBASE2[u2] + HG * kt + h
                            pe.wait_ge(S["exp_done"], n - 2)
                            i = pe.matmul(ps[:, score_bank(n), c0:QH], k2s[0:ROWS2, g * HG + h, kt * P:(kt + 1) * P],
                                          q2s[0:ROWS2, g * HG + h, half * QH + c0:(half + 1) * QH],
                                          start=True, stop=True)
                            if masked:
                                i = pe.matmul(ps[:, score_bank(n), c0:c0 + P], identb[:, :], maskk[:, :],
                                              start=False, stop=True, skip_group_check=True)
                            i.then_inc(S["s_ready"], 1)
                            if u1 is not None and todo and h < per:
                                max_tiles([todo.pop(0)])
                        if kt:
                            values2(u2, kt - 1)
                    if u1 is not None:
                        max_tiles(todo)
                    values2(u2, kts2(half) - 1)
                else:
                    max_tiles(range(TILES2))
                if u1 is not None:
                    pe.wait_ge(S["max_parts"], UNITS + u1 + 1)
                    maxima_rows(n0 + TILES2, 2 * ((n0 + TILES2) % 2))
                if u2 is not None:
                    n = n0 + (TILES2 + 1 if u1 is not None else 0)
                    output_blocks(n, 2 * (n % 2), UNITS + u2 + 1)

            pe.wait_ge(S["p1_free"], base2(UNITS) + 1 + 2)
            transposes(OX, (0, 1), S["o2t_psum"])
            pe.wait_ge(S["o2t_ready"], 2)
            for half in range(NHALF):
                for b in range(QB):
                    t = half * QB + b
                    i = pe.matmul(ps[:, 2 + half, b * D:(b + 1) * D], XT[:, t * P:(t + 1) * P], wo2[:, :],
                                  start=True, stop=True)
                i.then_inc(S["y2_ready"], 1)
            pe.wait_ge(S["n2_ready"], 1)
            transposes(NX, (4, 5), S["n2t_psum"])
            pe.wait_ge(S["n2t_ready"], 2)
            for t in range(NB):
                i = pe.matmul(ps[:, 6, t * E:(t + 1) * E], XT[:, t * P:(t + 1) * P], gw[:, :], start=True, stop=True)
            i.then_inc(S["gl_ready"], 1)

            def up(m):
                half, e, c = m // (E * FC), (m // FC) % E, m % FC
                if m >= 4:
                    pe.wait_ge(S["h_gelu"], m - 3)
                pe.matmul(ps[:, m % 4, :], fc1[:, e, c * P:(c + 1) * P], XT[:, half * QH:(half + 1) * QH],
                          start=True, stop=True).then_inc(S["h_psum"], 1)

            def gate(k):
                half, e = divmod(k, E)
                if k >= 2:
                    pe.wait_ge(S["h_gated"], FC * (k - 1))
                pe.matmul(ps[:, 4 + k % 2, :], sel[:, e, :], gT3[:, half * QH:(half + 1) * QH],
                          start=True, stop=True).then_inc(S["g_psum"], 1)

            pe.wait_ge(S["moe_in"], 32)
            pe.wait_ge(S["dg_ready"], 1)
            for t in range(NB):
                half, b = divmod(t, QB)
                pe.transpose(ps[0:E, 4 + half, b * P:(b + 1) * P], dg[:, 0, t, :], ident[:, :])
                i = pe.transpose(ps[0:PARTS * E, 2 + half, b * P // 2:(b + 1) * P // 2].bitcast(BF16),
                                 dg3[:, t, :, :].rearrange("p j e -> p (j e)"), identb[:, :])
            i.then_inc(S["gt_psum"], 1)
            pe.wait_ge(S["gt_ready"], 1)
            gate(0)
            up(0)
            up(1)
            MM = NHALF * E * FC
            for m in range(MM):
                half, e, c = m // (E * FC), (m // FC) % E, m % FC
                if m % FC == 1 and m // FC + 1 < NHALF * E:
                    gate(m // FC + 1)
                if m + 2 < MM:
                    up(m + 2)
                if e == 0 and c == 0:
                    pe.matmul(ps[:, 6 + half, :], fc2b[:, :], gT[:, half * QH:(half + 1) * QH],
                              start=True, stop=False, skip_group_check=True)
                pe.wait_ge(S["h_gated"], m + 1)
                i = pe.matmul(ps[:, 6 + half, :], fc2[:, e, c, :], PRf[:, (4 + m % 4) * QH:(5 + m % 4) * QH],
                              start=False, stop=(e == E - 1 and c == FC - 1), skip_group_check=True)
                i.then_inc(S["h_used"], 1)
            for half in range(NHALF):
                pe.wait_ge(S["yt_copied"], half + 1)
                if half == 0:
                    pe.wait_ge(S["h_gelu"], MM)
                for b in range(QB):
                    t = half * QB + b
                    i = pe.transpose(ps[:, half, b * P:(b + 1) * P], XT[:, t * P:(t + 1) * P], ident[:, :])
                i.then_inc(S["yo_psum"], 1)


def kernel(**inputs):
    import ml_dtypes
    import concourse.bacc as bacc
    from concourse.bass_utils import run_bass_kernel_spmd

    a = {k: np.asarray(v) for k, v in inputs.items()}
    bf = ml_dtypes.bfloat16
    f = lambda n: a["L0_ffn_" + n]
    xa = lambda n: a["L0_xattn_" + n]
    col = lambda v: v.reshape(D, 1)
    row = lambda v: v.reshape(1, D)
    padrows = np.zeros((ROWS2 - PROD, SKP), bf)
    padrows[ROWS1 - PROD:, :SK] = 1
    masked = np.triu(np.ones((P, P), bool), 1)
    sel = np.zeros((PARTS * E, E, P), bf)
    for j in range(PARTS):
        for e in range(E):
            sel[j * E + e, e, :] = 1
    arrays = {
        "x": a["x"], "ctxT": np.ascontiguousarray(a["ctx_1024"][0].T),
        "Wq": xa("Wq"), "Wk": xa("Wk"), "Wv": xa("Wv"), "Wo": xa("Wo"), "Wqkv": f("Wqkv"), "Wo2": f("Wo"),
        "gw": f("gate_W"),
        "cols": np.concatenate([col(xa("bq")), col(xa("bk")), col(f("bqkv")[:D]), col(f("bqkv")[D:2 * D])], 1),
        "bv": row(xa("bv")), "bo": row(xa("bo")), "bv2": row(f("bqkv")[2 * D:]), "bo2": row(f("bo")),
        "l1w": row(f("ln1_w")), "l1b": row(f("ln1_b")), "l2w": row(f("ln2_w")), "l2b": row(f("ln2_b")),
        "fc1T": np.ascontiguousarray(f("fc1_w").transpose(2, 0, 1)),
        "fc2T": np.ascontiguousarray(f("fc2_w").reshape(E, D, FC, P).transpose(3, 0, 2, 1)),
        "b1c": np.ascontiguousarray(f("fc1_b").reshape(E * FC, P).T), "fc2b": f("fc2_b"),
        "ident": np.eye(P, dtype=np.float32), "identb": np.eye(P, dtype=bf),
        "maskq": np.where(masked, -1e30, 0.0).astype(bf), "maskk": np.where(masked.T, -1e30, 0.0).astype(bf),
        "iota": np.tile(np.arange(E, dtype=np.float32), (P, 1)), "sel": sel,
        "zeros": np.zeros((PARTS, P, SKP - SK), bf), "padrows": padrows,
        "zrows": np.zeros((ROWS1 - PROD, 3 * HG * QH), bf),
    }
    nc = bacc.Bacc("TRN2", target_bir_lowering=False, num_devices=1)
    dram = {n: nc.dram_tensor("in_" + n, v.shape, mybir.dt.from_np(v.dtype), kind="ExternalInput").ap()
            for n, v in arrays.items()}
    dram["out"] = nc.dram_tensor("out", (1, N, D), F32, kind="ExternalOutput").ap()
    build(nc, dram)
    r = run_bass_kernel_spmd(nc, [{"in_" + n: v for n, v in arrays.items()}], core_ids=[0])
    return r.results[0]["out"]
```

```python
from contextlib import ExitStack

import numpy as np

import concourse.bass as bass
from concourse import mybir

F32 = mybir.dt.float32
BF16 = mybir.dt.bfloat16
U32 = mybir.dt.uint32
ALU = mybir.AluOpType
ACT = mybir.ActivationFunctionType
AX = mybir.AxisListType

P = 128
D = 128
H, HD = 16, 8
N = 1024
NB = N // P
SK = 6404
KT = SK // P
TAIL = SK - KT * P
SKP = KT * P + 32
HG = 4
NG = H // HG
QH = 512
NHALF = N // QH
UNITS = NG * NHALF
QB = QH // P
PARTS = 3
PROD = PARTS * PARTS * HD
ROWS1 = 96
ROWS2 = ROWS1 + PARTS
VC = HD + 1
STEP = 3
TURNS = (KT - 2) // STEP
MCH = TURNS + 1
MK = SK // MCH
MW = SK - (MCH - 1) * MK
CW = 512
CHUNKS = -(-SK // CW)
KRING = 5
VG = -(-KT // 4)
E, F, FC = 8, 512, 4
SCALE = float(np.float32(1.0) / np.sqrt(np.float32(HD)))
EPS = 1e-5

TILES = HG * QB
SLOTS = 4
AHEAD = 2
SPU = 1 + HG * KT
APU = 1 + KT
ORDER = ((0, "max", 1, "max", 2, "max", "values", "max", 3, "max"),
         (0, "max", 1, "max", 2, "max", "values", "max", 3, "max"),
         (0, "max", 1, "max", "max", 2, "max", "values", "max", 3, "max"))
ORDER_LAST = ((0, 1, 2, 3, "values"),) * STEP
assert MW <= 512 and SPU % 3 == 0 and TURNS * STEP == KT - 2
assert TILES % SLOTS == 0 and sum(o.count("max") for o in ORDER) == TILES


ACT_TURNS = ((0, 3), (3, 5), (5, TURNS))
PE_TURNS = ((0, 1), (1, 2), (2, 6), (6, 7), (7, TURNS))


def with_output(step):
    return 1 if 2 <= step < UNITS else 0


def first_use(step):
    n = AHEAD
    for s in range(step):
        n += TILES * MCH + with_output(s) + 1 - (AHEAD if s == UNITS - 1 else 0)
    return n


def loop_use(step):
    return first_use(step) + with_output(step) + TILES - AHEAD


def tile_use(u, t):
    if t < AHEAD:
        return t if u == 0 else maxima_use(u - 1) - AHEAD + t
    return first_use(u) + t - AHEAD if t < 2 * AHEAD else loop_use(u) - TILES + t


def maxima_use(step):
    return first_use(step + 1) - 1


def output_use(u):
    return first_use(u + 2) + AHEAD if u + 2 < UNITS else first_use(UNITS) + u + 2 - UNITS


def unit2(u):
    half, g = divmod(u, NG)
    return g, half


def kts2(half):
    return (half + 1) * QB


def cols2(half, kt):
    return max(0, kt - half * QB) * P


POST_PORTS = (0, 1, 3, 4, 6, 7)
POST_AT = (1, 4, 7, 11, 14, 18, 23, 26)


def order2():
    HANDOVER = 200
    pe = lambda columns, passes=1: passes * columns / 1.8
    vector = lambda columns: 65 + columns / 0.96
    scalar = lambda columns: 50 + columns / 1.2
    side = []
    for u in range(UNITS):
        side += [("max", u, t) for t in range(HG * QB)]
        if u:
            side.insert(len(side) - HG * QB + AHEAD, ("rows", u - 1, 0))
    side.append(("rows", UNITS - 1, 0))
    main = [(w, u, x) for u in range(UNITS) for kt in range(kts2(u // NG) + 1)
            for w, x in ([("score", (kt, h)) for h in range(HG)] if kt < kts2(u // NG) else [])
            + ([("values", kt - 1)] if kt else [])]
    way = [(0, 1800), (2500, 2000), (6000, 3500), (10500, 3500), (15500, 700), (18000, 1400), (20500, 1300),
           (23000, 1900)]
    staging = 16000
    items, now, dve, act = [], 0.0, 0.0, 0.0
    slot, scores = [0.0, 0.0], [0.0] * 3
    ready, exps, oa, outs = {}, {}, {}, []
    post = [(10000, 1500), (14000, 2000), (20000, 3500), (26000, 1500), (30000, 3000), (36000, 4500),
            (42000, 800), (46000, 800)]
    stage = post_stage = 0
    post_start = None
    while side or main:
        if post_start is not None and post_stage < len(post) and now >= post_start + post[post_stage][0]:
            items.append(("post", post_stage, 0))
            if post_stage in POST_PORTS:
                now = max(now, slot[0]) + 900
            dve = max(dve, now) + post[post_stage][1]
            if post_stage in POST_PORTS:
                slot = [slot[1], dve + HANDOVER]
            post_stage += 1
            continue
        if stage < len(way) and now >= way[stage][0]:
            items.append(("way", stage, 0))
            dve = max(dve, now) + way[stage][1]
            stage += 1
            continue
        starts = []
        free = slot[0]
        if outs and main[:1] != [] and oa[outs[0]] <= now or outs and not main:
            starts.append((max(now, free, oa[outs[0]]) - 1, 0, ("out", outs[0], 0)))
        if side:
            w, u, t = side[0]
            after = ready["parts", u] if w == "rows" else 0.0
            if u == NG and w == "max" and t == 0:
                after = way[-1][0] + staging
            starts.append((max(now, free, after), 1, side[0]))
        if main:
            w, u, x = main[0]
            half = u // NG
            if w == "score" and ("rows", u) in ready:
                starts.append((max(now, scores[0], ready["rows", u]), 2, main[0]))
            if w == "values":
                starts.append((max(now, exps[u, x]), 2, main[0]))
        start, _, item = min(starts)
        items.append(item)
        w, u, x = item
        half = u // NG
        start = max(start, now)
        if w in ("max", "rows", "out"):
            if w == "max":
                columns = (half * QB + x % QB + 1) * P
                now = start + pe(columns + P)
                dve = max(dve, now + HANDOVER) + vector(columns)
                if x == HG * QB - 1:
                    ready["parts", u] = dve + 1000
            if w == "rows":
                now = start + pe(QH, 2)
                dve = max(dve, now + HANDOVER) + vector(QH)
                act = max(act, now + HANDOVER) + (HG - 1) * scalar(QH)
                ready["rows", u] = max(act, dve) + HANDOVER
            if w == "out":
                now = start + pe(QH, 4)
                dve = max(dve, now + HANDOVER) + 600
                outs.pop(0)
                if u == NG - 1:
                    assert stage == len(way)
                    post_start = now
            slot = [slot[1], (max(dve, act) if w == "rows" else dve) + HANDOVER]
            if w != "out":
                side.pop(0)
        else:
            main.pop(0)
            columns = QH - cols2(half, x[0] if w == "score" else x)
            if w == "score":
                now = start + pe(columns + P * (x[0] >= half * QB))
                act = max(act, now + HANDOVER) + scalar(columns)
                scores = scores[1:] + [act + HANDOVER]
                exps[u, x[0]] = act + HANDOVER
            else:
                now = start + pe(columns, 4) + 60
                if x == kts2(half) - 1:
                    act = max(act, now + HANDOVER) + scalar(QH)
                    oa[u] = act + HANDOVER
                    outs.append(u)
    return items + [("out", u, 0) for u in outs]


ITEMS2 = order2()
SLOTTED2 = [x for x in ITEMS2 if x[0] in ("max", "rows", "out") or x[0] == "post" and x[1] in POST_PORTS]
USE2 = {x: n for n, x in enumerate(SLOTTED2)}


def build(nc, A):
    ctx = ExitStack()
    with ctx:
        def sb(name, shape, dt=F32):
            return ctx.enter_context(nc.sbuf_tensor(name, shape, dt))

        def sem(name):
            return ctx.enter_context(nc.semaphore(name))

        ps = ctx.enter_context(nc.psum_tensor("ps", [P, 8, 512], F32))
        ACC = 7
        score_bank = lambda n: 4 + n % 3
        LAST_RING = [4, 5, 6, output_use(UNITS - 1) % SLOTS]
        WAY = [[b for b in range(SLOTS) if b not in (output_use(UNITS - 1) % SLOTS,
                                                   output_use(UNITS - 2) % SLOTS)]
               + [output_use(UNITS - 2) % SLOTS], [1, 3, 3]]
        unit_bank = lambda u, n: LAST_RING[n % len(LAST_RING)] if u == UNITS - 1 else score_bank(n)

        kparts = nc.dram_tensor("kparts", [PARTS, P, SKP], BF16, kind="Internal").ap()
        qparts = nc.dram_tensor("qparts", [PARTS, P, N], BF16, kind="Internal").ap()
        k2parts = nc.dram_tensor("k2parts", [PARTS, P, N], BF16, kind="Internal").ap()
        q2parts = nc.dram_tensor("q2parts", [PARTS, P, N], BF16, kind="Internal").ap()

        KS = sb("KS", [P, 2, HG * SKP], BF16)
        keys = [KS[:, p, :].rearrange("r (h n) -> r h n", h=HG) for p in range(2)]
        ctxT = KS[:, 1, 0:2 * SK].bitcast(F32)
        flat = KS[:, :, :].rearrange("r a n -> r (a n)")
        q2s = [flat[:, a:a + H * QH].rearrange("r (h n) -> r h n", h=H) for a in (0, 2 * H * QH)]
        k2s = [flat[:, a:a + H * QH].rearrange("r (h n) -> r h n", h=H) for a in (H * QH, HG * SKP)]
        w0 = HG * SKP + H * QH
        fc1 = flat[:, w0:w0 + 2 * E * F].bitcast(F32).rearrange("d (e f) -> d e f", e=E)
        fc2 = flat[:, w0 + 2 * E * F:w0 + 4 * E * F].bitcast(F32).rearrange(
            "f (e c d) -> f e c d", e=E, c=FC)
        QU = sb("QU", [P, 3, HG, QH], BF16)
        V = sb("V", [P, KT, H, VC])
        V2 = V[:, 0:NB, :, :]
        VTAIL = sb("VTAIL", [P, NG, P])
        VST = sb("VST", [P, STEP, HG, 32])
        PR = sb("PR", [P, STEP, HG, QH])
        PRf = PR[:, :, :, :].rearrange("k a h q -> k (a h q)")
        PTAIL = sb("PTAIL", [P, QH])
        OA = sb("OA", [P, QH])
        OX = sb("OX", [P, NB, D])
        X = sb("X", [P, NB, D])
        Z = sb("Z", [P, NB, D])
        NX = sb("NX", [P, NB, D])
        XT = sb("XT", [P, N])
        PM = sb("PM", [P, HG, QB, MCH])
        C32 = sb("C32", [P, HG, QB])
        C3 = sb("C3", [P, HG, QB, PARTS], BF16)
        exp_warm = sb("exp_warm", [P, 1])
        RD = sb("RD", [P, QB, HG])
        st = sb("st", [P, NB, 6])
        mv = sb("mv", [P, NB, 2])
        ve = sb("ve", [P, NB])
        sd = sb("sd", [P, NB])
        rs = sb("rs", [P, NB])
        nt = sb("nt", [P, NB])
        ident = sb("ident", [P, P])
        identb = sb("identb", [P, P], BF16)
        maskk = sb("maskk", [P, P], BF16)
        maskq = sb("maskq", [P, P], BF16)
        iota = sb("iota", [P, E])
        sel = sb("sel", [PARTS * E, E, P], BF16)
        wq, wk, wv, wo, wo2 = (sb(n, [P, D]) for n in ("wq", "wk", "wv", "wo", "wo2"))
        wqkv = sb("wqkv", [P, 3 * D])
        gw = sb("gw", [P, E])
        cols = sb("cols", [P, 4])
        b1c = sb("b1c", [P, E * FC])
        fc2b = sb("fc2b", [E, D])
        rows = {n: sb("r_" + n, [P, D]) for n in ("bv", "bo", "l1w", "l1b", "l2w", "l2b", "bv2", "bo2")}
        top = sb("top", [P, NB, E])
        topi = sb("topi", [P, NB, E], U32)
        topf = sb("topf", [P, NB, 2])
        gts = sb("gts", [P, 4, NB])
        dg = sb("dg", [P, 2, NB, E])
        dg3 = sb("dg3", [P, NB, PARTS, E], BF16)
        dgr = sb("dgr", [P, NB, E])
        QUf = QU[:, :, :, :].rearrange("r a h n -> r (a h n)")
        gT = QUf[0:E, 0:2 * N].bitcast(F32)
        gT3 = QUf[0:PARTS * E, 2 * N:3 * N]

        kr = PRf[:, 0:KRING * CW].rearrange("p (a n) -> p a n", a=KRING)
        qf = PRf[:, KRING * CW:KRING * CW + N]
        qr = PRf[:, KRING * CW + N:KRING * CW + 2 * N]
        s0 = KRING * CW + 2 * N
        q3 = PRf[:, s0:s0 + PARTS * N // 2].bitcast(BF16).rearrange("p (j n) -> p j n", j=PARTS)
        K3 = KS[:, 1, 2 * SK:2 * SK + KRING * PARTS * CW].rearrange("p (a j n) -> p a j n", a=KRING, j=PARTS)
        def split_place(half, k):
            place = flat[:, w0:w0 + 4 * E * F].bitcast(F32) if half else flat[:, 2 * H * QH:HG * SKP].bitcast(F32)
            a = k * (2 * QH + PARTS * QH // 2)
            return (place[:, a:a + QH], place[:, a + QH:a + 2 * QH],
                    place[:, a + 2 * QH:a + 2 * QH + PARTS * QH // 2].bitcast(BF16).rearrange(
                        "p (j n) -> p j n", j=PARTS))
        splits = [[split_place(half, k) for k in range(2)] for half in range(NHALF)]
        half_blocks = [slice(half * QB, (half + 1) * QB) for half in range(NHALF)]

        ctx_in = [sem(f"ctx_in{c}") for c in range(CHUNKS)]
        names = """x_in wkv_in wq_in const_in late_in pad_in kstored0 kstored1 kstored2 kstored3 kstored4 rows_in0
            rows_in1 qstored keys_in0 keys_in1 qu_in0 qu_in1 qu_in2 zrows_in k_proj k_p1 k_r1 k_p2 k_p3
            v_proj v_out ones_set ln_var ln_sqrt xn_ready xt_psum xt_ready q_proj q_f32 q_p1 q_r1 q_p2 q_p3
            p1_ready p1_free max_parts shift_rows shift_rows2 shift2_rows s_ready exp_done av_done acc_copied
            vst_ready chain ot_psum ot_ready y_ready nx_ready nxt_psum nxt_ready q2_proj k2_proj v2_proj
            q2_f32 q2_p1 q2_r1 q2_p2 q2_p3 k2_f32 k2_p1 k2_r1 k2_p2 k2_p3 v2_out q2stored k2stored q2_in0
            q2_in1 k2_in0 k2_in1 moe_in n2_ready gate_d gate_e dg_ready post_psum post_read h_psum h_gelu
            g_psum h_gated h_used yt_copied yo_psum out_ready out_done""".split()
        S = {n: sem(n) for n in names}
        kstored = [S[f"kstored{a}"] for a in range(KRING)]
        keys_in = [S["keys_in0"], S["keys_in1"]]
        qu_in = [S["qu_in0"], S["qu_in1"], S["qu_in2"]]

        cwidth = lambda c: min(CW, SK - c * CW)
        PLAN = [("xt", 0), ("v", 0), ("qf", 0), ("v", 1), ("q1", 0), ("v", 2), ("q2", 0)]
        PLAN += [("v", n) for n in range(3, VG)] + [("vt", 0)]

        BASE1 = output_use(UNITS - 1) + 1 + SLOTS - 2
        READY2 = 1 - (SLOTS - 2)
        SBASE2 = [SPU * UNITS]
        ABASE2 = [APU * UNITS]
        for u in range(UNITS):
            SBASE2.append(SBASE2[-1] + HG * kts2(u // NG))
            ABASE2.append(ABASE2[-1] + kts2(u // NG))

        PORTS = [[], []]
        for k in POST_PORTS:
            n = BASE1 + USE2["post", k, 0]
            PORTS[0].append((2 * (n % 2), S["p1_ready"], n + READY2, S["p1_free"], n + 1 + 2))
            c = len(PORTS[1]) + 1
            PORTS[1].append((7, S["post_psum"], c, S["post_read"], c))

        block = ctx.enter_context(nc.Block())

        @block.sync
        def _(sp):
            def put(dst, src, s):
                sp.dma_start(dst, src).then_inc(s, 16)

            put(X[:, :, :], A["x"].rearrange("a (b p) d -> p (a b) d", p=P), S["x_in"])
            put(wk[:, :], A["Wk"], S["wkv_in"])
            put(cols[:, :], A["cols"], S["wkv_in"])
            for c in range(CHUNKS):
                a, w = c * CW, cwidth(c)
                put(ctxT[:, a:a + w], A["ctxT"][:, a:a + w], ctx_in[c])
                if c == 3:
                    put(ident[:, :], A["ident"], S["const_in"])
                    put(wq[:, :], A["Wq"], S["wq_in"])
                    put(wv[:, :], A["Wv"], S["wq_in"])
                    put(rows["bv"][:, :], A["bv"].to_broadcast([P, D]), S["wq_in"])
            put(kparts[:, :, SK:SKP], A["zeros"].rearrange("j p n -> j p n"), S["pad_in"])
            put(identb[:, :], A["identb"], S["const_in"])

            def stage_queries(u):
                g, half = divmod(u, NHALF)
                src = qparts[:, :, half * QH:(half + 1) * QH].rearrange("j (h d) n -> j d h n", d=HD)
                for j in range(PARTS):
                    for i in range(PARTS):
                        r = (PARTS * j + i) * HD
                        put(QU[r:r + HD, u % 3, :, :], src[i, :, g * HG:(g + 1) * HG, :], qu_in[u % 3])

            def stage_keys(g, parts=range(PARTS)):
                src = kparts.rearrange("j (h d) n -> j d h n", d=HD)
                for j in parts:
                    for i in range(PARTS):
                        r = (PARTS * j + i) * HD
                        put(keys[g % 2][r:r + HD, :, :], src[j, :, g * HG:(g + 1) * HG, :], keys_in[g % 2])

            for c in range(CHUNKS):
                sp.wait_ge(S["k_p3"], c + 1)
                a, w = c * CW, cwidth(c)
                put(kparts[:, :, a:a + w].rearrange("j p n -> p j n"), K3[:, c % KRING, :, 0:w], kstored[c % KRING])
            for r in range(KRING):
                sp.wait_ge(kstored[r], 16 * len(range(r, CHUNKS, KRING)))
            sp.wait_ge(S["pad_in"], 16)
            stage_keys(0, [0])
            sp.wait_ge(S["q_p3"], 1)
            put(qparts.rearrange("j p n -> p j n"), q3, S["qstored"])
            stage_keys(0, [1, 2])
            sp.wait_ge(S["qstored"], 16)
            stage_queries(0)
            put(keys[0][PROD:ROWS2, :, :], A["padrows"][:, None, :].to_broadcast([ROWS2 - PROD, HG, SKP]),
                S["rows_in0"])
            put(QU[PROD:ROWS1, :, :, :].rearrange("r a h n -> r (a h n)"), A["zrows"], S["zrows_in"])
            stage_queries(1)
            stage_queries(2)
            for n in ("bo", "l1w", "l1b", "l2w", "l2b", "bv2", "bo2"):
                put(rows[n][:, :], A[n].to_broadcast([P, D]), S["late_in"])
            for dst, n in ((wo, "Wo"), (wo2, "Wo2"), (wqkv, "Wqkv"), (gw, "gw"), (b1c, "b1c"), (fc2b, "fc2b"),
                           (maskk, "maskk"), (maskq, "maskq"), (iota, "iota")):
                put(dst[:, :], A[n], S["late_in"])
            put(sel[:, :, :], A["sel"], S["late_in"])
            sp.wait_ge(S["av_done"], 1)
            put(keys[1][PROD:ROWS2, :, :], A["padrows"][:, None, :].to_broadcast([ROWS2 - PROD, HG, SKP]),
                S["rows_in1"])
            stage_keys(1)
            def fixed_rows(dst, name, a, b, s):
                put(dst[a:b, :, :], A[name][:, None, 0:QH].to_broadcast([b - a, H, QH]), s)

            def stage_half(half):
                n = slice(half * QH, (half + 1) * QH)
                for k, (t, parts) in enumerate((("q2", q2parts), ("k2", k2parts))):
                    sp.wait_ge(S[t + "_p3"], half + 1)
                    put(parts[:, :, n].rearrange("j p n -> p j n"), splits[half][k][2], S[t + "stored"])
                for k, (t, parts, dst) in enumerate((("q2", q2parts, q2s), ("k2", k2parts, k2s))):
                    sp.wait_ge(S[t + "stored"], 16 * (half + 1))
                    src = parts[:, :, n].rearrange("j (h d) n -> j d h n", d=HD)
                    for j in range(PARTS):
                        for i in range(PARTS):
                            r = (PARTS * j + i) * HD
                            put(dst[half][r:r + HD, :, :], src[j if k else i], S[t + f"_in{half}"])

            for u in range(UNITS):
                sp.wait_ge(S["av_done"], 1 + APU * (u + 1))
                if u + 3 < UNITS:
                    stage_queries(u + 3)
                if u % NHALF == NHALF - 1 and u // NHALF + 2 < NG:
                    stage_keys(u // NHALF + 2)
                if u == UNITS - 3:
                    fixed_rows(q2s[0], "zrows", PROD, ROWS1, S["q2_in0"])
                    fixed_rows(k2s[0], "padrows", PROD, ROWS2, S["k2_in0"])
                if u == UNITS - 2:
                    stage_half(0)
                    fixed_rows(q2s[1], "zrows", PROD, ROWS1, S["q2_in1"])
            fixed_rows(k2s[1], "padrows", PROD, ROWS2, S["k2_in1"])
            stage_half(1)
            put(fc1, A["fc1T"], S["moe_in"])
            put(fc2, A["fc2T"], S["moe_in"])
            for half in range(NHALF):
                sp.wait_ge(S["out_ready"], half + 1)
                put(A["out"].rearrange("a (b p) d -> p (a b) d", p=P)[:, half * QB:(half + 1) * QB, :],
                    NX[:, half * QB:(half + 1) * QB, :], S["out_done"])
            sp.wait_ge(S["out_done"], 16 * NHALF)

        @block.gpsimd
        def _(pool):
            pool.memset(V[:, :, :, HD:VC], 1.0).then_inc(S["ones_set"], 1)
            pool.memset(VTAIL[:, :, :], 0.0).then_inc(S["ones_set"], 1)
            pool.memset(VST[:, :, :, :], 0.0).then_inc(S["ones_set"], 1)
            pool.wait_ge(S["ones_set"], 3)
            for h in range(HG):
                pool.memset(VTAIL[32 * h:32 * h + TAIL, :, 32 * h + HD:32 * h + VC], 1.0).then_inc(S["ones_set"], 1)
            pool.wait_ge(S["ones_set"], 3 + HG)
            pool.wait_ge(S["v_out"], VG)

            def stage(u, kt, slot):
                if u or not (isinstance(kt, int) and kt < STEP):
                    pool.wait_ge(S["av_done"], APU * u + kt - 1)
                g = u // NHALF
                pool.tensor_copy(VST[:, slot, :, 0:VC], V[:, bass.ds(kt, 1), g * HG:(g + 1) * HG, :]
                                 .rearrange("k a h c -> k (a h) c")).then_inc(S["vst_ready"], 1)

            for u in range(UNITS):
                stage(u, 0, 0)
                stage(u, 1, 1)
                with pool.Fori(0, TURNS) as i:
                    for j in range(STEP):
                        stage(u, i * STEP + (j + 2), (j + 2) % STEP)

        @block.scalar
        def _(act):
            def ln_sqrt(n, blocks=slice(0, NB)):
                act.wait_ge(S["ln_var"], n)
                act.activation(sd[:, blocks], ve[:, blocks], ACT.Sqrt).then_inc(S["ln_sqrt"], 1)

            act.wait_ge(S["wkv_in"], 32)
            ln_sqrt(1)

            for c in range(CHUNKS + 1):
                if c < CHUNKS:
                    w = cwidth(c)
                    act.wait_ge(S["k_proj"], c + 1)
                    if c >= KRING:
                        act.wait_ge(kstored[c % KRING], 16 * (c // KRING))
                    act.activation(K3[:, c % KRING, 0, 0:w], ps[:, score_bank(c), 0:w], ACT.Identity,
                                   bias=cols[:, 1:2]).then_inc(S["k_p1"], 1)
                if c >= 1:
                    b, w = (c - 1) % KRING, cwidth(c - 1)
                    act.wait_ge(S["k_r1"], c)
                    act.activation(K3[:, b, 1, 0:w], kr[:, b, 0:w], ACT.Copy).then_inc(S["k_p2"], 1)
            for kind, c in PLAN:
                for half in range(NHALF):
                    q = slice(half * QH, (half + 1) * QH)
                    if kind == "q1":
                        act.wait_ge(S["q_f32"], half + 1)
                        act.activation(q3[:, 0, q], qf[:, q], ACT.Copy).then_inc(S["q_p1"], 1)
                    if kind == "q2":
                        act.wait_ge(S["q_r1"], half + 1)
                        act.activation(q3[:, 1, q], qr[:, q], ACT.Copy).then_inc(S["q_p2"], 1)

            def exp_tile(n, dst, src):
                act.wait_ge(S["s_ready"], n + 1)
                act.activation(dst, src, ACT.Exp).then_inc(S["exp_done"], 1)

            def exp_keys(u, kt, at):
                if u or not (isinstance(kt, int) and kt < STEP):
                    act.wait_ge(S["av_done"], APU * u + kt - 1)
                for h in range(HG):
                    first = isinstance(kt, int) and kt == 0
                    n = h if first else 1 + HG * kt + h
                    bank = unit_bank(u, h if first else 1 + HG * at + h)
                    exp_tile(SPU * u + n, PR[:, at % STEP, h, :], ps[:, bank, :])

            def shift_rows(u, dst, bank):
                for h in (0, 1):
                    act.activation(dst[:, h, :], ps[32 * h:32 * h + PARTS, bank, :], ACT.Copy)\
                       .then_inc(S["shift_rows"], 1)

            for step in range(UNITS + 1):
                u = step - 1
                if u >= 0:
                    exp_keys(u, 0, 0)
                    if u:
                        act.wait_ge(S["av_done"], 1 + APU * u)
                    exp_tile(SPU * u + HG, PTAIL[:, :], ps[:, unit_bank(u, HG), :])
                    exp_keys(u, 1, 1)
                    for begin, end in ACT_TURNS if u == UNITS - 1 else ((0, TURNS),):
                        if begin:
                            ln_sqrt(2 if begin == ACT_TURNS[1][0] else 3, half_blocks[0])
                            act.activation(exp_warm[:, :], cols[:, 0:1], ACT.Exp)
                        with act.Fori(begin, end) as i:
                            for j in range(STEP):
                                exp_keys(u, i * STEP + (j + 2), j + 2)
                if step < UNITS:
                    n = maxima_use(step)
                    act.wait_ge(S["p1_ready"], n + 1)
                    shift_rows(step, QU[ROWS1:ROWS2, step % 3, :, :], n % SLOTS)
                if u >= 0:
                    act.wait_ge(S["av_done"], 1 + APU * (u + 1))
                    if u:
                        act.wait_ge(S["p1_free"], output_use(u - 1) + 1 + SLOTS)
                    act.activation(OA[:, :], ps[:, ACC, :], ACT.Copy).then_inc(S["acc_copied"], 1)

            def post(k, half):
                if k == 2:
                    ln_sqrt(6 + half, half_blocks[half])
                if k == 5:
                    act.wait_ge(S["gate_d"], half + 1)
                    act.activation(gts[:, 1, half_blocks[half]], gts[:, 0, half_blocks[half]], ACT.Exp)\
                       .then_inc(S["gate_e"], 1)

            for what, u, x in ITEMS2:
                if what == "way":
                    if u in (2, 3):
                        ln_sqrt(2 + u, half_blocks[1])
                    if u in (5, 6):
                        part = u - 5
                        for k, t in enumerate(("q2", "k2")):
                            f, r, parts = splits[1][k]
                            act.wait_ge(S[t + ("_r1" if part else "_f32")], 2 - part)
                            act.activation(parts[:, part, :], r if part else f, ACT.Copy)\
                               .then_inc(S[t + f"_p{part + 1}"], 1)
                    continue
                if what == "post":
                    post(u, 0)
                    continue
                g, half = unit2(u)
                if what == "score":
                    kt, h = x
                    a = ABASE2[u] + kt
                    if h == 0:
                        act.wait_ge(S["av_done"], a - STEP + 2)
                    c0 = cols2(half, kt)
                    n = SBASE2[u] + HG * kt + h
                    exp_tile(n, PR[:, a % STEP, h, c0:QH], ps[:, score_bank(n), c0:QH])
                if what == "values" and x == kts2(half) - 1:
                    act.wait_ge(S["av_done"], 1 + ABASE2[u + 1])
                    if u:
                        act.wait_ge(S["p1_free"], BASE1 + USE2["out", u - 1, 0] + 1 + 2)
                    act.activation(OA[:, :], ps[:, ACC, :], ACT.Copy).then_inc(S["acc_copied"], 1)
                if what == "rows":
                    n = BASE1 + USE2[what, u, x]
                    act.wait_ge(S["p1_ready"], n + READY2)
                    for h in range(HG - 1):
                        act.activation(q2s[half][ROWS1:ROWS2, g * HG + h, :],
                                       ps[32 * h:32 * h + PARTS, 2 * (n % 2), :], ACT.Copy)\
                           .then_inc(S["shift2_rows"], 1)

            for m in range(NHALF * E * FC):
                if m in POST_AT:
                    post(POST_AT.index(m), 1)
                e, c = (m // FC) % E, m % FC
                act.wait_ge(S["h_psum"], m + 1)
                if m >= 4:
                    act.wait_ge(S["h_gated"], m - 3)
                act.activation(PRf[:, (m % 4) * QH:(m % 4 + 1) * QH], ps[:, m % 4, :], ACT.Gelu,
                               bias=b1c[:, e * FC + c:e * FC + c + 1]).then_inc(S["h_gelu"], 1)
            for half in range(NHALF):
                act.wait_ge(S["h_used"], (half + 1) * E * FC)
                act.activation(XT[:, half * QH:(half + 1) * QH], ps[:, 6 + half, :], ACT.Copy)\
                   .then_inc(S["yt_copied"], 1)

        @block.vector
        def _(dve):
            chained = [0]

            maxima_out = [0]

            def link(ins):
                chained[0] += 1
                ins.then_inc(S["chain"], 1)
                dve.wait_ge(S["chain"], chained[0])

            lns = [0]

            def layernorm_statistics(src, blocks=slice(0, NB)):
                bs = range(blocks.start, blocks.stop)
                for b in bs:
                    i = dve.bn_stats(st[:, b, :], src[:, b, :])
                link(i)
                for b in bs:
                    i = dve.bn_aggr(mv[:, b, :], st[:, b, :])
                link(i)
                lns[0] += 1
                dve.tensor_scalar(ve[:, blocks], mv[:, blocks, 1], EPS, None, ALU.add).then_inc(S["ln_var"], 1)

            def layernorm_rows(src, dst, last, blocks=slice(0, NB)):
                bs = range(blocks.start, blocks.stop)
                v, r, t = ve[:, blocks], rs[:, blocks], nt[:, blocks]
                dve.wait_ge(S["ln_sqrt"], lns[0])
                link(dve.reciprocal(r, sd[:, blocks]))
                link(dve.tensor_tensor(t, r, r, ALU.mult))
                link(dve.tensor_tensor(t, t, v, ALU.mult))
                link(dve.tensor_scalar(t, t, -0.5, 1.5, ALU.mult, ALU.add))
                link(dve.tensor_tensor(r, r, t, ALU.mult))
                for b in bs:
                    i = dve.tensor_scalar(dst[:, b, :], src[:, b, :], mv[:, b, 0:1], rs[:, b:b + 1],
                                          ALU.subtract, ALU.mult)
                last(i)

            def over_rows(dst, in0, row, op, blocks=slice(0, NB)):
                n = blocks.stop - blocks.start
                return dve.tensor_tensor(dst[:, blocks, :], in0[:, blocks, :],
                                         row[:, None, :].to_broadcast([P, n, D]), op)

            dve.wait_ge(S["x_in"], 16)
            layernorm_statistics(X)
            layernorm_rows(X, NX, lambda i: i.then_inc(S["xn_ready"], 1))

            vb = rows["bv"][:, :].rearrange("p (h d) -> p h d", d=HD)
            dve.wait_ge(S["wkv_in"], 32)
            for c in range(CHUNKS + 1):
                if c < CHUNKS:
                    b, w = c % KRING, cwidth(c)
                    dve.wait_ge(S["k_p1"], c + 1)
                    if c >= KRING:
                        dve.wait_ge(S["k_p3"], c - KRING + 1)
                    dve.scalar_tensor_tensor(out=kr[:, b, 0:w], in0=ps[:, score_bank(c), 0:w], scalar=cols[:, 1:2],
                                             in1=K3[:, b, 0, 0:w], op0=ALU.add, op1=ALU.subtract)\
                       .then_inc(S["k_r1"], 1)
                if c >= 1:
                    b, w = (c - 1) % KRING, cwidth(c - 1)
                    dve.wait_ge(S["k_p2"], c)
                    dve.tensor_tensor(K3[:, b, 2, 0:w], kr[:, b, 0:w], K3[:, b, 1, 0:w],
                                      ALU.subtract).then_inc(S["k_p3"], 1)
            for kind, c in PLAN:
                for half in range(NHALF):
                    q = slice(half * QH, (half + 1) * QH)
                    if kind == "xt":
                        dve.wait_ge(S["xt_psum"], half + 1)
                        dve.tensor_copy(XT[:, q], ps[:, half, :]).then_inc(S["xt_ready"], 1)
                    if kind == "qf":
                        dve.wait_ge(S["q_proj"], half + 1)
                        dve.tensor_scalar(qf[:, q], ps[:, 2 + half, :], cols[:, 0:1], SCALE,
                                          ALU.add, ALU.mult).then_inc(S["q_f32"], 1)
                    if kind == "q1":
                        dve.wait_ge(S["q_p1"], half + 1)
                        dve.tensor_tensor(qr[:, q], qf[:, q], q3[:, 0, q], ALU.subtract).then_inc(S["q_r1"], 1)
                if kind == "q2":
                    dve.wait_ge(S["q_p2"], NHALF)
                    dve.tensor_tensor(q3[:, 2, :], qr, q3[:, 1, :], ALU.subtract).then_inc(S["q_p3"], 1)
                if kind == "v":
                    n = min(4, KT - 4 * c)
                    dve.wait_ge(S["v_proj"], c + 1)
                    dve.wait_ge(S["wq_in"], 48)
                    dve.tensor_tensor(V[:, 4 * c:4 * c + n, :, 0:HD],
                                      ps[:, score_bank(CHUNKS + c), 0:n * D].rearrange("p (t h d) -> p t h d", t=n, d=HD),
                                      vb[:, None, :, :].to_broadcast([P, n, H, HD]), ALU.add)\
                       .then_inc(S["v_out"], 1)
                if kind == "vt":
                    dve.wait_ge(S["av_done"], 1)
                    dve.wait_ge(S["ones_set"], 3 + HG)
                    for h in range(HG):
                        r = slice(32 * h, 32 * h + TAIL)
                        i = dve.tensor_tensor(
                            VTAIL[r, :, 32 * h:32 * h + HD],
                            ps[r, SLOTS - 1, 0:D].rearrange("p (g h d) -> p g h d", g=NG, d=HD)[:, :, h, :],
                            vb[r, :, :].rearrange("p (g h) d -> p g h d", g=NG)[:, :, h, :], ALU.add)
                        i.then_inc(S["p1_free"], 1)

            def negated_maxima_parts(partial):
                if partial is not None:
                    link(dve.tensor_reduce(C32[:, :, :], partial, AX.X, ALU.max, negate=True))
                for part in range(PARTS - 1):
                    link(dve.tensor_copy(C3[:, :, :, part], C32[:, :, :]))
                    link(dve.tensor_tensor(C32[:, :, :], C32[:, :, :], C3[:, :, :, part], ALU.subtract))
                dve.tensor_copy(C3[:, :, :, PARTS - 1], C32[:, :, :]).then_inc(S["max_parts"], 1)
                maxima_out[0] += 1
                dve.wait_ge(S["max_parts"], maxima_out[0])

            def negated_maxima_rows(dst, bank, n):
                dve.wait_ge(S["p1_ready"], n)
                dve.tensor_copy(dst[:, 2, :], ps[64:64 + PARTS, bank, :]).then_inc(S["shift_rows2"], 1)
                dve.tensor_copy(dst[:, 3, :], ps[96:96 + PARTS, bank, :]).then_inc(S["p1_free"], 1)

            def normalise(g, half, bank, n):
                dve.wait_ge(S["p1_ready"], n)
                t = ps[:, bank, :].rearrange("p (b h c) -> p b h c", b=QB, c=32)
                link(dve.reciprocal(RD[:, :, :], t[:, :, :, HD]))
                o = OX[:, half * QB:(half + 1) * QB, g * HG * HD:(g + 1) * HG * HD]
                dve.tensor_tensor(o.rearrange("p b (h d) -> p b h d", d=HD), t[:, :, :, 0:HD],
                                  RD[:, :, :, None].to_broadcast([P, QB, HG, HD]), ALU.mult)\
                   .then_inc(S["p1_free"], 1)

            def reduce_tile(n, t, bank, at):
                h, qb = divmod(t, QB)
                dve.wait_ge(S["p1_ready"], n + 1)
                dve.tensor_reduce(PM[:, h, qb, at], ps[:, bank, 0:MW], AX.X, ALU.max).then_inc(S["p1_free"], 1)

            def reduce_first(u, tiles):
                for t in tiles:
                    n = tile_use(u, t)
                    reduce_tile(n, t, n % SLOTS, slice(0, 1))

            reduce_first(0, range(AHEAD))
            for step in range(UNITS):
                reduce_first(step, range(AHEAD, 2 * AHEAD))
                if with_output(step):
                    n = output_use(step - 2)
                    normalise(*divmod(step - 2, NHALF), n % SLOTS, n + 1)
                reduce_first(step, range(2 * AHEAD, TILES))
                n0 = loop_use(step)
                with dve.Fori(0, TURNS) as i:
                    for t in range(TILES):
                        reduce_tile(n0 + TILES * i + t, t, (n0 + t) % SLOTS, bass.ds(i + 1, 1))
                dve.wait_ge(S["p1_free"], n0 + TILES * TURNS + SLOTS)
                negated_maxima_parts(PM[:, :, :, :])
                if step < UNITS - 1:
                    reduce_first(step + 1, range(AHEAD))
                n = maxima_use(step)
                negated_maxima_rows(QU[ROWS1:ROWS2, step % 3, :, :], n % SLOTS, n + 1)
            v2b = rows["bv2"][:, :].rearrange("p (h d) -> p h d", d=HD)
            dve.wait_ge(S["late_in"], 16 * 17)
            def way(half):
                bank_a, bank_b, bank_c = WAY[half]
                n = output_use(UNITS - 2 + half)
                normalise(NG - 1, half, n % SLOTS, n + 1)
                blocks = half_blocks[half]
                columns = slice(half * QH, (half + 1) * QH)
                over_rows(X, X, rows["bo"], ALU.add, blocks).then_inc(S["nx_ready"], 1)
                dve.wait_ge(S["ot_psum"], half + 1)
                dve.tensor_copy(XT[:, columns], ps[:, bank_a, :]).then_inc(S["ot_ready"], 1)
                yield
                dve.wait_ge(S["nx_ready"], 2 * half + 1)
                dve.wait_ge(S["y_ready"], half + 1)
                xs = X[:, blocks, :].rearrange("p b d -> p (b d)")
                link(dve.tensor_tensor(xs, xs, ps[:, bank_b, :], ALU.add))
                layernorm_statistics(X, blocks)
                yield
                layernorm_rows(X, Z, link, blocks)
                layernorm_statistics(Z, blocks)
                yield
                layernorm_rows(Z, NX, link, blocks)
                link(over_rows(NX, NX, rows["l1w"], ALU.mult, blocks))
                over_rows(NX, NX, rows["l1b"], ALU.add, blocks).then_inc(S["nx_ready"], 1)
                yield
                dve.wait_ge(S["nxt_psum"], half + 1)
                dve.tensor_copy(XT[:, columns], ps[:, bank_a, :]).then_inc(S["nxt_ready"], 1)
                yield
                (fq, rq, q3s), (fk, rk, k3s) = splits[half]
                dve.wait_ge(S["q2_proj"], half + 1)
                dve.tensor_scalar(fq, ps[:, bank_b, :], cols[:, 2:3], SCALE, ALU.add, ALU.mult)\
                   .then_inc(S["q2_f32"], 1)
                dve.wait_ge(S["k2_proj"], half + 1)
                dve.tensor_scalar(fk, ps[:, bank_a, :], cols[:, 3:4], None, ALU.add).then_inc(S["k2_f32"], 1)
                if half == 0:
                    dve.wait_ge(S["q2_f32"], 1)
                    dve.wait_ge(S["k2_f32"], 1)
                    for f, r, parts, done in ((fq, rq, q3s, "q2_p3"), (fk, rk, k3s, "k2_p3")):
                        link(dve.tensor_copy(parts[:, 0, :], f))
                        link(dve.tensor_tensor(r, f, parts[:, 0, :], ALU.subtract))
                        link(dve.tensor_copy(parts[:, 1, :], r))
                        dve.tensor_tensor(parts[:, 2, :], r, parts[:, 1, :], ALU.subtract).then_inc(S[done], 1)
                else:
                    for part, j in (("_r1", 0), ("_p3", 1)):
                        yield
                        for t, (f, r, parts) in (("q2", splits[1][0]), ("k2", splits[1][1])):
                            dve.wait_ge(S[t + f"_p{j + 1}"], 1)
                            dve.tensor_tensor(parts[:, 2, :] if j else r, r if j else f, parts[:, j, :],
                                              ALU.subtract).then_inc(S[t + part], 1)
                dve.wait_ge(S["v2_proj"], half + 1)
                dve.wait_ge(S["vst_ready"], KT * (UNITS - 1) + (half + 1) * QB)
                dve.tensor_tensor(V2[:, blocks, :, 0:HD], ps[:, bank_c, :].rearrange("p (t h d) -> p t h d", t=QB, d=HD),
                                  v2b[:, None, :, :].to_broadcast([P, QB, H, HD]), ALU.add).then_inc(S["v2_out"], 1)
                yield

            for _ in way(0):
                pass
            second = way(1)

            def post(half):
                ports = iter(PORTS[half])
                blocks = half_blocks[half]
                columns = slice(half * QH, (half + 1) * QH)

                def port():
                    bank, ready, n, read, count = next(ports)
                    dve.wait_ge(ready, n)
                    return bank, read, count

                link(over_rows(Z, Z, rows["bo2"], ALU.add, blocks))
                bank, read, _ = port()
                dve.tensor_copy(XT[:, columns], ps[:, bank, :]).then_inc(read, 1)
                yield
                bank, read, count = port()
                zs = Z[:, blocks, :].rearrange("p b d -> p (b d)")
                dve.tensor_tensor(zs, zs, ps[:, bank, :], ALU.add).then_inc(read, 1)
                dve.wait_ge(read, count)
                layernorm_statistics(Z, blocks)
                yield
                layernorm_rows(Z, NX, link, blocks)
                link(over_rows(NX, NX, rows["l2w"], ALU.mult, blocks))
                over_rows(NX, NX, rows["l2b"], ALU.add, blocks).then_inc(S["n2_ready"], 1)
                yield
                bank, read, _ = port()
                dve.tensor_copy(XT[:, columns], ps[:, bank, :]).then_inc(read, 1)
                link(dve.tensor_tensor(X[:, blocks, :], X[:, blocks, :], Z[:, blocks, :], ALU.add))
                yield
                bank, read, count = port()
                dve.tensor_copy(dgr[:, blocks, :], ps[:, bank, 0:QB * E].rearrange("p (b e) -> p b e", e=E))\
                   .then_inc(read, 1)
                dve.wait_ge(read, count)
                bs = range(blocks.start, blocks.stop)
                for b in bs:
                    i = dve.max(top[:, b, :], dgr[:, b, :])
                link(i)
                for b in bs:
                    i = dve.max_index(topi[:, b, :], top[:, b, :], dgr[:, b, :])
                link(i)
                dve.tensor_tensor(gts[:, 0, blocks], top[:, blocks, 1], top[:, blocks, 0], ALU.subtract)\
                   .then_inc(S["gate_d"], 1)
                link(dve.tensor_copy(topf[:, blocks, :], topi[:, blocks, 0:2]))
                yield
                dve.wait_ge(S["gate_e"], half + 1)
                link(dve.tensor_scalar(gts[:, 2, blocks], gts[:, 1, blocks], 1.0, None, ALU.add))
                link(dve.reciprocal(gts[:, 2, blocks], gts[:, 2, blocks]))
                link(dve.tensor_tensor(gts[:, 3, blocks], gts[:, 1, blocks], gts[:, 2, blocks], ALU.mult))
                for r in range(2):
                    for b in bs:
                        i = dve.tensor_scalar(dg[:, r, b, :], iota[:, :], topf[:, b, r:r + 1],
                                              gts[:, 2 + r, b:b + 1], ALU.is_equal, ALU.mult)
                link(i)
                link(dve.tensor_tensor(dg[:, 0, blocks, :], dg[:, 0, blocks, :], dg[:, 1, blocks, :], ALU.add))
                link(dve.tensor_copy(dg3[:, blocks, 0, :], dg[:, 0, blocks, :]))
                link(dve.tensor_tensor(dgr[:, blocks, :], dg[:, 0, blocks, :], dg3[:, blocks, 0, :], ALU.subtract))
                link(dve.tensor_copy(dg3[:, blocks, 1, :], dgr[:, blocks, :]))
                dve.tensor_tensor(dg3[:, blocks, 2, :], dgr[:, blocks, :], dg3[:, blocks, 1, :], ALU.subtract)\
                   .then_inc(S["dg_ready"], 1)
                yield
                bank, read, _ = port()
                dve.tensor_copy(gT[:, columns], ps[0:E, bank, :]).then_inc(read, 1)
                yield
                bank, read, _ = port()
                dve.tensor_copy(gT3[:, columns], ps[0:PARTS * E, bank, 0:QH // 2].bitcast(BF16)).then_inc(read, 1)
                yield

            post0, post1 = post(0), post(1)
            for what, u, t in ITEMS2:
                if what == "way":
                    next(second)
                if what == "post":
                    next(post0)
                if what not in ("max", "rows", "out"):
                    continue
                g, half = unit2(u)
                n = BASE1 + USE2[what, u, t]
                bank = 2 * (n % 2)
                if what == "max":
                    h, qb = divmod(t, QB)
                    w = (half * QB + qb + 1) * P
                    dve.wait_ge(S["p1_ready"], n + READY2)
                    tile = ps[:, bank:bank + 2, :].rearrange("p a n -> p (a n)")
                    dve.tensor_reduce(C32[:, h, qb:qb + 1], tile[:, 0:w], AX.X, ALU.max, negate=True)\
                       .then_inc(S["p1_free"], 1)
                    if t == TILES - 1:
                        dve.wait_ge(S["p1_free"], n + 1 + 2)
                        negated_maxima_parts(None)
                if what == "rows":
                    dve.wait_ge(S["p1_ready"], n + READY2)
                    dve.tensor_copy(q2s[half][ROWS1:ROWS2, g * HG + 3, :],
                                    ps[96:96 + PARTS, bank, :]).then_inc(S["p1_free"], 1)
                if what == "out":
                    normalise(g, half, bank, n + READY2)

            for m in range(NHALF * E * FC):
                if m in POST_AT:
                    next(post1)
                dve.wait_ge(S["h_gelu"], m + 1)
                dve.wait_ge(S["g_psum"], m // FC + 1)
                if m >= 4:
                    dve.wait_ge(S["h_used"], m - 3)
                dve.tensor_tensor(PRf[:, (4 + m % 4) * QH:(5 + m % 4) * QH],
                                  PRf[:, (m % 4) * QH:(m % 4 + 1) * QH],
                                  ps[:, 4 + (m // FC) % 2, :], ALU.mult).then_inc(S["h_gated"], 1)
            for half in range(NHALF):
                dve.wait_ge(S["yo_psum"], half + 1)
                xs = X[:, half * QB:(half + 1) * QB, :].rearrange("p b d -> p (b d)")
                os = NX[:, half * QB:(half + 1) * QB, :].rearrange("p b d -> p (b d)")
                dve.tensor_tensor(os, xs, ps[:, half, :], ALU.add).then_inc(S["out_ready"], 1)

        @block.tensor
        def _(pe):
            def transposes(src, banks, ready):
                for half, bank in enumerate(banks):
                    for b in range(QB):
                        i = pe.transpose(ps[:, bank, b * P:(b + 1) * P], src[:, half * QB + b, :], ident[:, :])
                    i.then_inc(ready, 1)

            pe.wait_ge(S["wkv_in"], 32)
            for c in range(CHUNKS):
                w = cwidth(c)
                pe.wait_ge(ctx_in[c], 16)
                if c >= 3:
                    pe.wait_ge(S["k_r1"], c - 2)
                pe.matmul(ps[:, score_bank(c), 0:w], wk[:, :], ctxT[:, c * CW:c * CW + w],
                          start=True, stop=True).then_inc(S["k_proj"], 1)
            for kind, c in PLAN:
                if kind == "xt":
                    pe.wait_ge(S["xn_ready"], 1)
                    pe.wait_ge(S["const_in"], 32)
                    pe.wait_ge(S["wq_in"], 48)
                    transposes(NX, (0, 1), S["xt_psum"])
                if kind == "qf":
                    for half in range(NHALF):
                        pe.wait_ge(S["xt_ready"], half + 1)
                        pe.matmul(ps[:, 2 + half, :], wq[:, :], XT[:, half * QH:(half + 1) * QH],
                                  start=True, stop=True).then_inc(S["q_proj"], 1)
                if kind == "v":
                    if c < 3:
                        pe.wait_ge(S["k_r1"], CHUNKS + c - 2)
                    else:
                        pe.wait_ge(S["v_out"], c - 2)
                    for t in range(4 * c, min(4 * c + 4, KT)):
                        i = pe.matmul(ps[:, score_bank(CHUNKS + c), (t % 4) * D:(t % 4 + 1) * D],
                                      ctxT[:, t * P:(t + 1) * P], wv[:, :], start=True, stop=True)
                    i.then_inc(S["v_proj"], 1)
                if kind == "vt":
                    pe.wait_ge(S["q_f32"], NHALF)
                    for h in range(HG):
                        i = pe.matmul(ps[32 * h:32 * h + TAIL, SLOTS - 1, 0:D], ctxT[:, KT * P:SK], wv[:, :],
                                      start=True, stop=True, tile_position=(0, 32 * h))
                    i.then_inc(S["av_done"], 1)

            def fill(n):
                pe.wait_ge(S["p1_free"], n + 1)

            def max_tile(u, n, t, bank, k0):
                h, qb = divmod(t, QB)
                fill(n)
                pe.matmul(ps[:, bank, 0:MW], QU[0:PROD, u % 3, h, qb * P:(qb + 1) * P],
                          keys[(u // NHALF) % 2][0:PROD, h, bass.ds(k0, MW)],
                          start=True, stop=True).then_inc(S["p1_ready"], 1)

            def score_tile(u, kt, h, bank):
                k = h if isinstance(kt, int) and kt == 0 else 1 + HG * kt + h
                n = SPU * u + k
                if u == UNITS - 1:
                    first = isinstance(k, int) and k < len(LAST_RING)
                    pe.wait_ge(S["exp_done"], SPU * u if first else n - len(LAST_RING) + 1)
                elif not isinstance(n, int) or n >= 3:
                    pe.wait_ge(S["exp_done"], n - 2)
                pe.matmul(ps[:, bank, :], keys[(u // NHALF) % 2][0:ROWS2, h, bass.ds(kt * P, P)],
                          QU[0:ROWS2, u % 3, h, :], start=True, stop=True).then_inc(S["s_ready"], 1)

            def values(u, kt, slot):
                first = isinstance(kt, int) and kt == 0
                pe.wait_ge(S["exp_done"], SPU * u + (HG if first else 1 + HG * (kt + 1)))
                pe.wait_ge(S["vst_ready"], KT * u + kt + 1)
                if first and u:
                    pe.wait_ge(S["acc_copied"], u)
                for h in range(HG):
                    i = pe.matmul(ps[32 * h:32 * h + 32, ACC, :], VST[:, slot, h, :],
                                  PR[:, slot, h, :], start=first, stop=False, skip_group_check=True,
                                  tile_position=(0, 32 * h))
                i.then_inc(S["av_done"], 1)
                return i

            def maxima_rows(n, bank):
                fill(n)
                for h in range(HG):
                    for b in range(QB):
                        i = pe.matmul(ps[32 * h:32 * h + PARTS, bank, b * P:(b + 1) * P],
                                      C3[:, h, b, :], identb[:, :], start=True, stop=True,
                                      tile_position=(0, 32 * h))
                i.then_inc(S["p1_ready"], 1)

            def output_blocks(n, bank, copies):
                pe.wait_ge(S["acc_copied"], copies)
                fill(n)
                for b in range(QB):
                    i = pe.transpose(ps[:, bank, b * P:(b + 1) * P], OA[:, b * P:(b + 1) * P], ident[:, :])
                i.then_inc(S["p1_ready"], 1)

            def transpose_output(half):
                if half == 0:
                    pe.wait_ge(S["late_in"], 16 * 17)
                pe.wait_ge(S["p1_free"], output_use(UNITS - 2 + half) + 1 + SLOTS)
                for b in range(QB):
                    i = pe.transpose(ps[:, WAY[half][0], b * P:(b + 1) * P], OX[:, half * QB + b, :], ident[:, :])
                i.then_inc(S["ot_psum"], 1)

            def project_output(half):
                pe.wait_ge(S["ot_ready"], half + 1)
                for b in range(QB):
                    t = half * QB + b
                    i = pe.matmul(ps[:, WAY[half][1], b * D:(b + 1) * D], XT[:, t * P:(t + 1) * P], wo[:, :],
                                  start=True, stop=True)
                i.then_inc(S["y_ready"], 1)

            def transpose_normalised(half):
                pe.wait_ge(S["nx_ready"], 2 * half + 2)
                for b in range(QB):
                    i = pe.transpose(ps[:, WAY[half][0], b * P:(b + 1) * P], NX[:, half * QB + b, :], ident[:, :])
                i.then_inc(S["nxt_psum"], 1)

            def project_qkv(half):
                pe.wait_ge(S["nxt_ready"], half + 1)
                columns = slice(half * QH, (half + 1) * QH)
                pe.matmul(ps[:, WAY[half][1], :], wqkv[:, 0:D], XT[:, columns], start=True, stop=True)\
                  .then_inc(S["q2_proj"], 1)
                pe.matmul(ps[:, WAY[half][0], :], wqkv[:, D:2 * D], XT[:, columns], start=True, stop=True)\
                  .then_inc(S["k2_proj"], 1)
                if half:
                    pe.wait_ge(S["q2_f32"], 2)
                for b in range(QB):
                    t = half * QB + b
                    i = pe.matmul(ps[:, WAY[half][2], b * D:(b + 1) * D], XT[:, t * P:(t + 1) * P], wqkv[:, 2 * D:3 * D],
                                  start=True, stop=True)
                i.then_inc(S["v2_proj"], 1)

            ON_THE_WAY = (transpose_output, project_output, transpose_normalised, project_qkv)

            pe.wait_ge(S["v_out"], VG)
            def first_tiles(u, *tiles):
                for t in tiles if u < UNITS else ():
                    n = tile_use(u, t)
                    max_tile(u, n, t, n % SLOTS, 0)

            def staged(u):
                g = u // NHALF
                pe.wait_ge(qu_in[u % 3], 16 * 9 * (u // 3 + 1))
                pe.wait_ge(keys_in[g % 2], 16 * 9 * (g // 2 + 1))

            staged(0)
            first_tiles(0, *range(AHEAD))
            for step in range(UNITS + 1):
                u1, u2 = (step if step < UNITS else None), (step - 1 if step else None)

                def score(kt, *heads):
                    for h in heads:
                        score_tile(u2, kt, h, unit_bank(u2, 1 + HG * kt + h))

                first_tiles(step, *range(AHEAD, 2 * AHEAD))
                if u2 is None:
                    first_tiles(step, *range(2 * AHEAD, TILES))
                else:
                    if u2:
                        pe.wait_ge(S["exp_done"], SPU * u2 - 2)
                    pe.wait_ge(S["zrows_in"], 16)
                    pe.wait_ge(S["rows_in1" if (u2 // NHALF) % 2 else "rows_in0"], 16)
                    for h in range(HG):
                        if h < 2:
                            pe.wait_ge(S["shift_rows"], 2 * u2 + h + 1)
                        elif h == 2:
                            pe.wait_ge(S["shift_rows2"], u2 + 1)
                        else:
                            pe.wait_ge(S["p1_free"], maxima_use(u2) + 1 + SLOTS)
                        score_tile(u2, 0, h, unit_bank(u2, h))
                    if step >= 2:
                        n = output_use(step - 2)
                        output_blocks(n, n % SLOTS, step - 1)
                    pe.wait_ge(S["exp_done"], SPU * u2 + 2)
                    for h in range(HG):
                        i = pe.matmul(ps[32 * h:32 * h + 32, unit_bank(u2, HG), :],
                                      keys[(u2 // NHALF) % 2][0:ROWS2, h, KT * P:SKP], QU[0:ROWS2, u2 % 3, h, :],
                                      start=True, stop=True, tile_position=(0, 32 * h))
                    i.then_inc(S["s_ready"], 1)
                    first_tiles(step, 4, 5)
                    score(1, 0)
                    first_tiles(step, 6, 7)
                    score(1, 1, 2)
                    first_tiles(step, 8, 9)
                    values(u2, 0, 0)
                    first_tiles(step, 10, 11)
                    score(1, 3)
                    first_tiles(step, 12, 13, 14, 15)

                n0 = loop_use(step)
                for k, (begin, end) in enumerate(((0, TURNS),) if u1 is not None else PE_TURNS):
                    if k:
                        ON_THE_WAY[k - 1](0)
                    with pe.Fori(begin, end) as i:
                        t = 0
                        for j in range(STEP):
                            for what in (ORDER if u1 is not None else ORDER_LAST)[j]:
                                if what == "max" and u1 is not None:
                                    max_tile(u1, n0 + TILES * i + t, t, (n0 + t) % SLOTS, i * MK + MK)
                                    t += 1
                                if what == "values" and u2 is not None:
                                    values(u2, i * STEP + (j + 1), (j + 1) % STEP)
                                if isinstance(what, int) and u2 is not None:
                                    score_tile(u2, i * STEP + (j + 2), what,
                                                   unit_bank(u2, 1 + HG * (j + 2) + what))
                if u2 is not None:
                    values(u2, KT - 1, (KT - 1) % STEP)
                if u1 is not None:
                    if u1 < UNITS - 1:
                        staged(u1 + 1)
                        first_tiles(u1 + 1, *range(AHEAD))
                    pe.wait_ge(S["max_parts"], u1 + 1)
                    maxima_rows(maxima_use(u1), maxima_use(u1) % SLOTS)
                if u2 is not None:
                    pe.matmul(ps[:, ACC, :], VTAIL[:, u2 // NHALF, :], PTAIL[:, :], start=False, stop=True,
                              skip_group_check=True).then_inc(S["av_done"], 1)
            n = output_use(UNITS - 1)
            output_blocks(n, n % SLOTS, UNITS)

            def post(p, half):
                bank, ready = PORTS[half][p][:2]
                if p == 0:
                    pe.wait_ge(S["p1_free"], BASE1 + USE2["out", NG * (half + 1) - 1, 0] + 1 + 2)
                else:
                    pe.wait_ge(PORTS[half][p - 1][3], PORTS[half][p - 1][4])
                if p == 2:
                    pe.wait_ge(S["n2_ready"], half + 1)
                if p == 4:
                    pe.wait_ge(S["dg_ready"], half + 1)
                for b in range(QB):
                    t = half * QB + b
                    rows128, xt = slice(b * P, (b + 1) * P), XT[:, t * P:(t + 1) * P]
                    if p == 0:
                        i = pe.transpose(ps[:, bank, rows128], OX[:, t, :], ident[:, :])
                    if p == 1:
                        i = pe.matmul(ps[:, bank, rows128], xt, wo2[:, :], start=True, stop=True)
                    if p == 2:
                        i = pe.transpose(ps[:, bank, rows128], NX[:, t, :], ident[:, :])
                    if p == 3:
                        i = pe.matmul(ps[:, bank, b * E:(b + 1) * E], xt, gw[:, :], start=True, stop=True)
                    if p == 4:
                        i = pe.transpose(ps[0:E, bank, rows128], dg[:, 0, t, :], ident[:, :])
                    if p == 5:
                        i = pe.transpose(ps[0:PARTS * E, bank, b * P // 2:(b + 1) * P // 2].bitcast(BF16),
                                         dg3[:, t, :, :].rearrange("p j e -> p (j e)"), identb[:, :])
                i.then_inc(ready, 1)

            for t in ("v2_out", "q2_in0", "k2_in0"):
                pe.wait_ge(S[t], 1 if t == "v2_out" else 16 * 10)
            for what, u, x in ITEMS2:
                if what == "way":
                    if u in (0, 1, 4, 5):
                        ON_THE_WAY[(0, 1, 4, 5).index(u)](1)
                    continue
                if what == "post":
                    if u in POST_PORTS:
                        fill(BASE1 + USE2[what, u, x])
                        if SLOTTED2[USE2[what, u, x] - 2][0] == "rows":
                            pe.wait_ge(S["shift2_rows"], (HG - 1) * (SLOTTED2[USE2[what, u, x] - 2][1] + 1))
                        post(POST_PORTS.index(u), 0)
                    continue
                g, half = unit2(u)
                if (what, u, x) == ("max", NG, 0):
                    for t in ("v2_out", "q2_in1", "k2_in1"):
                        pe.wait_ge(S[t], 2 if t == "v2_out" else 16 * 10)
                if (what, u, x) in USE2:
                    n = BASE1 + USE2[what, u, x]
                    bank = 2 * (n % 2)
                    if n - BASE1 >= 2 and SLOTTED2[n - BASE1 - 2][0] == "rows":
                        pe.wait_ge(S["shift2_rows"], (HG - 1) * (SLOTTED2[n - BASE1 - 2][1] + 1))
                if what == "max":
                    h, qb = divmod(x, QB)
                    head = g * HG + h
                    q0 = (half * QB + qb) * P
                    fill(n)
                    for a in range(0, q0 + P, 512):
                        w = min(512, q0 + P - a)
                        pe.matmul(ps[:, bank + a // 512, 0:w], q2s[half][0:PROD, head, qb * P:(qb + 1) * P],
                                  k2s[a // QH][0:PROD, head, 0:w], start=True, stop=True)
                    pe.matmul(ps[:, bank + q0 // 512, q0 % 512:q0 % 512 + P], identb[:, :], maskq[:, :],
                              start=False, stop=True, skip_group_check=True).then_inc(S["p1_ready"], 1)
                if what == "rows":
                    pe.wait_ge(S["max_parts"], UNITS + u + 1)
                    maxima_rows(n, bank)
                if what == "out":
                    output_blocks(n, bank, UNITS + u + 1)
                if what == "score":
                    kt, h = x
                    c0 = cols2(half, kt)
                    n = SBASE2[u] + HG * kt + h
                    if kt == 0 and h == 0:
                        pe.wait_ge(S["shift2_rows"], (HG - 1) * (u + 1))
                        pe.wait_ge(S["p1_free"], BASE1 + USE2["rows", u, 0] + 1 + 2)
                    pe.wait_ge(S["exp_done"], n - 2)
                    k0 = kt % QB * P
                    i = pe.matmul(ps[:, score_bank(n), c0:QH], k2s[kt // QB][0:ROWS2, g * HG + h, k0:k0 + P],
                                  q2s[half][0:ROWS2, g * HG + h, c0:QH], start=True, stop=True)
                    if kt >= half * QB:
                        i = pe.matmul(ps[:, score_bank(n), c0:c0 + P], identb[:, :], maskk[:, :],
                                      start=False, stop=True, skip_group_check=True)
                    i.then_inc(S["s_ready"], 1)
                if what == "values":
                    a = ABASE2[u] + x
                    c0 = cols2(half, x)
                    pe.wait_ge(S["exp_done"], SBASE2[u] + HG * (x + 1))
                    if x == 0:
                        pe.wait_ge(S["acc_copied"], UNITS + u)
                    for h in range(HG):
                        i = pe.matmul(ps[32 * h:32 * h + VC, ACC, c0:QH], V2[:, x, g * HG + h, :],
                                      PR[:, a % STEP, h, c0:QH], start=(x == 0), stop=(x == kts2(half) - 1),
                                      skip_group_check=True, tile_position=(0, 32 * h))
                    i.then_inc(S["av_done"], 1)

            def up(m):
                half, e, c = m // (E * FC), (m // FC) % E, m % FC
                if m >= 4:
                    pe.wait_ge(S["h_gelu"], m - 3)
                pe.matmul(ps[:, m % 4, :], fc1[:, e, c * P:(c + 1) * P], XT[:, half * QH:(half + 1) * QH],
                          start=True, stop=True).then_inc(S["h_psum"], 1)

            def gate(k):
                half, e = divmod(k, E)
                if e == 0:
                    pe.wait_ge(*PORTS[half][-1][3:])
                if k >= 2:
                    pe.wait_ge(S["h_gated"], FC * (k - 1))
                pe.matmul(ps[:, 4 + k % 2, :], sel[:, e, :], gT3[:, half * QH:(half + 1) * QH],
                          start=True, stop=True).then_inc(S["g_psum"], 1)

            pe.wait_ge(S["moe_in"], 32)
            pe.wait_ge(S["p1_free"], BASE1 + len(SLOTTED2) + 2)
            gate(0)
            up(0)
            up(1)
            MM = NHALF * E * FC
            for m in range(MM):
                if m in POST_AT and POST_AT.index(m) in POST_PORTS:
                    post(POST_PORTS.index(POST_AT.index(m)), 1)
                half, e, c = m // (E * FC), (m // FC) % E, m % FC
                if m % FC == 1 and m // FC + 1 < NHALF * E:
                    gate(m // FC + 1)
                if m + 2 < MM:
                    up(m + 2)
                if e == 0 and c == 0:
                    pe.matmul(ps[:, 6 + half, :], fc2b[:, :], gT[:, half * QH:(half + 1) * QH],
                              start=True, stop=False, skip_group_check=True)
                pe.wait_ge(S["h_gated"], m + 1)
                i = pe.matmul(ps[:, 6 + half, :], fc2[:, e, c, :], PRf[:, (4 + m % 4) * QH:(5 + m % 4) * QH],
                              start=False, stop=(e == E - 1 and c == FC - 1), skip_group_check=True)
                i.then_inc(S["h_used"], 1)
            for half in range(NHALF):
                pe.wait_ge(S["yt_copied"], half + 1)
                if half == 0:
                    pe.wait_ge(S["h_gelu"], MM)
                for b in range(QB):
                    t = half * QB + b
                    i = pe.transpose(ps[:, half, b * P:(b + 1) * P], XT[:, t * P:(t + 1) * P], ident[:, :])
                i.then_inc(S["yo_psum"], 1)


def kernel(**inputs):
    import ml_dtypes
    import concourse.bacc as bacc
    from concourse.bass_utils import run_bass_kernel_spmd

    a = {k: np.asarray(v) for k, v in inputs.items()}
    bf = ml_dtypes.bfloat16
    f = lambda n: a["L0_ffn_" + n]
    xa = lambda n: a["L0_xattn_" + n]
    col = lambda v: v.reshape(D, 1)
    row = lambda v: v.reshape(1, D)
    padrows = np.zeros((ROWS2 - PROD, SKP), bf)
    padrows[ROWS1 - PROD:, :SK] = 1
    masked = np.triu(np.ones((P, P), bool), 1)
    sel = np.zeros((PARTS * E, E, P), bf)
    for j in range(PARTS):
        for e in range(E):
            sel[j * E + e, e, :] = 1
    arrays = {
        "x": a["x"], "ctxT": np.ascontiguousarray(a["ctx_1024"][0].T),
        "Wq": xa("Wq"), "Wk": xa("Wk"), "Wv": xa("Wv"), "Wo": xa("Wo"), "Wqkv": f("Wqkv"), "Wo2": f("Wo"),
        "gw": f("gate_W"),
        "cols": np.concatenate([col(xa("bq")), col(xa("bk")), col(f("bqkv")[:D]), col(f("bqkv")[D:2 * D])], 1),
        "bv": row(xa("bv")), "bo": row(xa("bo")), "bv2": row(f("bqkv")[2 * D:]), "bo2": row(f("bo")),
        "l1w": row(f("ln1_w")), "l1b": row(f("ln1_b")), "l2w": row(f("ln2_w")), "l2b": row(f("ln2_b")),
        "fc1T": np.ascontiguousarray(f("fc1_w").transpose(2, 0, 1)),
        "fc2T": np.ascontiguousarray(f("fc2_w").reshape(E, D, FC, P).transpose(3, 0, 2, 1)),
        "b1c": np.ascontiguousarray(f("fc1_b").reshape(E * FC, P).T), "fc2b": f("fc2_b"),
        "ident": np.eye(P, dtype=np.float32), "identb": np.eye(P, dtype=bf),
        "maskq": np.where(masked, -1e30, 0.0).astype(bf), "maskk": np.where(masked.T, -1e30, 0.0).astype(bf),
        "iota": np.tile(np.arange(E, dtype=np.float32), (P, 1)), "sel": sel,
        "zeros": np.zeros((PARTS, P, SKP - SK), bf), "padrows": padrows,
        "zrows": np.zeros((ROWS1 - PROD, 3 * HG * QH), bf),
    }
    nc = bacc.Bacc("TRN2", target_bir_lowering=False, num_devices=1)
    dram = {n: nc.dram_tensor("in_" + n, v.shape, mybir.dt.from_np(v.dtype), kind="ExternalInput").ap()
            for n, v in arrays.items()}
    dram["out"] = nc.dram_tensor("out", (1, N, D), F32, kind="ExternalOutput").ap()
    build(nc, dram)
    r = run_bass_kernel_spmd(nc, [{"in_" + n: v for n, v in arrays.items()}], core_ids=[0])
    return r.results[0]["out"]
```
